# Optimizing a Trainium2 kernel written in Bass

```python
import numpy as np
import jax
import jax.numpy as jnp

def _softmax(x, axis=-1):
    return jax.nn.softmax(x, axis=axis)

def _gelu(x):
    return jax.nn.gelu(x, approximate=True)

def _silu(x):
    return jax.nn.silu(x)

def _sigmoid(x):
    return jax.nn.sigmoid(x)

def _layernorm(x, axis=-1, eps=1e-05):
    m = jnp.mean(x, axis=axis, keepdims=True)
    v = jnp.var(x, axis=axis, keepdims=True)
    return (x - m) / jnp.sqrt(v + eps)

def _scatter_add(tgt, idx, src, axis=0):
    return tgt.at[idx].add(src)

def _segment_sum(src, seg, n):
    return jax.ops.segment_sum(src, seg, n)
kernel_name = 'mk_macaron_d2_jaxref_r8_3be298'

def setup_inputs(seed: int=0):
    np.random.seed(seed)
    _w = jnp.asarray

    def _L0_attn_setup():
        import jax, jax.numpy as jnp
        import numpy as np
        import math
        D_MODEL = 256
        NUM_HEADS = 16
        D_K = D_MODEL // NUM_HEADS
        SEQ_LEN = 256
        BATCH = 2

        def _rope_cache(s):
            half = D_K // 2
            inv_freq = 1.0 / 10000.0 ** (jnp.arange(half, dtype=jnp.float32) / half)
            angles = jnp.arange(s, dtype=jnp.float32)[:, None] * inv_freq[None, :]
            return (jnp.cos(angles), jnp.sin(angles))

        def _apply_rope(x, cos, sin):
            x_even = x[..., 0::2]
            x_odd = x[..., 1::2]
            rot_even = x_even * cos - x_odd * sin
            rot_odd = x_even * sin + x_odd * cos
            return jnp.stack((rot_even, rot_odd), axis=-1).reshape(x.shape)
        key = jax.random.key(seed)
        ks = jax.random.split(key, 9)
        sc = 1.0 / math.sqrt(D_MODEL)
        return {'x': jax.random.normal(ks[0], (BATCH, SEQ_LEN, D_MODEL), jnp.float32), 'Wq': jax.random.normal(ks[1], (D_MODEL, D_MODEL), jnp.float32) * sc, 'bq': jax.random.normal(ks[2], (D_MODEL,), jnp.float32) * 0.01, 'Wk': jax.random.normal(ks[3], (D_MODEL, D_MODEL), jnp.float32) * sc, 'bk': jax.random.normal(ks[4], (D_MODEL,), jnp.float32) * 0.01, 'Wv': jax.random.normal(ks[5], (D_MODEL, D_MODEL), jnp.float32) * sc, 'bv': jax.random.normal(ks[6], (D_MODEL,), jnp.float32) * 0.01, 'Wo': jax.random.normal(ks[7], (D_MODEL, D_MODEL), jnp.float32) * sc, 'bo': jax.random.normal(ks[8], (D_MODEL,), jnp.float32) * 0.01}
    _L0_attn_in = _L0_attn_setup()

    def _L0_ffn_setup():
        import jax, jax.numpy as jnp
        import numpy as np
        D_MODEL = 256
        D_FF = 1024

        def absmean_quant(w):
            scale = jnp.mean(jnp.abs(w))
            mask = (jnp.abs(w) >= scale * 0.7).astype(w.dtype)
            return jnp.sign(w) * mask
        key = jax.random.key(seed)
        k_x, k_w1, k_w2 = jax.random.split(key, 3)
        x = jax.random.normal(k_x, (4, 512, D_MODEL), dtype=jnp.float32)
        w1 = jax.random.normal(k_w1, (D_FF, D_MODEL), dtype=jnp.float32)
        b1 = jnp.zeros((D_FF,), dtype=jnp.float32)
        w2 = jax.random.normal(k_w2, (D_MODEL, D_FF), dtype=jnp.float32)
        b2 = jnp.zeros((D_MODEL,), dtype=jnp.float32)
        return {'x': x, 'w1': w1, 'b1': b1, 'w2': w2, 'b2': b2}
    _L0_ffn_in = _L0_ffn_setup()

    def _L1_attn_setup():
        import jax, jax.numpy as jnp
        import numpy as np
        B, L, DM, DI, DN, DR, DC = (2, 128, 256, 512, 16, 128, 4)

        def _mamba_forward(hidden_states, in_proj_weight, conv1d_weight, x_proj_weight, dt_proj_weight, dt_proj_bias, A_log, D, out_proj_weight):
            b, l, dm = hidden_states.shape
            di, dc = conv1d_weight.shape
            dn = A_log.shape[1]
            dr = dt_proj_weight.shape[1]
            xz = jnp.einsum('bld,ed->ble', hidden_states, in_proj_weight)
            x, z = (xz[..., :di], xz[..., di:])
            xp = jnp.pad(x, ((0, 0), (dc - 1, 0), (0, 0)))
            x_conv = sum((xp[:, w:w + l, :] * conv1d_weight[:, w] for w in range(dc)))
            x_conv = jax.nn.silu(x_conv)
            x_dbl = jnp.einsum('bld,ed->ble', x_conv, x_proj_weight)
            dt_low = x_dbl[..., :dr]
            Bm = x_dbl[..., dr:dr + dn]
            Cm = x_dbl[..., dr + dn:]
            delta = jax.nn.softplus(jnp.einsum('blr,dr->bld', dt_low, dt_proj_weight) + dt_proj_bias)
            A = -jnp.exp(A_log)
            deltaA = jnp.exp(jnp.einsum('bld,dn->lbdn', delta, A))
            dBu = jnp.einsum('bld,bln,bld->lbdn', delta, Bm, x_conv)
            C_t = jnp.transpose(Cm, (1, 0, 2))

            def step(h, inp):
                dA, dbu, c = inp
                h = dA * h + dbu
                y = jnp.einsum('bdn,bn->bd', h, c)
                return (h, y)
            h0 = jnp.zeros((b, di, dn), dtype=x_conv.dtype)
            _, ys = jax.lax.scan(step, h0, (deltaA, dBu, C_t))
            y = jnp.transpose(ys, (1, 0, 2)) + x_conv * D
            y = y * jax.nn.silu(z)
            return jnp.einsum('bld,ed->ble', y, out_proj_weight)
        key = jax.random.key(seed)
        ks = jax.random.split(key, 8)
        hidden_states = jax.random.normal(ks[0], (B, L, DM), dtype=jnp.float32)
        in_proj_weight = jax.random.normal(ks[1], (2 * DI, DM), dtype=jnp.float32) * 0.02
        conv1d_weight = jax.random.normal(ks[2], (DI, DC), dtype=jnp.float32) * 0.2
        x_proj_weight = jax.random.normal(ks[3], (DR + 2 * DN, DI), dtype=jnp.float32) * 0.02
        dt_proj_weight = jax.random.normal(ks[4], (DI, DR), dtype=jnp.float32) * 0.02
        dt_proj_bias = jax.random.normal(ks[5], (DI,), dtype=jnp.float32) * 0.1 - 4.0
        A_log = jnp.log(jnp.broadcast_to(jnp.arange(1, DN + 1, dtype=jnp.float32), (DI, DN)))
        D = jnp.ones((DI,), dtype=jnp.float32)
        out_proj_weight = jax.random.normal(ks[6], (DM, DI), dtype=jnp.float32) * 0.02
        return {'hidden_states': hidden_states, 'in_proj_weight': in_proj_weight, 'conv1d_weight': conv1d_weight, 'x_proj_weight': x_proj_weight, 'dt_proj_weight': dt_proj_weight, 'dt_proj_bias': dt_proj_bias, 'A_log': A_log, 'D': D, 'out_proj_weight': out_proj_weight}
    _L1_attn_in = _L1_attn_setup()

    def _L1_ffn_setup():
        import jax, jax.numpy as jnp
        import numpy as np
        B, S, H = (4, 128, 256)
        E = 16
        K = 2
        I = 128
        N_SHARED = 2
        I_SHARED = I * N_SHARED
        RATIO = 0.1
        EPS = 1e-09

        def _swiglu(x, wg, wu, wd):
            return jax.nn.silu(x @ wg) * (x @ wu) @ wd
        key = jax.random.key(seed)
        ks = jax.random.split(key, 9)
        scale = 0.02
        x = jax.random.normal(ks[0], (B, S, H), dtype=jnp.float32)
        centroids = jax.random.normal(ks[1], (E, H), dtype=jnp.float32)
        gate_bias = jnp.zeros((E,), dtype=jnp.float32)
        wg_s = jax.random.normal(ks[2], (H, I_SHARED), dtype=jnp.float32) * scale
        wu_s = jax.random.normal(ks[3], (H, I_SHARED), dtype=jnp.float32) * scale
        wd_s = jax.random.normal(ks[4], (I_SHARED, H), dtype=jnp.float32) * scale
        wg = jax.random.normal(ks[5], (E, H, I), dtype=jnp.float32) * scale
        wu = jax.random.normal(ks[6], (E, H, I), dtype=jnp.float32) * scale
        wd = jax.random.normal(ks[7], (E, I, H), dtype=jnp.float32) * scale
        return {'x': x, 'centroids': centroids, 'gate_bias': gate_bias, 'wg_s': wg_s, 'wu_s': wu_s, 'wd_s': wd_s, 'wg': wg, 'wu': wu, 'wd': wd}
    _L1_ffn_in = _L1_ffn_setup()
    _d = {'L0_attn_x': _L0_attn_in['x'], 'L0_attn_Wq': _L0_attn_in['Wq'], 'L0_attn_bq': _L0_attn_in['bq'], 'L0_attn_Wk': _L0_attn_in['Wk'], 'L0_attn_bk': _L0_attn_in['bk'], 'L0_attn_Wv': _L0_attn_in['Wv'], 'L0_attn_bv': _L0_attn_in['bv'], 'L0_attn_Wo': _L0_attn_in['Wo'], 'L0_attn_bo': _L0_attn_in['bo'], 'L0_ffn_w1': _L0_ffn_in['w1'], 'L0_ffn_b1': _L0_ffn_in['b1'], 'L0_ffn_w2': _L0_ffn_in['w2'], 'L0_ffn_b2': _L0_ffn_in['b2'], 'L1_attn_in_proj_weight': _L1_attn_in['in_proj_weight'], 'L1_attn_conv1d_weight': _L1_attn_in['conv1d_weight'], 'L1_attn_x_proj_weight': _L1_attn_in['x_proj_weight'], 'L1_attn_dt_proj_weight': _L1_attn_in['dt_proj_weight'], 'L1_attn_dt_proj_bias': _L1_attn_in['dt_proj_bias'], 'L1_attn_A_log': _L1_attn_in['A_log'], 'L1_attn_D': _L1_attn_in['D'], 'L1_attn_out_proj_weight': _L1_attn_in['out_proj_weight'], 'L1_ffn_centroids': _L1_ffn_in['centroids'], 'L1_ffn_gate_bias': _L1_ffn_in['gate_bias'], 'L1_ffn_wg_s': _L1_ffn_in['wg_s'], 'L1_ffn_wu_s': _L1_ffn_in['wu_s'], 'L1_ffn_wd_s': _L1_ffn_in['wd_s'], 'L1_ffn_wg': _L1_ffn_in['wg'], 'L1_ffn_wu': _L1_ffn_in['wu'], 'L1_ffn_wd': _L1_ffn_in['wd']}
    _x0 = _d['L0_attn_x']
    _d['L0_attn_x'] = jax.random.normal(jax.random.fold_in(jax.random.key(seed), 1), (1, 1024, 256), dtype=_x0.dtype)
    del _x0
    return _d

def reference(L0_attn_x, L0_attn_Wq, L0_attn_bq, L0_attn_Wk, L0_attn_bk, L0_attn_Wv, L0_attn_bv, L0_attn_Wo, L0_attn_bo, L0_ffn_w1, L0_ffn_b1, L0_ffn_w2, L0_ffn_b2, L1_attn_in_proj_weight, L1_attn_conv1d_weight, L1_attn_x_proj_weight, L1_attn_dt_proj_weight, L1_attn_dt_proj_bias, L1_attn_A_log, L1_attn_D, L1_attn_out_proj_weight, L1_ffn_centroids, L1_ffn_gate_bias, L1_ffn_wg_s, L1_ffn_wu_s, L1_ffn_wd_s, L1_ffn_wg, L1_ffn_wu, L1_ffn_wd):

    def _L0_attn_ref(x, Wq, bq, Wk, bk, Wv, bv, Wo, bo):
        import jax, jax.numpy as jnp
        import numpy as np
        import math
        D_MODEL = 256
        NUM_HEADS = 16
        D_K = D_MODEL // NUM_HEADS
        SEQ_LEN = 256
        BATCH = 2

        def _rope_cache(s):
            half = D_K // 2
            inv_freq = 1.0 / 10000.0 ** (jnp.arange(half, dtype=jnp.float32) / half)
            angles = jnp.arange(s, dtype=jnp.float32)[:, None] * inv_freq[None, :]
            return (jnp.cos(angles), jnp.sin(angles))

        def _apply_rope(x, cos, sin):
            x_even = x[..., 0::2]
            x_odd = x[..., 1::2]
            rot_even = x_even * cos - x_odd * sin
            rot_odd = x_even * sin + x_odd * cos
            return jnp.stack((rot_even, rot_odd), axis=-1).reshape(x.shape)
        b, s, d = x.shape

        def proj(W, bias):
            y = jnp.einsum('bsd,ed->bse', x, W) + bias
            return y.reshape(b, s, NUM_HEADS, D_K).transpose(0, 2, 1, 3)
        Q, K, V = (proj(Wq, bq), proj(Wk, bk), proj(Wv, bv))
        cos, sin = _rope_cache(s)
        Q = _apply_rope(Q, cos, sin)
        K = _apply_rope(K, cos, sin)
        scores = jnp.einsum('bhqd,bhkd->bhqk', Q, K) * (1.0 / math.sqrt(D_K))
        causal = jnp.tril(jnp.ones((s, s), bool))
        scores = jnp.where(causal[None, None], scores, -jnp.inf)
        probs = jax.nn.softmax(scores, axis=-1)
        att = jnp.einsum('bhqk,bhkd->bhqd', probs, V)
        att = att.transpose(0, 2, 1, 3).reshape(b, s, d)
        return jnp.einsum('bsd,ed->bse', att, Wo) + bo

    def _L0_ffn_ref(x, w1, b1, w2, b2):
        import jax, jax.numpy as jnp
        import numpy as np
        D_MODEL = 256
        D_FF = 1024

        def absmean_quant(w):
            scale = jnp.mean(jnp.abs(w))
            mask = (jnp.abs(w) >= scale * 0.7).astype(w.dtype)
            return jnp.sign(w) * mask
        w1_q = absmean_quant(w1)
        w2_q = absmean_quant(w2)
        h = jnp.einsum('bsd,fd->bsf', x, w1_q) + b1
        h = jax.nn.gelu(h, approximate=False)
        out = jnp.einsum('bsf,df->bsd', h, w2_q) + b2
        return out

    def _L1_attn_ref(hidden_states, in_proj_weight, conv1d_weight, x_proj_weight, dt_proj_weight, dt_proj_bias, A_log, D, out_proj_weight):
        import jax, jax.numpy as jnp
        import numpy as np
        B, L, DM, DI, DN, DR, DC = (2, 128, 256, 512, 16, 128, 4)

        def _mamba_forward(hidden_states, in_proj_weight, conv1d_weight, x_proj_weight, dt_proj_weight, dt_proj_bias, A_log, D, out_proj_weight):
            b, l, dm = hidden_states.shape
            di, dc = conv1d_weight.shape
            dn = A_log.shape[1]
            dr = dt_proj_weight.shape[1]
            xz = jnp.einsum('bld,ed->ble', hidden_states, in_proj_weight)
            x, z = (xz[..., :di], xz[..., di:])
            xp = jnp.pad(x, ((0, 0), (dc - 1, 0), (0, 0)))
            x_conv = sum((xp[:, w:w + l, :] * conv1d_weight[:, w] for w in range(dc)))
            x_conv = jax.nn.silu(x_conv)
            x_dbl = jnp.einsum('bld,ed->ble', x_conv, x_proj_weight)
            dt_low = x_dbl[..., :dr]
            Bm = x_dbl[..., dr:dr + dn]
            Cm = x_dbl[..., dr + dn:]
            delta = jax.nn.softplus(jnp.einsum('blr,dr->bld', dt_low, dt_proj_weight) + dt_proj_bias)
            A = -jnp.exp(A_log)
            deltaA = jnp.exp(jnp.einsum('bld,dn->lbdn', delta, A))
            dBu = jnp.einsum('bld,bln,bld->lbdn', delta, Bm, x_conv)
            C_t = jnp.transpose(Cm, (1, 0, 2))

            def step(h, inp):
                dA, dbu, c = inp
                h = dA * h + dbu
                y = jnp.einsum('bdn,bn->bd', h, c)
                return (h, y)
            h0 = jnp.zeros((b, di, dn), dtype=x_conv.dtype)
            _, ys = jax.lax.scan(step, h0, (deltaA, dBu, C_t))
            y = jnp.transpose(ys, (1, 0, 2)) + x_conv * D
            y = y * jax.nn.silu(z)
            return jnp.einsum('bld,ed->ble', y, out_proj_weight)
        return _mamba_forward(hidden_states, in_proj_weight, conv1d_weight, x_proj_weight, dt_proj_weight, dt_proj_bias, A_log, D, out_proj_weight)

    def _L1_ffn_ref(x, centroids, gate_bias, wg_s, wu_s, wd_s, wg, wu, wd):
        import jax, jax.numpy as jnp
        import numpy as np
        B, S, H = (4, 128, 256)
        E = 16
        K = 2
        I = 128
        N_SHARED = 2
        I_SHARED = I * N_SHARED
        RATIO = 0.1
        EPS = 1e-09

        def _swiglu(x, wg, wu, wd):
            return jax.nn.silu(x @ wg) * (x @ wu) @ wd
        shared = _swiglu(x, wg_s, wu_s, wd_s) * RATIO
        affinity = jax.nn.sigmoid(jnp.einsum('bsh,eh->bse', x, centroids))
        biased = affinity + gate_bias
        _, top_idx = jax.lax.top_k(biased, K)
        top_aff = jnp.take_along_axis(affinity, top_idx, axis=-1)
        weights = top_aff / (top_aff.sum(-1, keepdims=True) + EPS)
        mask = (jax.nn.one_hot(top_idx, E, dtype=x.dtype) * weights[..., None]).sum(-2)
        routed = jnp.zeros_like(x)
        for e in range(E):
            routed = routed + mask[..., e:e + 1] * _swiglu(x, wg[e], wu[e], wd[e])
        return shared + routed
    x = L0_attn_x
    x = x + 0.5 * _L0_ffn_ref(_layernorm(x, axis=-1), L0_ffn_w1, L0_ffn_b1, L0_ffn_w2, L0_ffn_b2)
    x = x + _L0_attn_ref(_layernorm(x, axis=-1), L0_attn_Wq, L0_attn_bq, L0_attn_Wk, L0_attn_bk, L0_attn_Wv, L0_attn_bv, L0_attn_Wo, L0_attn_bo)
    x = x + 0.5 * _L0_ffn_ref(_layernorm(x, axis=-1), L0_ffn_w1, L0_ffn_b1, L0_ffn_w2, L0_ffn_b2)
    x = x + 0.5 * _L1_ffn_ref(_layernorm(x, axis=-1), L1_ffn_centroids, L1_ffn_gate_bias, L1_ffn_wg_s, L1_ffn_wu_s, L1_ffn_wd_s, L1_ffn_wg, L1_ffn_wu, L1_ffn_wd)
    x = x + _L1_attn_ref(_layernorm(x, axis=-1), L1_attn_in_proj_weight, L1_attn_conv1d_weight, L1_attn_x_proj_weight, L1_attn_dt_proj_weight, L1_attn_dt_proj_bias, L1_attn_A_log, L1_attn_D, L1_attn_out_proj_weight)
    x = x + 0.5 * _L1_ffn_ref(_layernorm(x, axis=-1), L1_ffn_centroids, L1_ffn_gate_bias, L1_ffn_wg_s, L1_ffn_wu_s, L1_ffn_wd_s, L1_ffn_wg, L1_ffn_wu, L1_ffn_wd)
    return x

_drawn_inputs = setup_inputs


def setup_inputs(seed=0):
    import zlib

    import numpy as np

    out = dict(_drawn_inputs(seed))
    spreads = {'L0_ffn_b1': (0.0, 0.1),
     'L0_ffn_b2': (0.0, 0.1),
     'L1_attn_D': (1.0, 0.2),
     'L1_ffn_gate_bias': (0.0, 0.1)}
    factors = {}
    for name, (base, spread) in spreads.items():
        noise = np.random.default_rng([zlib.crc32(name.encode()), seed]).standard_normal(out[name].shape)
        drawn = base * np.exp(spread * noise) if base else spread * noise
        out[name] = jnp.asarray(drawn.astype(out[name].dtype))
    for name, factor in factors.items():
        out[name] = (out[name] * factor).astype(out[name].dtype)
    return out
```

```python
from contextlib import ExitStack

import numpy as np
import concourse.bass as bass
from concourse import mybir

F = mybir.dt.float32
R = mybir.dt.float32r
BF = mybir.dt.bfloat16
U32 = mybir.dt.uint32
ALU = mybir.AluOpType
ACT = mybir.ActivationFunctionType
AX = mybir.AxisListType.X

P = 128
S = 1024
D = 256
NT = S // P
CH = 512
NCH = S // CH
TC = CH // P
FF = 1024
NH = 16
DI = 512
DN = 16
NE = 16
EPS = 1e-5

CONST = {}
_at = 0
for _name, _n in (("ident", 128), ("CC", 128), ("SS", 128), ("iota", 16), ("b2", 256), ("bqkv", 768), ("bo", 256),
                  ("b1", 8), ("cw", 16), ("dtb", 4), ("Alog", 64), ("Dp", 4), ("gb", 16), ("hot", 32)):
    CONST[_name] = (_at, _n)
    _at += _n
NCONST = _at

WSTAGE = {"qkv": 1536, "o": 512, "in": 2048, "xp": 768, "dt": 512, "outw": 1024, "cen": 32, "sh": 1536}


class Line:

    def __init__(self, engine, sem):
        self.e, self.sem, self.n, self.waited = engine, sem, 0, {}

    def wait(self, *tokens):
        for t in tokens:
            if t is None:
                continue
            if isinstance(t, list):
                self.wait(*t)
                continue
            key, sem, v = t
            if self.waited.get(key, 0) < v:
                self.waited[key] = v
                self.e.wait_ge(sem, v)

    def __call__(self, fn, *tokens, inc=True):
        self.wait(*tokens)
        if not inc:
            fn(self.e)
            return None
        self.n += 1
        fn(self.e).then_inc(self.sem, 1)
        return (id(self), self.sem, self.n)

    @property
    def last(self):
        return (id(self), self.sem, self.n) if self.n else None


class Slots:

    def __init__(self, items):
        self.free = [(i, []) for i in items]

    def get(self):
        return self.free.pop(0)

    def put(self, item, *tokens):
        self.free.append((item, list(tokens)))


class Area:

    def __init__(self, t, n):
        self.t, self.n, self.at = t, n, 0

    def take(self, n):
        a = self.at
        self.at += n
        assert self.at <= self.n, (self.at, self.n)
        return self.t[:, a:a + n]


def build(nc, d):
    ctx = ExitStack()
    with ctx:
        def sb(name, shape, dt):
            return ctx.enter_context(nc.sbuf_tensor(name, shape, dt))

        nsem = [0]

        def sem(name):
            nsem[0] += 1
            return ctx.enter_context(nc.semaphore(name))

        PS = ctx.enter_context(nc.psum_tensor("PS", [P, 8, 512], F))
        X = sb("X", [P, NT, D], F)
        C = sb("C", [P, NCONST], F)
        BC16 = sb("BC16", [P, 3 * P], BF)
        W1Q = sb("W1Q", [P, 2, FF], R)
        W2Q = sb("W2Q", [P, 8, D], R)
        XN = sb("XN", [P, 2, 2, NCH, CH], R)
        HOT = sb("HOT", [P, 32], R)
        NRA, NFA = 22528, 17792
        RA = sb("RA", [P, NRA], R)
        FA = sb("FA", [P, NFA], F)
        SM = sb("SM", [P, 320], F)

        pe = Line(nc.tensor, sem("s_pe"))
        act = Line(nc.scalar, sem("s_act"))
        dve = Line(nc.vector, sem("s_dve"))
        pool = Line(nc.gpsimd, sem("s_pool"))
        sp = Line(nc.sync, sem("s_sp"))
        lines = (pe, act, dve, pool)

        def cst(name):
            a, n = CONST[name]
            return C[:, a:a + n]

        ident = cst("ident")
        identb, maskS, maskT = (BC16[:, i * P:(i + 1) * P] for i in range(3))

        class Chan:

            def __init__(self, name):
                self.sem, self.n = sem(name), 0

            def __call__(self, out, in_, *tokens):
                sp.wait(*tokens)
                self.n += 16
                nc.sync.dma_start(out, in_).then_inc(self.sem, 16)
                return (id(self), self.sem, self.n)

        def everyone():
            return [x.last for x in lines]

        banks = Slots([PS[:, i, :] for i in range(8)])

        def mm(out, lhsT, rhs, start, stop, *tokens, inc=False, skip=False):
            return pe(lambda e: e.matmul(out, lhsT, rhs, start=start, stop=stop, skip_group_check=skip),
                      *tokens, inc=inc)

        def group(out, pairs, *tokens, start=True, stop=True, skip=False):
            t = None
            for i, (a, b) in enumerate(pairs):
                t = mm(out, a, b, start and i == 0, stop and i == len(pairs) - 1,
                       *(tokens if i == 0 else ()), inc=i == len(pairs) - 1, skip=skip)
            return t

        def three(a, b):
            return [(a[0], b[0]), (a[1], b[0]), (a[0], b[1])]

        def tr(out, in_, *tokens, inc=True):
            return pe(lambda e: e.matmul(out, in_, ident, start=True, stop=True, is_transpose=True),
                      *tokens, inc=inc)

        def split(hi, lo, src, *tokens, on=None):
            on = on or act
            if on is act:
                t1 = act(lambda e: e.activation(hi, src, ACT.Copy), *tokens)
            else:
                t1 = on(lambda e: e.tensor_copy(hi, src), *tokens)
            t2 = dve(lambda e: e.tensor_tensor(lo, src, hi.bitcast(F), ALU.subtract), t1, *tokens)
            return [t1, t2]

        cc = Chan("s_c")
        t_c = cc(C[:, :], d["cst"])
        b16 = FA[:, NFA - 384:NFA]
        t_c16 = dve(lambda e: e.tensor_copy(BC16[:, :], b16), Chan("s_b16")(b16, d["b16"]))
        t_x = [None] * NT
        for h in range(2):
            cx = Chan(f"s_x{h}")
            t = cx(X[:, h * 4:h * 4 + 4, :], d["x"][:, h * 4:h * 4 + 4, :])
            for i in range(4):
                t_x[h * 4 + i] = t
        t_hot = dve(lambda e: e.tensor_copy(HOT[:, :], cst("hot")), t_c)

        def quantize():
            fa = Area(FA, NFA)
            out = []
            for i, (name, Q, n) in enumerate((("w1", W1Q, 2), ("w2", W2Q, 8))):
                w = fa.take(2048)
                tmp = fa.take(2048)
                t_w = Chan(f"s_{name}")(w, d[name])
                Qf = Q[:, :, :].rearrange("p a b -> p (a b)")
                s = SM[:, i * 4:i * 4 + 4]
                t = act(lambda e: e.activation(tmp, w, ACT.Abs, accum_out=s[:, 0:1]), t_w)
                bk, fr = banks.get()
                ones = cst("ident")
                ones1 = fa.take(128)
                t1 = dve(lambda e: e.memset(ones1, 1.0))
                t = mm(bk[:, 0:1], ones1, s[:, 0:1], True, True, t, t1, *fr, inc=True)
                t = dve(lambda e: e.tensor_scalar(s[:, 1:2], bk[:, 0:1], 1.0 / (FF * D), 0.7, ALU.mult, ALU.mult), t)
                banks.put(bk, t)
                t = dve(lambda e: e.tensor_scalar(s[:, 2:3], s[:, 1:2], -1.0, None, ALU.mult), t)
                t = dve(lambda e: e.tensor_scalar(tmp, w, s[:, 2:3], None, ALU.is_le), t)
                t = dve(lambda e: e.scalar_tensor_tensor(Qf, w, s[:, 1:2], tmp, ALU.is_ge, ALU.subtract), t)
                out.append(t)
            return out

        t_w1q, t_w2q = quantize()
        b2h = SM[:, 8:8 + 256]
        t_b2h = pool(lambda e: e.tensor_scalar(b2h, cst("b2"), 0.5, None, ALU.mult), t_c)
        eps = SM[:, 300:304]
        mhalf = SM[:, 304:308]
        t_eps = pool(lambda e: e.memset(mhalf, -0.5))

        def norm(ch, tmps, st, t_in, t_xnfree):
            tk = []
            for i in range(TC):
                t = ch * TC + i
                a = dve(lambda e: e.bn_stats(st[:, i * 6:i * 6 + 6], X[:, t, :]), t_in[t], t_xnfree)
                tk.append(dve(lambda e: e.bn_aggr(st[:, 24 + 2 * i:26 + 2 * i], st[:, i * 6:i * 6 + 6]), a))
            mv = st[:, 24:32].rearrange("p (t c) -> p t c", c=2)
            rs = st[:, 32:36]
            a = pool(lambda e: e.tensor_scalar(rs, mv[:, :, 1], EPS, None, ALU.add), tk)
            a = pool(lambda e: e.tensor_tensor(rs, rs, mhalf, ALU.pow), a, t_eps)
            b0, f0 = banks.get()
            b1, f1 = banks.get()
            for i in range(TC):
                t = ch * TC + i
                tmp, fr = tmps.get()
                n = dve(lambda e: e.tensor_scalar(tmp, X[:, t, :], st[:, 24 + 2 * i:25 + 2 * i], rs[:, i:i + 1],
                                                  ALU.subtract, ALU.mult), a, *fr)
                tr(b0[:, i * P:i * P + P], tmp[:, 0:P], n, t_c, *f0, inc=False)
                p = tr(b1[:, i * P:i * P + P], tmp[:, P:2 * P], *f1)
                tmps.put(tmp, p)
            out = []
            for k, b in ((0, b0), (1, b1)):
                tt = split(XN[:, 0, k, ch, :], XN[:, 1, k, ch, :], b, p, t_xnfree)
                banks.put(b, *tt)
                out += tt
            return out, n

        def xn(k, ch, a=0, b=CH):
            return (XN[:, 0, k, ch, a:b], XN[:, 1, k, ch, a:b])

        def ffn0(t_in):
            bar = everyone()
            ra, fa = Area(RA, NRA), Area(FA, NFA)
            H = [ra.take(8 * CH).rearrange("p (f n) -> p f n", f=8) for _ in range(2 * 2)]
            hs = Slots([fa.take(CH) for _ in range(4)])
            tmps = Slots([fa.take(D) for _ in range(4)])
            t_out = [None] * NT
            for ln in lines:
                ln.wait(bar)
            for ch in range(NCH):
                st = fa.take(40)
                t_xn, t_n = norm(ch, tmps, st, t_in, None)
                Hh, Hl = H[2 * ch], H[2 * ch + 1]
                xa = X[:, ch * TC:ch * TC + TC, :]
                t_b = pool(lambda e: e.tensor_tensor(xa, xa, b2h.unsqueeze(1).broadcast_to([P, TC, D]), ALU.add),
                           t_n, t_b2h)
                accs = [banks.get() for _ in range(TC)]
                t_h = []

                def down(f):
                    for i in range(TC):
                        acc, fr = accs[i]
                        t = group(acc[:, 0:D], [(Hh[:, f, i * P:i * P + P], W2Q[:, f, :]),
                                                (Hl[:, f, i * P:i * P + P], W2Q[:, f, :])],
                                  t_h[f], t_w2q, *(fr if f == 0 else ()), start=f == 0, stop=f == 7)
                        if f == 7:
                            accs[i] = (acc, t)

                for f in range(8):
                    bk, fr = banks.get()
                    ps = [(W1Q[:, k, f * P:f * P + P], x) for k in range(2) for x in xn(k, ch)]
                    t = group(bk, ps, t_xn, t_w1q, *fr)
                    h, fh = hs.get()
                    b1 = cst("b1")[:, f:f + 1]
                    t = act(lambda e: e.activation(h, bk, ACT.Gelu, bias=b1), t, *fh)
                    banks.put(bk, t)
                    tt = split(Hh[:, f, :], Hl[:, f, :], h, t, on=dve)
                    hs.put(h, *tt)
                    t_h.append(tt)
                    if f:
                        down(f - 1)
                down(7)
                for i in range(TC):
                    acc, t = accs[i]
                    xt = X[:, ch * TC + i, :]
                    t = dve(lambda e: e.scalar_tensor_tensor(xt, acc[:, 0:D], 0.5, xt, ALU.mult, ALU.add), t, t_b)
                    banks.put(acc, t)
                    t_out[ch * TC + i] = t
            return t_out

        wst = [FA[:, NFA - 3072:NFA - 1536], FA[:, NFA - 1536:NFA]]
        ch_w = [Chan("s_wst0"), Chan("s_wst1")]

        def attention(t_in):
            bar = everyone()
            for ln in lines:
                ln.wait(bar)
            ra, fa = Area(RA, NRA), Area(FA, NFA - 3072)
            Wq = [ra.take(1536).rearrange("p (k n) -> p k n", k=2) for _ in range(2)]
            Wo = [ra.take(512).rearrange("p (k n) -> p k n", k=2) for _ in range(2)]
            KT = ra.take(8 * S).rearrange("p (j n) -> p j n", j=8)
            QT = ra.take(8 * CH).rearrange("p (j n) -> p j n", j=8)
            Qs = [ra.take(1024) for _ in range(TC)]
            kk = ra.take(2048)
            Ks = Slots([kk[:, 0:1024], kk[:, 1024:2048]])
            AT = [kk[:, 0:1024].rearrange("p (k n) -> p k n", k=2), kk[:, 1024:2048].rearrange("p (k n) -> p k n", k=2)]
            V = fa.take(8 * 512).rearrange("p (t n) -> p t n", t=8)
            PT = Slots([fa.take(1024) for _ in range(8)])
            qk, t1b, t2b = fa.take(512), fa.take(512), fa.take(512)
            raw = fa.take(512)
            att = FA[:, 4096 + 8192:4096 + 8192 + 1024].rearrange("p (t n) -> p t n", t=TC)
            tmps = Slots([t1b[:, 0:256], t1b[:, 256:512]])
            M = SM[:, 264:264 + 16]
            st = t2b[:, 0:40]
            rc = t2b[:, 64:80]
            t = ch_w[0](wst[0], d["qkv"], bar)
            t_wq = split(Wq[0].rearrange("p k n -> p (k n)"), Wq[1].rearrange("p k n -> p (k n)"), wst[0], t, on=dve)
            t = ch_w[1](wst[1][:, 0:512], d["o"], bar)
            t_wo = split(Wo[0].rearrange("p k n -> p (k n)"), Wo[1].rearrange("p k n -> p (k n)"), wst[1][:, 0:512], t, on=dve)
            t_wst = [t_wq[1], t_wo[1]]
            pads = []
            for q in Qs:
                v = q.bitcast(F).rearrange("p (h c) -> p h c", c=64)[:, :, 32:48]
                pads.append(pool(lambda e: e.memset(v, 0.0)))
            for i in range(2):
                v = kk[:, 1024 * i:1024 * i + 1024].bitcast(F).rearrange("p (h c) -> p h c", c=64)
                a, b = v[:, :, 32:34], v[:, :, 34:48]
                pads.append(pool(lambda e: e.memset(a, -1.0)))
                pads.append(pool(lambda e: e.memset(b, 0.0)))
            vv = V.rearrange("p t (h c) -> p (t h) c", c=32)
            pads.append(pool(lambda e: e.memset(vv[:, :, 16:17], 1.0)))
            pads.append(pool(lambda e: e.memset(vv[:, :, 17:32], 0.0)))
            t_out = [None] * NT
            t_qt = None
            t_kk = []
            t_qk = t_t1 = t_t2 = None
            t_att = t_raw = None
            t_ptend = None
            for ch in range(NCH):
                t_xn, t_n = norm(ch, tmps, st, t_in, None)
                xa = X[:, ch * TC:ch * TC + TC, :]
                bo = cst("bo").unsqueeze(1).broadcast_to([P, TC, D])
                t_b = pool(lambda e: e.tensor_tensor(xa, xa, bo, ALU.add), t_n, t_c)
                t_qs = []
                for i in range(TC):
                    t = ch * TC + i
                    A = [xn(k, ch, i * P, i * P + P) for k in range(2)]
                    b0, f0 = banks.get()
                    b1, f1 = banks.get()
                    m0 = group(b0, [p for k in range(2) for p in three(A[k], [w[:, k, 0:512] for w in Wq])],
                               t_xn, t_wq, *f0)
                    m1 = group(b1[:, 0:256], [p for k in range(2) for p in three(A[k], [w[:, k, 512:768] for w in Wq])], *f1)
                    bq = cst("bqkv")[:, 0:512]
                    bv = cst("bqkv")[:, 512:768].rearrange("p (h c) -> p h c", c=16)
                    r1 = dve(lambda e: e.tensor_tensor(qk, b0, bq, ALU.add), m0, t_qk, t_att)
                    banks.put(b0, r1)
                    vt = V[:, t, :].rearrange("p (h c) -> p h c", c=32)[:, :, 0:16]
                    r2 = dve(lambda e: e.tensor_tensor(vt, b1[:, 0:256].rearrange("p (h c) -> p h c", c=16), bv, ALU.add),
                             m1, pads)
                    banks.put(b1, r2)
                    cs = cst("CC")[:, t * 16:t * 16 + 16].unsqueeze(1).broadcast_to([P, 32, 16])
                    q3 = qk.rearrange("p (h c) -> p h c", c=16)
                    o3 = t1b.rearrange("p (h c) -> p h c", c=16)
                    w3 = t2b.rearrange("p (h c) -> p h c", c=16)
                    se = cst("SS")[:, t * 16:t * 16 + 8].unsqueeze(1).broadcast_to([P, 32, 8])
                    so = cst("SS")[:, t * 16 + 8:t * 16 + 16].unsqueeze(1).broadcast_to([P, 32, 8])
                    a = pool(lambda e: e.tensor_tensor(o3, q3, cs, ALU.mult), r1, t_t1, t_n, tmps.free[0][1], tmps.free[1][1], t_att)
                    b = dve(lambda e: e.tensor_tensor(w3[:, :, 0:8], q3[:, :, 8:16], se, ALU.mult), r1, t_t2, t_n)
                    c = dve(lambda e: e.tensor_tensor(w3[:, :, 8:16], q3[:, :, 0:8], so, ALU.mult), t_t2)
                    r = dve(lambda e: e.tensor_tensor(qk, t1b, t2b, ALU.add), a, b, c)
                    t_t1 = t_t2 = r
                    rq = qk[:, 0:256].rearrange("p (h c) -> p h c", c=16)
                    rk = qk[:, 256:512].rearrange("p (h c) -> p h c", c=16)
                    Q3 = Qs[i].rearrange("p (h c) -> p h c", c=64)
                    ks, fk = Ks.get()
                    K3 = ks.rearrange("p (h c) -> p h c", c=64)
                    e1 = act(lambda e: e.activation(Q3[:, :, 0:16], rq, ACT.Copy), r, pads, t_qs[-1:] if False else None)
                    e2 = act(lambda e: e.activation(Q3[:, :, 48:64], rq, ACT.Copy), r)
                    e3 = dve(lambda e: e.tensor_tensor(Q3[:, :, 16:32], rq, Q3[:, :, 0:16].bitcast(F), ALU.subtract), e1)
                    g1 = act(lambda e: e.activation(K3[:, :, 0:16], rk, ACT.Copy), *fk, t_kk)
                    g2 = act(lambda e: e.activation(K3[:, :, 16:32], rk, ACT.Copy))
                    g3 = dve(lambda e: e.tensor_tensor(K3[:, :, 48:64], rk, K3[:, :, 0:16].bitcast(F), ALU.subtract), g1)
                    t_qk = [e3, e2, g3, g2]
                    t_qs.append([e1, e2, e3])
                    for half in range(2):
                        bk, fr = banks.get()
                        for j in range(4):
                            jj = half * 4 + j
                            p = tr(bk[:, j * P:j * P + P], ks[:, jj * P:jj * P + P].bitcast(F), g1, g2, g3, *fr, inc=j == 3)
                        dst = KT[:, half * 4:half * 4 + 4, t * P:t * P + P]
                        src = bk.rearrange("p (j n) -> p j n", j=4)
                        if half:
                            tk = act(lambda e: e.activation(dst, src, ACT.Copy), p)
                        else:
                            tk = dve(lambda e: e.tensor_copy(dst, src), p)
                        banks.put(bk, tk)
                        t_qs[-1].append(tk)
                    Ks.put(ks, p)

                def qtr(i, toks, free):
                    out = []
                    for half in range(2):
                        bk, fr = banks.get()
                        for j in range(4):
                            jj = half * 4 + j
                            p = tr(bk[:, j * P:j * P + P], Qs[i][:, jj * P:jj * P + P].bitcast(F), toks, *fr, inc=j == 3)
                        dst = QT[:, half * 4:half * 4 + 4, i * P:i * P + P]
                        src = bk.rearrange("p (j n) -> p j n", j=4)
                        if half:
                            tk = act(lambda e: e.activation(dst, src, ACT.Copy), p, free)
                        else:
                            tk = dve(lambda e: e.tensor_copy(dst, src), p, free)
                        banks.put(bk, tk)
                        out.append(tk)
                    return out, p

                t_q1 = []
                for i in range(TC):
                    tt, _ = qtr(i, t_qs[i], t_qt)
                    t_q1.append(tt)
                t_q2 = []
                t_m2 = None
                for i in range(TC):
                    t = ch * TC + i
                    w = (t + 1) * P
                    for h in range(NH):
                        j, o = h // 2, 64 * (h % 2)
                        pair = banks2.get()
                        bk, fr = pair
                        flat = bk.rearrange("p b n -> p (b n)")
                        for c0 in range(0, w, 512):
                            c1 = min(w, c0 + 512)
                            mm(flat[:, c0:c1], QT[o:o + 64, j, i * P:i * P + P], KT[o:o + 64, j, c0:c1], True,
                               c1 < w, t_q1[i], t_qs, *fr)
                        m = mm(flat[:, w - P:w], identb, maskS, False, True, t_c16, inc=True)
                        r = dve(lambda e: e.reduce_max(M[:, h:h + 1], flat[:, 0:w], AX), m, t_m2)
                        banks2.put(bk, r)
                    Q3 = Qs[i].rearrange("p (h c) -> p h c", c=64)
                    a = dve(lambda e: e.tensor_copy(Q3[:, :, 32], M), r)
                    b = dve(lambda e: e.tensor_tensor(Q3[:, :, 33], M, Q3[:, :, 32].bitcast(F), ALU.subtract), a)
                    t_m2 = b
                    tt, t_qsr = qtr(i, [a, b], m)
                    t_q2.append(tt)
                t_qsfree = t_qsr
                nk = ch * TC + TC
                items = [(g, kp) for g in range(4) for kp in range(nk // 2)]
                pend = None
                acc = None

                def pv(g, kp, slots, acc):
                    t = None
                    for u in range(2):
                        kt = 2 * kp + u
                        c0 = max(0, (kt - ch * TC) * P)
                        for hh in range(4):
                            pt, te = slots[hh]
                            t = mm(acc[0][32 * hh:32 * hh + 32, c0:CH], V[:, kt, (4 * g + hh) * 32:(4 * g + hh) * 32 + 32],
                                   pt[:, u * 512 + c0:u * 512 + CH], kt == 0, kt == nk - 1, te, *acc[1],
                                   inc=hh == 3 and u == 1)
                    for pt, te in slots:
                        PT.put(pt, t)
                    return t

                def finish(g, acc, t):
                    nonlocal t_raw, t_att
                    t = dve(lambda e: e.tensor_copy(raw, acc[0]), t, t_raw)
                    banks.put(acc[0], t)
                    bk, fr = banks.get()
                    for i in range(TC):
                        p = tr(bk[:, i * P:i * P + P], raw[:, i * P:i * P + P], t, *fr, inc=i == TC - 1)
                    t_raw = p
                    b4 = bk.rearrange("p (t h c) -> p t h c", h=4, c=32)
                    r3 = rc.rearrange("p (t h) -> p t h", h=4)
                    a = dve(lambda e: e.reciprocal(r3, b4[:, :, :, 16]), p)
                    for i in range(TC):
                        o = att[:, i, g * 64:g * 64 + 64].rearrange("p (h c) -> p h c", c=16)
                        s = b4[:, i, :, 0:16]
                        rr = r3[:, i, :].unsqueeze(2).broadcast_to([P, 4, 16])
                        a = dve(lambda e: e.tensor_tensor(o, s, rr, ALU.mult), a, t_qk)
                    banks.put(bk, a)
                    return a

                for g, kp in items + [(None, None)]:
                    if g is not None:
                        slots = []
                        for hh in range(4):
                            h = 4 * g + hh
                            j, o = h // 2, 64 * (h % 2)
                            bk, fr = banks2.get()
                            pt, fp = PT.get()
                            for u in range(2):
                                kt = 2 * kp + u
                                c0 = max(0, (kt - ch * TC) * P)
                                diag = kt >= ch * TC
                                t = mm(bk[:, u, c0:CH], KT[o:o + 64, j, kt * P:kt * P + P], QT[o:o + 64, j, c0:CH],
                                       True, not diag, t_q2, *fr, inc=not diag)
                                if diag:
                                    t = mm(bk[:, u, c0:c0 + P], identb, maskT, False, True, inc=True)
                            c0 = max(0, (2 * kp - ch * TC) * P)
                            c1 = max(0, (2 * kp + 1 - ch * TC) * P)
                            p2 = pt.rearrange("p (u n) -> p u n", u=2)
                            if c0 == c1:
                                te = act(lambda e: e.activation(p2, bk, ACT.Exp, scale=0.25), t, *fp)
                            else:
                                te = act(lambda e: e.activation(p2[:, 0, c0:], bk[:, 0, c0:], ACT.Exp, scale=0.25), t, *fp)
                                te = act(lambda e: e.activation(p2[:, 1, c1:], bk[:, 1, c1:], ACT.Exp, scale=0.25), t)
                            banks2.put(bk, te)
                            slots.append((pt, te))
                    if pend:
                        pg, pk, ps_ = pend
                        if pk == 0:
                            acc = banks.get()
                        t = pv(pg, pk, ps_, acc)
                        if pk == nk // 2 - 1:
                            t_att = finish(pg, acc, t)
                    pend = (g, kp, slots) if g is not None else None
                t_qt = pe.last
                b0, f0 = banks.get()
                b1, f1 = banks.get()
                for i in range(TC):
                    tr(b0[:, i * P:i * P + P], att[:, i, 0:P], t_att, *f0, inc=False)
                    p = tr(b1[:, i * P:i * P + P], att[:, i, P:2 * P], *f1)
                t_at = []
                for k, b in ((0, b0), (1, b1)):
                    tt = split(AT[0][:, k, :], AT[1][:, k, :], b, p)
                    banks.put(b, *tt)
                    t_at += tt
                for i in range(TC):
                    bk, fr = banks.get()
                    A = [[a[:, k, i * P:i * P + P] for a in AT] for k in range(2)]
                    m = group(bk[:, 0:D], [q for k in range(2) for q in three(A[k], [w[:, k, :] for w in Wo])],
                              t_at, t_wo, *fr)
                    xt = X[:, ch * TC + i, :]
                    t = dve(lambda e: e.tensor_tensor(xt, bk[:, 0:D], xt, ALU.add), m, t_b)
                    banks.put(bk, t)
                    t_out[ch * TC + i] = t
                t_kk = [m]
                if ch + 1 < NCH:
                    pads = []
                    for i in range(2):
                        v = kk[:, 1024 * i:1024 * i + 1024].bitcast(F).rearrange("p (h c) -> p h c", c=64)
                        a, b = v[:, :, 32:34], v[:, :, 34:48]
                        pads.append(pool(lambda e: e.memset(a, -1.0), m))
                        pads.append(pool(lambda e: e.memset(b, 0.0)))
                    for q in Qs:
                        v = q.bitcast(F).rearrange("p (h c) -> p h c", c=64)[:, :, 32:34]
                        pads.append(pool(lambda e: e.memset(v, 0.0)))
            return t_out

        nmoe = [0]

        def experts(t_in):
            u_ = nmoe[0]
            nmoe[0] += 1
            bar = everyone()
            for ln in lines:
                ln.wait(bar)
            ra, fa = Area(RA, NRA), Area(FA, NFA - 3072)
            Cn = [ra.take(32).rearrange("p (k n) -> p k n", k=2) for _ in range(2)]
            WS = Slots([[ra.take(768) for _ in range(2)] for _ in range(3)])
            H = Slots([[ra.take(CH) for _ in range(2)] for _ in range(4)])
            MT = [ra.take(CH) for _ in range(NCH)]
            st_, cen = fa.take(40), fa.take(32)
            tmps = Slots([fa.take(D) for _ in range(4)])
            bufs = Slots([fa.take(CH) for _ in range(6)])
            stage = Slots(list(range(4)))
            chs = ch_e
            sts = [fa.take(768) for _ in range(4)]
            small = fa.take(1024)
            t = ch_w[0](cen, d["cen"], bar)
            t_cn = split(Cn[0].rearrange("p k n -> p (k n)"), Cn[1].rearrange("p k n -> p (k n)"), cen, t, on=dve)

            def load(e_):
                s, fr = stage.get()
                t = chs[s](sts[s], d["we"][e_], bar, *fr)
                w, fw = WS.get()
                tt = split(w[0], w[1], sts[s], t, *fw, on=dve)
                stage.put(s, *tt)
                return w, tt

            t_xns, t_b = [], None
            for ch in range(NCH):
                t_xn, t_n = norm(ch, tmps, st_, t_in, None)
                t_xns.append(t_xn)
            t_mt = []
            smf = [None]
            for ch in range(NCH):
                bk, fr = banks.get()
                for i in range(TC):
                    A = [xn(k, ch, i * P, i * P + P) for k in range(2)]
                    m = group(bk[:, i * 16:i * 16 + 16], [q for k in range(2) for q in three(A[k], [w[:, k, :] for w in Cn])],
                              t_xns[ch], t_cn, *fr)
                aff = small[:, 0:64].rearrange("p (t e) -> p t e", e=16)
                bi = small[:, 64:128].rearrange("p (t e) -> p t e", e=16)
                top, ix = small[:, 128:160], small[:, 160:192].bitcast(U32)
                mk = small[:, 192:256].rearrange("p (t e) -> p t e", e=16)
                sm, rv = small[:, 256:260], small[:, 260:264]
                wn = small[:, 264:264 + 256].rearrange("p (t c) -> p t c", c=64)
                z = dve(lambda e: e.memset(wn, 0.0), smf[0])
                a = act(lambda e: e.activation(aff, bk[:, 0:64].rearrange("p (t e) -> p t e", e=16), ACT.Sigmoid), m, smf[0])
                banks.put(bk, a)
                gb = cst("gb").unsqueeze(1).broadcast_to([P, TC, 16])
                b = dve(lambda e: e.tensor_tensor(bi, aff, gb, ALU.add), a)
                for i in range(TC):
                    c = dve(lambda e: e.max(top[:, i * 8:i * 8 + 8], bi[:, i, :]), b)
                    c = dve(lambda e: e.max_index(ix[:, i * 8:i * 8 + 8], top[:, i * 8:i * 8 + 8], bi[:, i, :]), c)
                    c = dve(lambda e: e.tensor_scalar(mk[:, i, :], cst("iota"), ix[:, i * 8:i * 8 + 1], None, ALU.is_equal), c)
                    c = dve(lambda e: e.scalar_tensor_tensor(mk[:, i, :], cst("iota"), ix[:, i * 8 + 1:i * 8 + 2],
                                                             mk[:, i, :], ALU.is_equal, ALU.add), c)
                c = dve(lambda e: e.tensor_tensor(mk, mk, aff, ALU.mult), c)
                c = dve(lambda e: e.reduce_sum(sm, mk, AX), c)
                c = dve(lambda e: e.tensor_scalar(sm, sm, 1e-9, None, ALU.add), c)
                c = dve(lambda e: e.reciprocal(rv, sm), c)
                rr = rv.unsqueeze(2).broadcast_to([P, TC, 16])
                c1 = dve(lambda e: e.tensor_tensor(wn[:, :, 0:16], mk, rr, ALU.mult), c, z)
                c2 = dve(lambda e: e.tensor_tensor(wn[:, :, 32:48], mk, rr, ALU.mult), c, z)
                bk, fr = banks.get()
                for i in range(TC):
                    p = tr(bk[0:64, i * P:i * P + P], wn[:, i, :], c1, c2, *fr, inc=i == TC - 1)
                smf[0] = [p, c1, c2]
                mt = MT[ch]
                g = act(lambda e: e.activation(mt[0:64, :], bk[0:64, :], ACT.Copy), p)
                g = dve(lambda e: e.tensor_tensor(mt[32:64, :], bk[32:64, :], mt[32:64, :].bitcast(F), ALU.subtract), g)
                banks.put(bk, g)
                t_mt.append(g)
            accs = [banks.get() for _ in range(4)]
            todo = list(range(NE + 2))
            ready = [load(todo.pop(0)), load(todo.pop(0))]
            pend = []

            def down(w, hh, ch, tt, first, last, out):
                for i in range(TC):
                    t8 = ch * TC + i
                    acc, fr = accs[t8 // 2]
                    o = acc[:, (t8 % 2) * D:(t8 % 2) * D + D]
                    A = [x[:, i * P:i * P + P] for x in hh]
                    B = [x[:, 512:768] for x in w]
                    m = group(o, three(A, B), tt, *(fr if first else ()), start=first and t8 % 2 == 0,
                              stop=last, skip=True)
                    if last:
                        out[t8] = m
                return m

            fin = [None] * NT
            for n in range(NE + 2):
                w, t_w = ready.pop(0)
                mlast = []
                for ch in range(NCH):
                    bg, fg = banks.get()
                    bu, fu = banks.get()
                    X2 = [xn(k, ch) for k in range(2)]
                    mg = group(bg, [q for k in range(2) for q in three([x[:, k * P:k * P + P] for x in w], X2[k])],
                               t_w, t_xns[ch], *fg)
                    mu = group(bu, [q for k in range(2) for q in three([x[:, 256 + k * P:256 + k * P + P] for x in w], X2[k])], *fu)
                    s, fs = bufs.get()
                    h, fh = bufs.get()
                    t = act(lambda e: e.activation(s, bg, ACT.Silu), mg, *fs)
                    banks.put(bg, t)
                    if n < 2:
                        t = dve(lambda e: e.scalar_tensor_tensor(h, s, 0.1, bu, ALU.mult, ALU.mult), t, mu, *fh)
                        banks.put(bu, t)
                    else:
                        bm, fm = banks.get()
                        hot = HOT[0:64, n - 2:n - 1].broadcast_to([64, P])
                        mk_ = mm(bm, hot, MT[ch][0:64, :], True, True, t_mt[ch], t_hot, *fm, inc=True)
                        t = dve(lambda e: e.tensor_tensor(h, s, bu, ALU.mult), t, mu, *fh)
                        banks.put(bu, t)
                        t = dve(lambda e: e.tensor_tensor(h, h, bm, ALU.mult), t, mk_)
                        banks.put(bm, t)
                    bufs.put(s, t)
                    hh, fhh = H.get()
                    tt = split(hh[0], hh[1], h, t, *fhh, on=dve)
                    bufs.put(h, *tt)
                    if pend:
                        pw, ph, pc, pt_, pn = pend.pop(0)
                        m = down(pw, ph, pc, pt_, pn == 0, pn == NE + 1, fin)
                        H.put(ph, m)
                        if pc == NCH - 1:
                            WS.put(pw, m)
                            if todo:
                                ready.append(load(todo.pop(0)))
                    pend.append((w, hh, ch, tt, n))
                    if n == 0 and ch == 0 and todo:
                        ready.append(load(todo.pop(0)))
            for pw, ph, pc, pt_, pn in pend:
                down(pw, ph, pc, pt_, pn == 0, pn == NE + 1, fin)
            t_out = [None] * NT
            for t8 in range(NT):
                acc, _ = accs[t8 // 2]
                o = acc[:, (t8 % 2) * D:(t8 % 2) * D + D]
                xt = X[:, t8, :]
                t_out[t8] = dve(lambda e: e.scalar_tensor_tensor(xt, o, 0.5, xt, ALU.mult, ALU.add), fin[t8 | 1])
            for a in range(4):
                banks.put(accs[a][0], t_out[2 * a], t_out[2 * a + 1])
            return t_out

        def mamba(t_in):
            bar = everyone()
            for ln in lines:
                ln.wait(bar)
            ra, fa = Area(RA, NRA), Area(FA, NFA - 3072)

            def wsplit(name, n, i):
                out = [ra.take(n) for _ in range(2)]
                tk = []
                for a in range(0, n, 1536):
                    b = min(n, a + 1536)
                    t = ch_w[i % 2](wst[i % 2][:, 0:b - a], d[name][:, a:b], bar, wst_free[i % 2])
                    tt = split(out[0][:, a:b], out[1][:, a:b], wst[i % 2][:, 0:b - a], t, on=dve)
                    wst_free[i % 2] = tt
                    tk += tt
                    i += 1
                return out, tk, i

            wst_free = [None, None]
            Wi, t_wi, i = wsplit("in", 2048, 0)
            Wx, t_wx, i = wsplit("xp", 768, i)
            Wd, t_wd, i = wsplit("dt", 512, i)
            Wp, t_wp, i = wsplit("outw", 1024, i)
            XC2 = [ra.take(4 * CH).rearrange("p (m n) -> p m n", m=4) for _ in range(2)]
            DT = [ra.take(CH) for _ in range(2)]
            BCt = ra.take(CH)
            tmps = Slots([fa.take(D) for _ in range(2)])
            st_ = fa.take(40)
            st64 = fa.take(128)
            xr = fa.take(4 * 516).rearrange("p (m n) -> p m n", m=4)
            xc = fa.take(4 * CH).rearrange("p (m n) -> p m n", m=4)
            sz = fa.take(4 * CH).rearrange("p (m n) -> p m n", m=4)
            dl = fa.take(4 * CH).rearrange("p (m n) -> p m n", m=4)
            uu = fa.take(4 * CH).rearrange("p (m n) -> p m n", m=4)
            w6 = [FA[:, NFA - 3072 + CH * i:NFA - 3072 + CH * i + CH] for i in range(6)]
            bs = Slots([fa.take(CH) for _ in range(2)])
            sh = Slots([fa.take(CH) for _ in range(4)])
            sbb = Slots(w6[0:3])
            shc = Slots(w6[3:6])
            for s_ in (sbb, shc):
                s_.free = [(i, wst_free) for i, _ in s_.free]
            state, An = st64[:, 0:64], st64[:, 64:128]
            t_an = act(lambda e: e.activation(An, cst("Alog"), ACT.Exp), t_c)
            t_an = dve(lambda e: e.tensor_scalar(An, An, -1.0, None, ALU.mult), t_an)
            t_z = dve(lambda e: e.memset(xr[:, :, 0:3], 0.0))
            t_st = dve(lambda e: e.memset(state, 0.0))
            t_out = [None] * NT
            t_xc2 = t_dt = t_bc = t_y = t_xr = None
            for ch in range(NCH):
                t_xn, _ = norm(ch, tmps, st_, t_in, None)
                if ch:
                    t_z = dve(lambda e: e.tensor_copy(xr[:, :, 0:3], xr[:, :, 512:515]), t_xr)
                t_xr, t_xc, t_sz = [], [], []
                W3 = [w.rearrange("p (k n) -> p k n", k=2) for w in Wi]
                for m in range(8):
                    bk, fr = banks.get()
                    g = group(bk, [q for k in range(2) for q in three([w[:, k, m * P:m * P + P] for w in W3], xn(k, ch))],
                              t_xn, t_wi, *fr)
                    if m < 4:
                        a = act(lambda e: e.activation(xr[:, m, 3:515], bk, ACT.Copy), g, t_z)
                        banks.put(bk, a)
                        cw = cst("cw")
                        v = xc[:, m, :]
                        a = dve(lambda e: e.tensor_scalar(v, xr[:, m, 0:512], cw[:, 4 * m:4 * m + 1], None, ALU.mult), a, t_z, t_y)
                        for w in range(1, 4):
                            a = dve(lambda e: e.scalar_tensor_tensor(v, xr[:, m, w:w + 512], cw[:, 4 * m + w:4 * m + w + 1],
                                                                     v, ALU.mult, ALU.add), a)
                        t_xr.append(a)
                        a = act(lambda e: e.activation(v, v, ACT.Silu), a)
                        tt = split(XC2[0][:, m, :], XC2[1][:, m, :], v, a, t_xc2, on=dve)
                        t_xc.append([a] + tt)
                    else:
                        a = act(lambda e: e.activation(sz[:, m - 4, :], bk, ACT.Silu), g, t_y)
                        banks.put(bk, a)
                        t_sz.append(a)
                X3 = [w.rearrange("p (k n) -> p k n", k=4) for w in Wx]
                bd, fd = banks.get()
                bb, fb = banks.get()
                g1 = group(bd, [q for k in range(4) for q in three([w[:, k, 0:P] for w in X3], [x[:, k, :] for x in XC2])],
                           t_xc, t_wx, *fd)
                g2 = group(bb[0:64, :], [q for k in range(4) for q in three([w[:, k, P:P + 64] for w in X3], [x[:, k, :] for x in XC2])],
                           *fb)
                t_xc2 = g2
                t_dd = split(DT[0], DT[1], bd, g1, t_dt)
                banks.put(bd, *t_dd)
                a = act(lambda e: e.activation(BCt[0:64, :], bb[0:64, :], ACT.Copy), g2, t_bc)
                t_bb = dve(lambda e: e.tensor_tensor(BCt[32:64, :], bb[32:64, :], BCt[32:64, :].bitcast(F), ALU.subtract), a)
                banks.put(bb, t_bb)
                D3 = [w.rearrange("p (m n) -> p m n", m=4) for w in Wd]
                dd = []
                for m in range(4):
                    bk, fr = banks.get()
                    g = group(bk, three([w[:, m, :] for w in D3], DT), t_dd, t_wd, *fr)
                    b = cst("dtb")[:, m:m + 1]
                    v = dl[:, m, :]
                    u = uu[:, m, :]
                    a = act(lambda e: e.activation(v, bk, ACT.Abs, bias=b), g, t_y)
                    r = act(lambda e: e.activation(u, bk, ACT.Relu, bias=b), g, t_y)
                    banks.put(bk, a, r)
                    dd.append((v, u, a, r))
                t_dt = g
                ee = [act(lambda e, v=v: e.activation(v, v, ACT.Exp, scale=-1.0), a) for v, u, a, r in dd]
                ll = [act(lambda e, v=v: e.activation(v, v, ACT.Ln, bias=1.0), x) for (v, u, a, r), x in zip(dd, ee)]
                t_dl, t_u = [], []
                for m in range(4):
                    v, u, _, r = dd[m]
                    a = dve(lambda e: e.tensor_tensor(v, v, u, ALU.add), ll[m], r)
                    t_dl.append(a)
                    t_u.append(dve(lambda e: e.tensor_tensor(u, v, xc[:, m, :], ALU.mult), a, t_xc[m]))
                ys = [banks.get() for _ in range(4)]
                ab = Slots([banks.get() for _ in range(2)])
                cb, cfree = banks.get()
                bb, bfree = banks.get()
                gy = [None] * 4
                live = {}
                pend = []

                def spread_b(n):
                    return mm(bb, HOT[0:64, n:n + 1].broadcast_to([64, P]), BCt[0:64, :], True, True, t_bb, t_hot,
                              *live.get("b", bfree), inc=True)

                def store_b(g):
                    s_, f_ = bs.get()
                    t = act(lambda e: e.activation(s_, bb, ACT.Copy), g, *f_)
                    live["b"] = [t]
                    return s_, t

                def bring_c(n):
                    return mm(cb, HOT[0:64, 16 + n:17 + n].broadcast_to([64, P]), BCt[0:64, :], True, True,
                              *live.get("c", cfree), inc=True)

                def close():
                    n, m, h_, t3, gC = pend.pop(0)
                    c_, fc_ = shc.get()
                    t4 = dve(lambda e: e.tensor_tensor(c_, h_, cb, ALU.mult), t3, gC(), *fc_)
                    sh.put(h_, t4, live.get("s"))
                    live["c"] = [t4]
                    if m == 3 and n + 1 < DN:
                        tc[n + 1] = bring_c(n + 1)
                    yb, fy = ys[m]
                    gy[m] = mm(yb, ident, c_, n == 0, n == DN - 1, t4, *(fy if n == 0 else ()), inc=True)
                    shc.put(c_, gy[m])

                nb = store_b(spread_b(0))
                tc = {0: bring_c(0)}
                for n in range(DN):
                    Bs, t_B = nb
                    for m in range(4):
                        if m == 0 and n + 1 < DN:
                            gb = spread_b(n + 1)
                        k = 16 * m + n
                        (a_, _), fa_ = ab.get()
                        fa_ = fa_ or _
                        t1 = act(lambda e: e.activation(a_, dl[:, m, :], ACT.Exp, scale=An[:, k:k + 1]), t_dl[m], t_an, *fa_)
                        b_, fb_ = sbb.get()
                        t2 = pool(lambda e: e.tensor_tensor(b_, uu[:, m, :], Bs, ALU.mult), t_u[m], t_B, *fb_)
                        h_, fh_ = sh.get()
                        init = state[:, k:k + 1] if ch else 0.0
                        t3 = dve(lambda e: e.tensor_tensor_scan(h_, a_, b_, init, ALU.mult, ALU.add), t1, t2, t_st, *fh_)
                        ab.put((a_, _), t3)
                        sbb.put(b_, t3)
                        if len(pend) == 2:
                            close()
                        if m == 2 and n + 1 < DN:
                            nb = store_b(gb)
                        if ch + 1 < NCH:
                            live["s"] = dve(lambda e: e.tensor_copy(state[:, k:k + 1], h_[:, CH - 1:CH]), t3)
                        pend.append((n, m, h_, t3, lambda n=n: tc[n]))
                    bs.put(Bs, t2)
                while pend:
                    close()
                t_bc = pe.last
                t_st = live.get("s")
                for x in ((cb, live["c"]), (bb, live["b"])):
                    banks.put(x[0], *x[1])
                for (a_, _), f in ab.free:
                    banks.put(a_, *f)
                t_y, t_ys = [], []
                for m in range(4):
                    yb, _ = ys[m]
                    u = uu[:, m, :]
                    a = dve(lambda e: e.scalar_tensor_tensor(u, xc[:, m, :], cst("Dp")[:, m:m + 1], yb, ALU.mult, ALU.add), gy[m])
                    banks.put(yb, a)
                    a = dve(lambda e: e.tensor_tensor(u, u, sz[:, m, :], ALU.mult), a, t_sz[m])
                    tt = split(XC2[0][:, m, :], XC2[1][:, m, :], u, a, t_xc2, on=dve)
                    t_ys.append(tt)
                    t_y += [a] + tt
                P3 = [w.rearrange("p (k n) -> p k n", k=4) for w in Wp]
                for i in range(TC):
                    bk, fr = banks.get()
                    g = group(bk[:, 0:D], [q for k in range(4) for q in three([x[:, k, i * P:i * P + P] for x in XC2],
                                                                              [w[:, k, :] for w in P3])], t_ys, t_wp, *fr)
                    xt = X[:, ch * TC + i, :]
                    a = dve(lambda e: e.tensor_tensor(xt, bk[:, 0:D], xt, ALU.add), g)
                    banks.put(bk, a)
                    t_out[ch * TC + i] = a
                t_xc2 = g
                t_y.append(g)
            return t_out

        class Pairs:

            def get(self):
                if not self.own:
                    raise AssertionError
                return self.own.pop(0)

            def put(self, bk, *tokens):
                self.own.append((bk, list(tokens)))

        banks2 = Pairs()
        ch_e = [Chan(f"s_e{i}") for i in range(4)]

        def lend():
            frs = {}
            got = [banks.get() for _ in range(8)]
            for b, f in got:
                frs[b.offset] = (b, f)
            order = sorted(frs)
            lst = [frs[o] for o in order]
            banks2.own = [(PS[:, 2 * i:2 * i + 2, :], lst[2 * i][1] + lst[2 * i + 1][1]) for i in range(3)]
            for b, f in lst[6:]:
                banks.put(b, *f)

        def unlend():
            for bk, f in banks2.own:
                banks.put(bk[:, 0, :], *f)
                banks.put(bk[:, 1, :], *f)
            banks2.own = []

        t = ffn0(t_x)
        lend()
        t = attention(t)
        unlend()
        t = ffn0(t)
        t = experts(t)
        t = mamba(t)
        t = experts(t)
        co = Chan("s_out")
        for h in range(4):
            t_o = co(d["out"][:, 2 * h:2 * h + 2, :], X[:, 2 * h:2 * h + 2, :], t[2 * h], t[2 * h + 1])
        sp.wait(t_o)


def layout(i):
    f = np.float32
    x = np.asarray(i["L0_attn_x"])[0]

    def kt(w, k):
        return np.ascontiguousarray(w.reshape(k, P, -1).transpose(1, 0, 2))

    perm = np.array([h * 16 + c for h in range(NH) for c in list(range(0, 16, 2)) + list(range(1, 16, 2))])
    g = {n: np.asarray(i[n]) for n in i}
    wqkv = np.concatenate([g["L0_attn_Wq"][perm].T, g["L0_attn_Wk"][perm].T, g["L0_attn_Wv"].T], axis=1)
    bqkv = np.concatenate([g["L0_attn_bq"][perm], g["L0_attn_bk"][perm], g["L0_attn_bv"]])
    half = 8
    inv = (f(1.0) / np.power(f(10000.0), np.arange(half, dtype=f) / f(half))).astype(f)
    ang = (np.arange(S, dtype=f)[:, None] * inv[None, :]).astype(f)
    cos, sin = np.cos(ang).astype(f), np.sin(ang).astype(f)
    CC = np.concatenate([cos, cos], axis=1).reshape(NT, P, 16).transpose(1, 0, 2).reshape(P, NT * 16)
    SS = np.concatenate([-sin, sin], axis=1).reshape(NT, P, 16).transpose(1, 0, 2).reshape(P, NT * 16)
    hot = np.zeros((P, 32), f)
    for n in range(32):
        hot[n, n] = 1
        hot[32 + n, n] = 1

    def rows(v):
        return np.broadcast_to(np.asarray(v)[None, :], (P, len(v)))

    def cols(v, k):
        return np.asarray(v).reshape(k, P, -1).transpose(1, 0, 2).reshape(P, -1)

    a = np.arange(P)
    neg = f(-1e30)
    mS = np.where(a[None, :] > a[:, None], neg, f(0))
    mT = np.where(a[:, None] > a[None, :], neg, f(0))

    parts = {
        "ident": np.eye(P, dtype=f), "CC": CC, "SS": SS, "iota": rows(np.arange(16, dtype=f)),
        "b2": rows(g["L0_ffn_b2"]), "bqkv": rows(bqkv), "bo": rows(g["L0_attn_bo"]),
        "b1": cols(g["L0_ffn_b1"], 8), "cw": cols(g["L1_attn_conv1d_weight"], 4),
        "dtb": cols(g["L1_attn_dt_proj_bias"], 4), "Alog": cols(g["L1_attn_A_log"], 4),
        "Dp": cols(g["L1_attn_D"], 4), "gb": rows(g["L1_ffn_gate_bias"]), "hot": hot,
    }
    cst = np.concatenate([parts[n] for n in CONST], axis=1)
    xpw = g["L1_attn_x_proj_weight"].T
    xp = np.concatenate([xpw[:, 0:P], xpw[:, P:], xpw[:, P:]], axis=1)
    wgs, wus, wds = g["L1_ffn_wg_s"], g["L1_ffn_wu_s"], g["L1_ffn_wd_s"]
    we = []
    for s in range(2):
        we.append((wgs[:, s * P:s * P + P], wus[:, s * P:s * P + P], wds[s * P:s * P + P]))
    for e in range(NE):
        we.append((g["L1_ffn_wg"][e], g["L1_ffn_wu"][e], g["L1_ffn_wd"][e]))
    we = np.stack([np.concatenate([kt(a_, 2).reshape(P, 256), kt(b_, 2).reshape(P, 256), c_], axis=1) for a_, b_, c_ in we])
    return {
        "x": np.ascontiguousarray(x.reshape(NT, P, D).transpose(1, 0, 2)),
        "cst": np.ascontiguousarray(cst.astype(f)),
        "b16": np.concatenate([np.eye(P, dtype=f), mS, mT], axis=1).astype(f),
        "w1": kt(g["L0_ffn_w1"].T, 2).reshape(P, 2048), "w2": kt(g["L0_ffn_w2"].T, 8).reshape(P, 2048),
        "qkv": kt(wqkv, 2).reshape(P, 1536), "o": kt(g["L0_attn_Wo"].T, 2).reshape(P, 512),
        "in": kt(g["L1_attn_in_proj_weight"].T, 2).reshape(P, 2048), "xp": kt(xp, 4).reshape(P, 768),
        "dt": np.ascontiguousarray(g["L1_attn_dt_proj_weight"].T), "outw": kt(g["L1_attn_out_proj_weight"].T, 4).reshape(P, 1024),
        "cen": kt(g["L1_ffn_centroids"].T, 2).reshape(P, 32), "we": np.ascontiguousarray(we),
    }


def kernel(**inputs):
    import concourse.bacc as bacc
    from concourse.bass_utils import run_bass_kernel_spmd as run

    arrays = {f"in_{k}": v for k, v in layout(inputs).items()}
    nc = bacc.Bacc("TRN2", target_bir_lowering=False, num_devices=1)
    d = {}
    for k, v in arrays.items():
        d[k[3:]] = nc.dram_tensor(k, v.shape, mybir.dt.from_np(v.dtype), kind="ExternalInput").ap()
    d["out"] = nc.dram_tensor("out", (P, NT, D), F, kind="ExternalOutput").ap()
    build(nc, d)
    r = run(nc, [arrays], core_ids=[0])
    o = r.results[0]["out"]
    return np.ascontiguousarray(o.transpose(1, 0, 2)).reshape(1, S, D)
```

```python
from contextlib import ExitStack

import numpy as np
import concourse.bass as bass
from concourse import mybir

F = mybir.dt.float32
R = mybir.dt.float32r
BF = mybir.dt.bfloat16
U32 = mybir.dt.uint32
ALU = mybir.AluOpType
ACT = mybir.ActivationFunctionType
AX = mybir.AxisListType.X

P = 128
S = 1024
D = 256
NT = S // P
CH = 512
NCH = S // CH
TC = CH // P
FF = 1024
NH = 16
DI = 512
DN = 16
NE = 16
EPS = 1e-5
NB = (2 * S + NE * (P - 1)) // P
WB = 4

CONST = {}
_at = 0
for _name, _n in (("ident", 128), ("CC", 128), ("SS", 128), ("iota", 32), ("b2", 256), ("bqkv", 768), ("bo", 256),
                  ("b1", 8), ("cw", 16), ("dtb", 4), ("Alog", 64), ("Dp", 4), ("gb", 16), ("hot", 32)):
    CONST[_name] = (_at, _n)
    _at += _n
NCONST = _at

WSTAGE = {"qkv": 1536, "o": 512, "in": 2048, "xp": 768, "dt": 512, "outw": 1024, "cen": 32, "sh": 1536}


class Line:

    def __init__(self, engine, sem):
        self.e, self.sem, self.n, self.waited = engine, sem, 0, {}

    def wait(self, *tokens):
        for t in tokens:
            if t is None:
                continue
            if isinstance(t, list):
                self.wait(*t)
                continue
            key, sem, v = t
            if self.waited.get(key, 0) < v:
                self.waited[key] = v
                self.e.wait_ge(sem, v)

    def __call__(self, fn, *tokens, inc=True):
        self.wait(*tokens)
        if not inc:
            fn(self.e)
            return None
        self.n += 1
        fn(self.e).then_inc(self.sem, 1)
        return (self.sem.name, self.sem, self.n)

    @property
    def last(self):
        return (self.sem.name, self.sem, self.n) if self.n else None


class Slots:

    def __init__(self, items):
        self.free = [(i, []) for i in items]

    def get(self):
        return self.free.pop(0)

    def put(self, item, *tokens):
        self.free.append((item, list(tokens)))


class Area:

    def __init__(self, t, n):
        self.t, self.n, self.at = t, n, 0

    def take(self, n):
        a = self.at
        self.at += n
        assert self.at <= self.n, (self.at, self.n)
        return self.t[:, a:a + n]


def build(nc, d):
    ctx = ExitStack()
    with ctx:
        def sb(name, shape, dt):
            return ctx.enter_context(nc.sbuf_tensor(name, shape, dt))

        nsem = [0]

        def sem(name):
            nsem[0] += 1
            return ctx.enter_context(nc.semaphore(name))

        PS = ctx.enter_context(nc.psum_tensor("PS", [P, 8, 512], F))
        X = sb("X", [P, NT, D], F)
        C = sb("C", [P, NCONST], F)
        BC16 = sb("BC16", [P, 3 * P], BF)
        W1Q = sb("W1Q", [P, 2, FF], R)
        W2Q = sb("W2Q", [P, 8, D], R)
        XN = sb("XN", [P, 2, 2, NCH, CH], R)
        HOT = sb("HOT", [P, 32], R)
        TRI = sb("TRI", [P, 2 * P], BF)
        SM = sb("SM", [P, 320], F)
        early = ExitStack()
        NRA, NFA = 22528, 17792
        RA = early.enter_context(nc.sbuf_tensor("RA", [P, NRA], R))
        FA = early.enter_context(nc.sbuf_tensor("FA", [P, NFA], F))
        GX = nc.dram_tensor("GX", [NB * P, D], F, kind="Internal").ap()
        GY = nc.dram_tensor("GY", [NB * P, D], F, kind="Internal").ap()

        pe = Line(nc.tensor, sem("s_pe"))
        act = Line(nc.scalar, sem("s_act"))
        dve = Line(nc.vector, sem("s_dve"))
        pool = Line(nc.gpsimd, sem("s_pool"))
        sp = Line(nc.sync, sem("s_sp"))
        lines = (pe, act, dve, pool)

        def cst(name):
            a, n = CONST[name]
            return C[:, a:a + n]

        ident = cst("ident")
        identb, maskS, maskT = (BC16[:, i * P:(i + 1) * P] for i in range(3))

        class Chan:

            def __init__(self, name):
                self.sem, self.n = sem(name), 0

            def __call__(self, out, in_, *tokens):
                sp.wait(*tokens)
                self.n += 16
                nc.sync.dma_start(out, in_).then_inc(self.sem, 16)
                return (self.sem.name, self.sem, self.n)

        def everyone():
            return [x.last for x in lines]

        banks = Slots([PS[:, i, :] for i in range(8)])

        def mm(out, lhsT, rhs, start, stop, *tokens, inc=False, skip=False):
            return pe(lambda e: e.matmul(out, lhsT, rhs, start=start, stop=stop, skip_group_check=skip),
                      *tokens, inc=inc)

        def group(out, pairs, *tokens, start=True, stop=True, skip=False):
            t = None
            for i, (a, b) in enumerate(pairs):
                t = mm(out, a, b, start and i == 0, stop and i == len(pairs) - 1,
                       *(tokens if i == 0 else ()), inc=i == len(pairs) - 1, skip=skip)
            return t

        def three(a, b):
            return [(a[0], b[0]), (a[1], b[0]), (a[0], b[1])]

        def tr(out, in_, *tokens, inc=True):
            return pe(lambda e: e.matmul(out, in_, ident, start=True, stop=True, is_transpose=True),
                      *tokens, inc=inc)

        def split(hi, lo, src, *tokens, on=None):
            on = on or act
            if on is act:
                t1 = act(lambda e: e.activation(hi, src, ACT.Copy), *tokens)
            else:
                t1 = on(lambda e: e.tensor_copy(hi, src), *tokens)
            t2 = dve(lambda e: e.tensor_tensor(lo, src, hi.bitcast(F), ALU.subtract), t1, *tokens)
            return [t1, t2]

        cc = Chan("s_c")
        t_c = cc(C[:, :], d["cst"])
        b16 = FA[:, NFA - 640:NFA]
        t_c16 = Chan("s_b16")(b16, d["b16"])
        t_tri = dve(lambda e: e.tensor_copy(TRI[:, :], b16[:, 384:640]), t_c16)
        t_c16 = dve(lambda e: e.tensor_copy(BC16[:, :], b16[:, 0:384]), t_c16)
        t_x = [None] * NT
        for h in range(2):
            cx = Chan(f"s_x{h}")
            t = cx(X[:, h * 4:h * 4 + 4, :], d["x"][:, h * 4:h * 4 + 4, :])
            for i in range(4):
                t_x[h * 4 + i] = t
        t_hot = dve(lambda e: e.tensor_copy(HOT[:, :], cst("hot")), t_c)

        def quantize():
            fa = Area(FA, NFA)
            out = []
            for i, (name, Q, n) in enumerate((("w1", W1Q, 2), ("w2", W2Q, 8))):
                w = fa.take(2048)
                tmp = fa.take(2048)
                t_w = Chan(f"s_{name}")(w, d[name])
                Qf = Q[:, :, :].rearrange("p a b -> p (a b)")
                s = SM[:, i * 4:i * 4 + 4]
                t = act(lambda e: e.activation(tmp, w, ACT.Abs, accum_out=s[:, 0:1]), t_w)
                bk, fr = banks.get()
                ones = cst("ident")
                ones1 = fa.take(128)
                t1 = dve(lambda e: e.memset(ones1, 1.0))
                t = mm(bk[:, 0:1], ones1, s[:, 0:1], True, True, t, t1, *fr, inc=True)
                t = dve(lambda e: e.tensor_scalar(s[:, 1:2], bk[:, 0:1], 1.0 / (FF * D), 0.7, ALU.mult, ALU.mult), t)
                banks.put(bk, t)
                t = dve(lambda e: e.tensor_scalar(s[:, 2:3], s[:, 1:2], -1.0, None, ALU.mult), t)
                t = dve(lambda e: e.tensor_scalar(tmp, w, s[:, 2:3], None, ALU.is_le), t)
                t = dve(lambda e: e.scalar_tensor_tensor(Qf, w, s[:, 1:2], tmp, ALU.is_ge, ALU.subtract), t)
                out.append(t)
            return out

        t_w1q, t_w2q = quantize()
        b2h = SM[:, 8:8 + 256]
        t_b2h = pool(lambda e: e.tensor_scalar(b2h, cst("b2"), 0.5, None, ALU.mult), t_c)
        eps = SM[:, 300:304]
        mhalf = SM[:, 304:308]
        t_eps = pool(lambda e: e.memset(mhalf, -0.5))

        def norm(ch, tmps, st, t_in, t_xnfree, pair=False):
            tk = []
            for i in range(TC):
                t = ch * TC + i
                a = dve(lambda e: e.bn_stats(st[:, i * 6:i * 6 + 6], X[:, t, :]), t_in[t], t_xnfree)
                tk.append(dve(lambda e: e.bn_aggr(st[:, 24 + 2 * i:26 + 2 * i], st[:, i * 6:i * 6 + 6]), a))
            mv = st[:, 24:32].rearrange("p (t c) -> p t c", c=2)
            rs = st[:, 32:36]
            a = pool(lambda e: e.tensor_scalar(rs, mv[:, :, 1], EPS, None, ALU.add), tk)
            a = pool(lambda e: e.tensor_tensor(rs, rs, mhalf, ALU.pow), a, t_eps)
            if pair:
                bp, f0 = banks2.get()
                b0, b1, f1 = bp[:, 0, :], bp[:, 1, :], []
            else:
                b0, f0 = banks.get()
                b1, f1 = banks.get()
            for i in range(TC):
                t = ch * TC + i
                tmp, fr = tmps.get()
                n = dve(lambda e: e.tensor_scalar(tmp, X[:, t, :], st[:, 24 + 2 * i:25 + 2 * i], rs[:, i:i + 1],
                                                  ALU.subtract, ALU.mult), a, *fr)
                tr(b0[:, i * P:i * P + P], tmp[:, 0:P], n, t_c, *f0, inc=False)
                p = tr(b1[:, i * P:i * P + P], tmp[:, P:2 * P], *f1)
                tmps.put(tmp, p)
            out = []
            for k, b in ((0, b0), (1, b1)):
                tt = split(XN[:, 0, k, ch, :], XN[:, 1, k, ch, :], b, p, t_xnfree)
                if not pair:
                    banks.put(b, *tt)
                out += tt
            if pair:
                banks2.put(bp, *out)
            return out, n

        def xn(k, ch, a=0, b=CH):
            return (XN[:, 0, k, ch, a:b], XN[:, 1, k, ch, a:b])

        def ffn0(t_in):
            bar = everyone()
            ra, fa = Area(RA, NRA), Area(FA, NFA)
            H = [ra.take(8 * CH).rearrange("p (f n) -> p f n", f=8) for _ in range(2)]
            t_hfree = [None] * 8
            hs = Slots([fa.take(CH) for _ in range(4)])
            tmps = Slots([fa.take(D) for _ in range(4)])
            sts = [fa.take(40) for _ in range(NCH)]
            t_out = [None] * NT
            for ln in lines:
                ln.wait(bar)
            for ch in range(NCH):
                st = sts[ch]
                t_xn, t_n = norm(ch, tmps, st, t_in, None)
                Hh, Hl = H
                xa = X[:, ch * TC:ch * TC + TC, :]
                t_b = pool(lambda e: e.tensor_tensor(xa, xa, b2h.unsqueeze(1).broadcast_to([P, TC, D]), ALU.add),
                           t_n, t_b2h)
                accs = [banks.get() for _ in range(TC)]
                t_h = []

                def down(f):
                    for i in range(TC):
                        acc, fr = accs[i]
                        t = group(acc[:, 0:D], [(Hh[:, f, i * P:i * P + P], W2Q[:, f, :]),
                                                (Hl[:, f, i * P:i * P + P], W2Q[:, f, :])],
                                  t_h[f], t_w2q, *(fr if f == 0 else ()), start=f == 0, stop=f == 7)
                        if f == 7:
                            accs[i] = (acc, t)
                    t_hfree[f] = t

                for f in range(8):
                    bk, fr = banks.get()
                    ps = [(W1Q[:, k, f * P:f * P + P], x) for k in range(2) for x in xn(k, ch)]
                    t = group(bk, ps, t_xn, t_w1q, *fr)
                    h, fh = hs.get()
                    b1 = cst("b1")[:, f:f + 1]
                    t = act(lambda e: e.activation(h, bk, ACT.Gelu, bias=b1), t, *fh)
                    banks.put(bk, t)
                    tt = split(Hh[:, f, :], Hl[:, f, :], h, t, t_hfree[f], on=dve)
                    hs.put(h, *tt)
                    t_h.append(tt)
                    if f:
                        down(f - 1)
                down(7)
                for i in range(TC):
                    acc, t = accs[i]
                    xt = X[:, ch * TC + i, :]
                    t = dve(lambda e: e.scalar_tensor_tensor(xt, acc[:, 0:D], 0.5, xt, ALU.mult, ALU.add), t, t_b)
                    banks.put(acc, t)
                    t_out[ch * TC + i] = t
            return t_out

        def stage_of():
            return [FA[:, NFA - 3072:NFA - 1536], FA[:, NFA - 1536:NFA]]

        wst = stage_of()
        ch_w = [Chan("s_wst0"), Chan("s_wst1")]

        def attention(t_in):
            bar = everyone()
            for ln in lines:
                ln.wait(bar)
            ra, fa = Area(RA, NRA), Area(FA, NFA - 3072)
            Wq = [ra.take(1536).rearrange("p (k n) -> p k n", k=2) for _ in range(2)]
            Wo = [ra.take(512).rearrange("p (k n) -> p k n", k=2) for _ in range(2)]
            KT = ra.take(8 * S).rearrange("p (j n) -> p j n", j=8)
            QT = ra.take(8 * CH).rearrange("p (j n) -> p j n", j=8)
            Qall = ra.take(TC * 1024)
            kk = ra.take(2048)
            Ks = Slots([kk[:, 0:1024], kk[:, 1024:2048]])
            V = fa.take(8 * 512).rearrange("p (t n) -> p t n", t=8)
            PT = Slots([fa.take(1024) for _ in range(8)])
            sets = Slots([])
            set0 = (fa.take(512), fa.take(512), fa.take(512))
            raw = fa.take(512)
            sts_ = [fa.take(40) for _ in range(NCH)]
            rc = fa.take(16)
            M = fa.take(16)
            att = wst[0][:, 0:1024].rearrange("p (t n) -> p t n", t=TC)
            w1_ = wst[1]
            set1 = (w1_[:, 0:512], w1_[:, 512:1024], w1_[:, 1024:1536])
            t = ch_w[0](wst[0], d["qkv"], bar)
            t_wq = split(Wq[0].rearrange("p k n -> p (k n)"), Wq[1].rearrange("p k n -> p (k n)"), wst[0], t, on=dve)
            t = ch_w[1](wst[1][:, 0:512], d["o"], bar)
            t_wo = split(Wo[0].rearrange("p k n -> p (k n)"), Wo[1].rearrange("p k n -> p (k n)"), wst[1][:, 0:512], t, on=dve)
            t_wst = [t_wq[1], t_wo[1]]
            sets.free = [(set0, []), (set1, list(t_wst))]
            t_attfree = list(t_wst)
            pads = []
            Qv = Qall.bitcast(F).rearrange("p (t h c) -> p (t h) c", t=TC, c=64)
            pads.append(pool(lambda e: e.memset(Qv[:, :, 32:48], 0.0)))
            kv = kk.bitcast(F).rearrange("p (t h c) -> p (t h) c", t=2, c=64)
            pads.append(pool(lambda e: e.memset(kv[:, :, 32:34], -1.0)))
            pads.append(pool(lambda e: e.memset(kv[:, :, 34:48], 0.0)))
            vv = V.rearrange("p t (h c) -> p (t h) c", c=32)
            pads.append(pool(lambda e: e.memset(vv[:, :, 16:17], 1.0)))
            pads.append(pool(lambda e: e.memset(vv[:, :, 17:32], 0.0)))
            t_out = [None] * NT
            Q4 = Qall.rearrange("p (t h c) -> p t h c", t=TC, c=64)
            shared = {"raw": None, "kt": [], "qfree": None, "att": t_attfree, "qt": [None] * 4}

            def project(ch):
                qkv0, f0_ = sets.get()
                tmps = Slots([qkv0[1][:, 0:256], qkv0[1][:, 256:512], qkv0[2][:, 0:256], qkv0[2][:, 256:512]])
                tmps.free = [(x, list(f0_)) for x, _ in tmps.free]
                t_xn, t_n = norm(ch, tmps, sts_[ch], t_in, None, pair=True)
                sets.put(qkv0, *[f for _, f in tmps.free])
                xa = X[:, ch * TC:ch * TC + TC, :]
                bo = cst("bo").unsqueeze(1).broadcast_to([P, TC, D])
                t_b = pool(lambda e: e.tensor_tensor(xa, xa, bo, ALU.add), t_n, t_c)
                if ch:
                    z_ = pool(lambda e: e.memset(Qv[:, :, 32:34], 0.0), shared["qfree"])
                else:
                    z_ = pads
                t_q = []
                yield
                for i in range(TC):
                    t = ch * TC + i
                    A = [xn(k, ch, i * P, i * P + P) for k in range(2)]
                    bk, fr = banks2.get()
                    m0 = group(bk[:, 0, :], [p for k in range(2) for p in three(A[k], [w[:, k, 0:512] for w in Wq])],
                               t_xn, t_wq, *fr)
                    m1 = group(bk[:, 1, 0:256], [p for k in range(2) for p in three(A[k], [w[:, k, 512:768] for w in Wq])])
                    yield
                    st, fs = sets.get()
                    qk, t1b, t2b = st
                    bq = cst("bqkv")[:, 0:512]
                    bv = cst("bqkv")[:, 512:768].rearrange("p (h c) -> p h c", c=16)
                    r1 = dve(lambda e: e.tensor_tensor(qk, bk[:, 0, :], bq, ALU.add), m0, *fs)
                    vt = V[:, t, :].rearrange("p (h c) -> p h c", c=32)[:, :, 0:16]
                    r2 = dve(lambda e: e.tensor_tensor(vt, bk[:, 1, 0:256].rearrange("p (h c) -> p h c", c=16), bv, ALU.add),
                             m1, pads)
                    banks2.put(bk, r1, r2)
                    cs = cst("CC")[:, t * 16:t * 16 + 16].unsqueeze(1).broadcast_to([P, 32, 16])
                    q3 = qk.rearrange("p (h c) -> p h c", c=16)
                    o3 = t1b.rearrange("p (h c) -> p h c", c=16)
                    w3 = t2b.rearrange("p (h c) -> p h c", c=16)
                    se = cst("SS")[:, t * 16:t * 16 + 8].unsqueeze(1).broadcast_to([P, 32, 8])
                    so = cst("SS")[:, t * 16 + 8:t * 16 + 16].unsqueeze(1).broadcast_to([P, 32, 8])
                    a = pool(lambda e: e.tensor_tensor(o3, q3, cs, ALU.mult), r1, *fs)
                    b = dve(lambda e: e.tensor_tensor(w3[:, :, 0:8], q3[:, :, 8:16], se, ALU.mult), r1)
                    c = dve(lambda e: e.tensor_tensor(w3[:, :, 8:16], q3[:, :, 0:8], so, ALU.mult))
                    yield
                    r = dve(lambda e: e.tensor_tensor(qk, t1b, t2b, ALU.add), a, b, c)
                    rq = qk[:, 0:256].rearrange("p (h c) -> p h c", c=16)
                    rk = qk[:, 256:512].rearrange("p (h c) -> p h c", c=16)
                    Q3 = Q4[:, i, :, :]
                    ks, fk = Ks.get()
                    K3 = ks.rearrange("p (h c) -> p h c", c=64)
                    g1 = act(lambda e: e.activation(K3[:, :, 0:16], rk, ACT.Copy), r, pads, *fk)
                    e1 = act(lambda e: e.activation(Q3[:, :, 0:16], rq, ACT.Copy), z_, shared["qfree"])
                    g2 = act(lambda e: e.activation(K3[:, :, 16:32], rk, ACT.Copy))
                    e2 = act(lambda e: e.activation(Q3[:, :, 48:64], rq, ACT.Copy))
                    g3 = dve(lambda e: e.tensor_tensor(K3[:, :, 48:64], rk, K3[:, :, 0:16].bitcast(F), ALU.subtract), g1)
                    e3 = dve(lambda e: e.tensor_tensor(Q3[:, :, 16:32], rq, Q3[:, :, 0:16].bitcast(F), ALU.subtract), e1)
                    sets.put(st, e3, e2, g3, g2)
                    t_q.append([e1, e2, e3])
                    yield
                    bk, fr = banks2.get()
                    for jj in range(8):
                        p = tr(bk[:, jj // 4, (jj % 4) * P:(jj % 4) * P + P], ks[:, jj * P:jj * P + P].bitcast(F),
                               g1, g2, g3, *fr, inc=jj == 7)
                    Ks.put(ks, p)
                    dst = KT[:, :, t * P:t * P + P]
                    src = bk.rearrange("p b (j n) -> p (b j) n", n=P)
                    if i % 2:
                        tk = act(lambda e: e.activation(dst, src, ACT.Copy), p)
                    else:
                        tk = dve(lambda e: e.tensor_copy(dst, src), p)
                    banks2.put(bk, tk)
                    shared["kt"].append(tk)
                    yield
                shared["q", ch] = [t_q, z_]
                shared["b", ch] = t_b

            def turn(ch, g, toks, free, on):
                bk, fr = banks2.get()
                for b in range(2):
                    j = 2 * g + b
                    for i in range(TC):
                        p = tr(bk[:, b, i * P:i * P + P], Qall[:, i * 1024 + j * P:i * 1024 + j * P + P].bitcast(F),
                               toks, *fr, inc=b == 1 and i == TC - 1)
                dst = QT[:, 2 * g:2 * g + 2, :]
                if on is act:
                    tk = act(lambda e: e.activation(dst, bk, ACT.Copy), p, free)
                else:
                    tk = dve(lambda e: e.tensor_copy(dst, bk), p, free)
                banks2.put(bk, tk)
                return tk, p

            def maxima(ch, g):
                tq, _ = turn(ch, g, shared["q", ch], shared["qt"][g], dve)
                yield
                M3 = M.rearrange("p (t h) -> p t h", t=TC)
                Ms = M3
                kt_ = list(shared["kt"])
                t_m = shared.get("m")
                for i in range(TC):
                    w = (ch * TC + i + 1) * P
                    for hh in range(4):
                        j, o = 2 * g + hh // 2, 64 * (hh % 2)
                        bk, fr = banks2.get()
                        flat = bk.rearrange("p b n -> p (b n)")
                        for c0 in range(0, w, 512):
                            c1 = min(w, c0 + 512)
                            mm(flat[:, c0:c1], QT[o:o + 64, j, i * P:i * P + P], KT[o:o + 64, j, c0:c1], True,
                               c1 < w, tq, kt_, *fr)
                        m = mm(flat[:, w - P:w], identb, maskS, False, True, t_c16, inc=True)
                        r = dve(lambda e: e.reduce_max(M3[:, i, hh:hh + 1], flat[:, 0:w], AX), m, t_m)
                        banks2.put(bk, r)
                        yield
                a = dve(lambda e: e.tensor_copy(Q4[:, :, 4 * g:4 * g + 4, 32], M3), r)
                b = dve(lambda e: e.tensor_tensor(Q4[:, :, 4 * g:4 * g + 4, 33], M3, Q4[:, :, 4 * g:4 * g + 4, 32].bitcast(F),
                                                  ALU.subtract), a)
                shared["m"] = b
                yield
                shared["q2", g], shared["qfree"] = turn(ch, g, [a, b], m, dve if ch == 0 else dve)

            def heads(ch, g):
                nk = ch * TC + TC
                pend = None
                acc = None
                tq2 = shared["q2", g]

                def pv(kp, slots):
                    t = None
                    for u in range(2):
                        kt = 2 * kp + u
                        c0 = max(0, (kt - ch * TC) * P)
                        for hh in range(4):
                            pt, te = slots[hh]
                            t = mm(acc[0][32 * hh:32 * hh + 32, c0:CH], V[:, kt, (4 * g + hh) * 32:(4 * g + hh) * 32 + 32],
                                   pt[:, u * 512 + c0:u * 512 + CH], kt == 0, kt == nk - 1, te, *acc[1],
                                   inc=hh == 3 and u == 1)
                    for pt, te in slots:
                        PT.put(pt, t)
                    return t

                for kp in range(nk // 2 + 1):
                    if kp < nk // 2:
                        slots = []
                        for hh in range(4):
                            j, o = 2 * g + hh // 2, 64 * (hh % 2)
                            bk, fr = banks2.get()
                            pt, fp = PT.get()
                            for u in range(2):
                                kt = 2 * kp + u
                                c0 = max(0, (kt - ch * TC) * P)
                                diag = kt >= ch * TC
                                t = mm(bk[:, u, c0:CH], KT[o:o + 64, j, kt * P:kt * P + P], QT[o:o + 64, j, c0:CH],
                                       True, not diag, tq2, *fr, inc=not diag)
                                if diag:
                                    t = mm(bk[:, u, c0:c0 + P], identb, maskT, False, True, inc=True)
                            c0 = max(0, (2 * kp - ch * TC) * P)
                            c1 = max(0, (2 * kp + 1 - ch * TC) * P)
                            p2 = pt.rearrange("p (u n) -> p u n", u=2)
                            if c0 == c1:
                                te = act(lambda e: e.activation(p2, bk, ACT.Exp, scale=0.25), t, *fp)
                            else:
                                te = act(lambda e: e.activation(p2[:, 0, c0:], bk[:, 0, c0:], ACT.Exp, scale=0.25), t, *fp)
                                te = act(lambda e: e.activation(p2[:, 1, c1:], bk[:, 1, c1:], ACT.Exp, scale=0.25), t)
                            banks2.put(bk, te)
                            slots.append((pt, te))
                            yield
                    if pend:
                        if pend[0] == 0:
                            acc = banks.get()
                        t = pv(*pend)
                        yield
                    pend = (kp, slots)
                shared["qt"][g] = t
                t = dve(lambda e: e.tensor_copy(raw, acc[0]), t, shared["raw"])
                banks.put(acc[0], t)
                yield
                bk, fr = banks.get()
                for i in range(TC):
                    p = tr(bk[:, i * P:i * P + P], raw[:, i * P:i * P + P], t, *fr, inc=i == TC - 1)
                shared["raw"] = p
                b4 = bk.rearrange("p (t h c) -> p t h c", h=4, c=32)
                r3 = rc.rearrange("p (t h) -> p t h", h=4)
                a = dve(lambda e: e.reciprocal(r3, b4[:, :, :, 16]), p, shared.get("rc"))
                o4 = att[:, :, g * 64:g * 64 + 64].rearrange("p t (h c) -> p t h c", c=16)
                a = dve(lambda e: e.tensor_tensor(o4, b4[:, :, :, 0:16], r3.unsqueeze(3).broadcast_to([P, TC, 4, 16]),
                                                  ALU.mult), a, shared["att"])
                shared["rc"] = a
                banks.put(bk, a)

            def output(ch):
                yield
                bk, fr = banks2.get()
                for i in range(TC):
                    for k in range(2):
                        p = tr(bk[:, k, i * P:i * P + P], att[:, i, k * P:k * P + P], shared["rc"], *fr,
                               inc=i == TC - 1 and k == 1)
                shared["att"] = p
                AT = [XN[:, s_, :, ch, :] for s_ in range(2)]
                tt = split(AT[0], AT[1], bk, p)
                banks2.put(bk, *tt)
                yield
                for i in range(TC):
                    bk, fr = banks.get()
                    A = [[a[:, k, i * P:i * P + P] for a in AT] for k in range(2)]
                    m = group(bk[:, 0:D], [q for k in range(2) for q in three(A[k], [w[:, k, :] for w in Wo])],
                              tt, t_wo, *fr)
                    xt = X[:, ch * TC + i, :]
                    t = dve(lambda e: e.tensor_tensor(xt, bk[:, 0:D], xt, ALU.add), m, shared["b", ch])
                    banks.put(bk, t)
                    t_out[ch * TC + i] = t
                    yield

            def chain(*gens):
                for g_ in gens:
                    yield from g_

            def weave(*gens):
                live_ = [list(x) for x in gens]
                while live_:
                    for x in list(live_):
                        for _ in range(x[1]):
                            try:
                                next(x[0])
                            except StopIteration:
                                live_.remove(x)
                                break

            weave((project(0), 1))
            weave((maxima(0, 0), 1))
            for g in range(3):
                weave((maxima(0, g + 1), 2), (heads(0, g), 1))
            weave((chain(heads(0, 3), output(0)), 1), (project(1), 2))
            weave((maxima(1, 0), 1))
            for g in range(3):
                weave((maxima(1, g + 1), 1), (heads(1, g), 1))
            weave((heads(1, 3), 1))
            weave((output(1), 1))
            return t_out

        nmoe = [0]
        ch_g = [Chan(f"s_g{i}") for i in range(2)]
        ch_y = [Chan(f"s_y{i}") for i in range(2)]
        ch_s = [Chan(f"s_s{i}") for i in range(2)]
        s_scat = sem("s_scat")
        s_gath = [sem(f"s_gath{i}") for i in range(NT)]

        def experts(t_in):
            u_ = nmoe[0]
            nmoe[0] += 1
            bar = everyone()
            for ln in lines:
                ln.wait(bar)
            ra, fa = Area(RA, NRA), Area(FA, NFA)
            Cn = [ra.take(32).rearrange("p (k n) -> p k n", k=2) for _ in range(2)]
            WS = [[ra.take(768) for _ in range(2)] for _ in range(2)]
            H = Slots([[ra.take(CH) for _ in range(2)] for _ in range(3)])
            st_, cen = [fa.take(40) for _ in range(NCH)], fa.take(32)
            XT = fa.take(NT * D).rearrange("p (t n) -> p t n", t=NT)
            tmps = Slots([XT[:, i, :] for i in range(NT)])
            bufs = Slots([fa.take(CH) for _ in range(4)])
            small = Area(fa.take(1100), 1100)
            xin = Slots([fa.take(WB * D) for _ in range(2)])
            yout = Slots([fa.take(WB * D) for _ in range(2)])
            xts = Slots([fa.take(2 * D) for _ in range(2)])
            hb = Slots([fa.take(2 * P) for _ in range(2)])
            sg = Slots([fa.take(2 * P) for _ in range(2)])
            hts = Slots([fa.take(2 * P) for _ in range(2)])
            yg = Slots([fa.take(D) for _ in range(4)])
            sts = [bufs.free[0][0], None]
            sts = [fa.take(768) for _ in range(2)]
            t = ch_w[0](cen, d["cen"], bar)
            t_cn = split(Cn[0].rearrange("p k n -> p (k n)"), Cn[1].rearrange("p k n -> p (k n)"), cen, t, on=dve)
            t_ws = []
            for n in range(2):
                t = ch_s[n](sts[n], d["we"][n], bar)
                t_ws.append(split(WS[n][0], WS[n][1], sts[n], t, on=dve))
            t_xns, t_n = [], []
            for ch in range(NCH):
                t_xn, tn = norm(ch, tmps, st_[ch], t_in, None)
                t_xns.append(t_xn)
                t_n.append(tn)
            bk, fr = banks.get()
            for ch in range(NCH):
                for i in range(TC):
                    A = [xn(k, ch, i * P, i * P + P) for k in range(2)]
                    o = (ch * TC + i) * 16
                    m = group(bk[:, o:o + 16], [q for k in range(2) for q in three(A[k], [w[:, k, :] for w in Cn])],
                              t_xns[ch], t_cn, *fr)

            def t8(n):
                return small.take(NT * n).rearrange("p (t e) -> p t e", t=NT)

            aff, bi, o1, o2, top, ix = t8(16), t8(16), t8(16), t8(16), t8(8), t8(8).bitcast(U32)
            mb = t8(8).bitcast(BF)
            wt1, wt2, sm, s1, s2 = (small.take(NT) for _ in range(5))
            i1, i2 = small.take(NT).bitcast(U32), small.take(NT).bitcast(U32)
            nblk, endb, base, one16 = (small.take(16) for _ in range(4))
            eid = small.take(32).bitcast(U32)
            cmp_ = bufs.free[0][0][:, 0:NB * 16].rearrange("p (b e) -> p b e", e=16)
            es = small.take(32)
            z = dve(lambda e: e.memset(one16, 1.0))
            a = act(lambda e: e.activation(aff, bk[:, 0:128].rearrange("p (t e) -> p t e", e=16), ACT.Sigmoid), m)
            banks.put(bk, a)
            gb = cst("gb").unsqueeze(1).broadcast_to([P, NT, 16])
            b = dve(lambda e: e.tensor_tensor(bi, aff, gb, ALU.add), a)
            tops = [dve(lambda e: e.max(top[:, i, :], bi[:, i, :]), b) for i in range(NT)]
            ixs = [dve(lambda e: e.max_index(ix[:, i, :], top[:, i, :], bi[:, i, :]), tops[i]) for i in range(NT)]
            io = cst("iota")[:, 0:16].unsqueeze(1).broadcast_to([P, NT, 16])
            c1 = dve(lambda e: e.tensor_tensor(o1, io, ix[:, :, 0:1].broadcast_to([P, NT, 16]), ALU.is_equal), ixs)
            c2 = dve(lambda e: e.tensor_tensor(o2, io, ix[:, :, 1:2].broadcast_to([P, NT, 16]), ALU.is_equal), ixs)
            c = dve(lambda e: e.tensor_tensor(mb, o1, o2, ALU.add), c1, c2)
            bk, fr = banks.get()
            for t in range(NT):
                ps = [(TRI[:, P:2 * P], mb[:, u, :]) for u in range(t)] + [(TRI[:, 0:P], mb[:, t, :])]
                group(bk[:, t * 16:t * 16 + 16], ps, c, t_tri, *fr)
            m = group(bk[:, 128:144], [(TRI[:, P:2 * P], mb[:, u, :]) for u in range(NT)])

            accs = [banks.get() for _ in range(4)]
            fin = [None] * NT

            def down(n, ch, hh, tt):
                for i in range(TC):
                    t = ch * TC + i
                    acc, f_ = accs[t // 2]
                    o = acc[:, (t % 2) * D:(t % 2) * D + D]
                    fin[t] = group(o, three([x[:, i * P:i * P + P] for x in hh], [x[:, 512:768] for x in WS[n]]), tt,
                                   *(f_ if n == 0 else ()), start=n == 0 and t % 2 == 0, stop=n == 1, skip=True)
                H.put(hh, fin[t])

            def gateup(n, ch):
                bg, fg = banks.get()
                bu, fu = banks.get()
                X2 = [xn(k, ch) for k in range(2)]
                w = WS[n]
                mg = group(bg, [q for k in range(2) for q in three([x[:, k * 256:k * 256 + P] for x in w], X2[k])],
                           t_ws[n], t_xns[ch], *fg)
                mu = group(bu, [q for k in range(2) for q in three([x[:, k * 256 + P:k * 256 + 2 * P] for x in w], X2[k])], *fu)
                s_, fs = bufs.get()
                t = act(lambda e: e.activation(s_, bg, ACT.Silu), mg, *fs)
                banks.put(bg, t)
                return n, ch, bu, mu, s_, t

            def middle(n, ch, bu, mu, s_, t):
                h, fh = bufs.get()
                t = dve(lambda e: e.scalar_tensor_tensor(h, s_, 0.1, bu, ALU.mult, ALU.mult), t, mu, *fh)
                banks.put(bu, t)
                bufs.put(s_, t)
                hh, fhh = H.get()
                tt = split(hh[0], hh[1], h, t, *fhh, on=dve)
                bufs.put(h, *tt)
                return n, ch, hh, tt

            cb, cf = bufs.get()
            g0 = gateup(0, 0)
            r = bk[:, 0:128].rearrange("p (t e) -> p t e", e=16)
            ui = i1.bitcast(U32)
            nu = nblk.bitcast(U32)
            c = dve(lambda e: e.tensor_scalar(nu, bk[:, 128:144], float(P - 1), None, ALU.add), m)
            c = dve(lambda e: e.tensor_scalar(nu, nu, 7, None, ALU.logical_shift_right), c)
            c = dve(lambda e: e.tensor_copy(base, nu), c)
            c = dve(lambda e: e.tensor_tensor_scan(endb, one16, base, 0.0, ALU.mult, ALU.add), c, z)
            ce = c
            c = dve(lambda e: e.tensor_tensor(base, endb, base, ALU.subtract), c)
            c = dve(lambda e: e.tensor_scalar(base, base, float(P), None, ALU.mult), c)
            c = dve(lambda e: e.tensor_tensor(bi, r, base.unsqueeze(1).broadcast_to([P, NT, 16]), ALU.add), c)
            banks.put(bk, c)
            t_i = []
            for o, s_, ii in ((o1, s1, i1), (o2, s2, i2)):
                x = top_ = cmp_ if False else None
                a = dve(lambda e: e.tensor_tensor(cb[:, 0:128].rearrange("p (t e) -> p t e", e=16), bi, o, ALU.mult), c, *cf, *t_i[-1:])
                a = dve(lambda e: e.reduce_sum(s_, cb[:, 0:128].rearrange("p (t e) -> p t e", e=16), AX), a)
                t_i.append(dve(lambda e: e.tensor_copy(ii, s_), a))
            pool.wait(t_i, t_n, t_gx if u_ == 0 else None, t_gxfree[0])
            for t in range(NT):
                for ii in (i1, i2):
                    nc.gpsimd.indirect_dma_start(GX, bass.IndirectOffsetOnAxis(ap=ii[:, t:t + 1], axis=0), XT[:, t, :],
                                                 None).then_inc(s_scat, 16)
            t_sc = (s_scat.name, s_scat, 16 * 2 * NT * (u_ + 1))
            cmp0 = cb[0:1, 0:NB * 16].rearrange("p (b e) -> p b e", e=16)
            a = dve(lambda e: e.tensor_tensor(cmp0, cst("iota")[0:1, 0:NB].unsqueeze(2).broadcast_to([1, NB, 16]),
                                              endb[0:1, :].unsqueeze(1).broadcast_to([1, NB, 16]), ALU.is_ge), ce, t_i)
            a = dve(lambda e: e.reduce_sum(es[0:1, 0:NB], cmp0, AX), a)
            bufs.put(cb, a)
            t_e = dve(lambda e: e.tensor_scalar(eid[0:1, 0:NB], es[0:1, 0:NB], float(NE - 1), 768.0, ALU.min, ALU.mult), a)
            a1 = dve(lambda e: e.tensor_tensor(o1, o1, aff, ALU.mult), t_i)
            a2 = dve(lambda e: e.tensor_tensor(o2, o2, aff, ALU.mult), t_i)
            a1 = dve(lambda e: e.reduce_sum(wt1, o1, AX), a1)
            a2 = dve(lambda e: e.reduce_sum(wt2, o2, AX), a2)
            a = dve(lambda e: e.tensor_tensor(sm, wt1, wt2, ALU.add), a1, a2)
            a = dve(lambda e: e.tensor_scalar(sm, sm, 1e-9, 2.0, ALU.add, ALU.mult), a)
            a = dve(lambda e: e.reciprocal(sm, sm), a)
            t_w1 = dve(lambda e: e.tensor_tensor(wt1, wt1, sm, ALU.mult), a)
            t_w2 = dve(lambda e: e.tensor_tensor(wt2, wt2, sm, ALU.mult), a)
            g1 = gateup(0, 1)
            m0 = middle(*g0)
            g2 = gateup(1, 0)
            m1 = middle(*g1)
            down(*m0)
            g3 = gateup(1, 1)
            m2 = middle(*g2)
            down(*m1)
            m3 = middle(*g3)
            down(*m2)
            down(*m3)
            t_x1 = [None] * NT
            for t in range(NT):
                acc, _ = accs[t // 2]
                o = acc[:, (t % 2) * D:(t % 2) * D + D]
                xt = X[:, t, :]
                t_x1[t] = dve(lambda e: e.scalar_tensor_tensor(xt, o, 0.5, xt, ALU.mult, ALU.add), fin[t | 1], t_n)
            for a in range(4):
                banks.put(accs[a][0], t_x1[2 * a], t_x1[2 * a + 1])

            t_ld, t_st = {}, []
            gx3 = GX.rearrange("(b p) d -> p b d", p=P)
            gy3 = GY.rearrange("(b p) d -> p b d", p=P)
            groups = [(a, min(NB, a + WB)) for a in range(0, NB, WB)]

            def fetch(gi):
                a, b = groups[gi]
                x_, f_ = xin.get()
                t = ch_g[gi % 2](x_.rearrange("p (b n) -> p b n", n=D)[:, 0:b - a, :], gx3[:, a:b, :], t_sc, *f_)
                return x_, t

            gs = [fetch(0), fetch(1)]
            pairs = [(b, min(NB, b + 2)) for b in range(0, NB, 2)]
            outs = {}

            def stage1(pi):
                a, b = pairs[pi]
                x_, tl = gs[a // WB]
                bk, fr = banks.get()
                for u in range(a, b):
                    for k in range(2):
                        p = tr(bk[:, (u - a) * D + k * P:(u - a) * D + k * P + P],
                               x_[:, (u % WB) * D + k * P:(u % WB) * D + k * P + P], tl, *fr, inc=u == b - 1 and k == 1)
                if b % WB == 0 or b == NB:
                    xin.put(x_, p)
                    if len(gs) < len(groups):
                        gs.append(fetch(len(gs)))
                xt, fx = xts.get()
                w = (b - a) * D
                t = act(lambda e: e.activation(xt[:, 0:w], bk[:, 0:w], ACT.Copy), p, *fx)
                banks.put(bk, t)
                return xt, t

            def stage2(pi, xt, t):
                a, b = pairs[pi]
                bk, fr = banks.get()
                regs = []
                for u in range(a, b):
                    pe.wait(t_e)
                    v = nc.tensor.value_load(eid[0:1, u:u + 1], min_val=0, max_val=768 * (NE - 1))
                    regs.append(v)
                    for k in range(2):
                        m = mm(bk[:, (u - a) * D:(u - a) * D + D], xt[:, (u - a) * D + k * P:(u - a) * D + k * P + P],
                               WE[:, bass.ds(v + k * 256, 256)], k == 0, k == 1, t, t_we, *fr, inc=u == b - 1 and k == 1)
                xts.put(xt, m)
                s_, fs = sg.get()
                h_, fh = hb.get()
                nn = b - a
                b3 = bk.rearrange("p (u g n) -> p u g n", u=2, g=2)
                s3 = s_.rearrange("p (u n) -> p u n", u=2)
                h3 = h_.rearrange("p (u n) -> p u n", u=2)
                q = act(lambda e: e.activation(s3[:, 0:nn, :], b3[:, 0:nn, 0, :], ACT.Silu), m, *fs)
                q = dve(lambda e: e.tensor_tensor(h3[:, 0:nn, :], s3[:, 0:nn, :], b3[:, 0:nn, 1, :], ALU.mult), q, *fh)
                banks.put(bk, q)
                sg.put(s_, q)
                return regs, h_, q

            def stage3(pi, regs, h_, q):
                a, b = pairs[pi]
                bk, fr = banks.get()
                for u in range(b - a):
                    p = tr(bk[:, u * P:u * P + P], h_[:, u * P:u * P + P], q, *fr, inc=u == b - a - 1)
                hb.put(h_, p)
                ht, fh = hts.get()
                w = (b - a) * P
                t = dve(lambda e: e.tensor_copy(ht[:, 0:w], bk[:, 0:w]), p, *fh)
                banks.put(bk, t)
                return regs, ht, t

            def stage4(pi, regs, ht, t):
                a, b = pairs[pi]
                bk, fr = banks.get()
                for u in range(a, b):
                    v = regs[u - a]
                    m = mm(bk[:, (u - a) * D:(u - a) * D + D], ht[:, (u - a) * P:(u - a) * P + P],
                           WE[:, bass.ds(v + 512, 256)], True, True, t, *fr, inc=u == b - 1)
                hts.put(ht, m)
                gi = a // WB
                if gi not in outs:
                    outs[gi] = yout.get()
                y_, fy = outs[gi]
                o = (a % WB) * D
                w = (b - a) * D
                if pi % 2:
                    t = act(lambda e: e.activation(y_[:, o:o + w], bk[:, 0:w], ACT.Copy), m, *fy)
                else:
                    t = dve(lambda e: e.tensor_copy(y_[:, o:o + w], bk[:, 0:w]), m, *fy)
                banks.put(bk, t)
                outs.setdefault(("t", gi), []).append(t)
                if b % WB == 0 or b == NB:
                    ga, gb_ = groups[gi]
                    t = ch_y[gi % 2](gy3[:, ga:gb_, :], y_.rearrange("p (b n) -> p b n", n=D)[:, 0:gb_ - ga, :],
                                     outs[("t", gi)], t_gyfree[0])
                    yout.put(y_, t)
                    t_st.append(t)

            q1, q2, q3 = {}, {}, {}
            for i in range(len(pairs) + 3):
                if i < len(pairs):
                    q1[i] = stage1(i)
                if 0 <= i - 1 < len(pairs):
                    q2[i - 1] = stage2(i - 1, *q1.pop(i - 1))
                if 0 <= i - 2 < len(pairs):
                    q3[i - 2] = stage3(i - 2, *q2.pop(i - 2))
                if 0 <= i - 3 < len(pairs):
                    stage4(i - 3, *q3.pop(i - 3))
            t_gxfree[0] = [gs[-1][1], gs[-2][1]]
            pool.wait(t_st)
            t_out = [None] * NT
            for t in range(NT):
                ys_ = []
                for ii in (i1, i2):
                    y_, f_ = yg.get()
                    pool.wait(*f_)
                    nc.gpsimd.indirect_dma_start(y_, None, GY, bass.IndirectOffsetOnAxis(ap=ii[:, t:t + 1], axis=0))\
                        .then_inc(s_gath[t], 16)
                    ys_.append(y_)
                tg = (s_gath[t].name, s_gath[t], 32 * (u_ + 1))
                xt = X[:, t, :]
                a = dve(lambda e: e.scalar_tensor_tensor(xt, ys_[0], wt1[:, t:t + 1], xt, ALU.mult, ALU.add), tg, t_x1[t], t_w1)
                yg.put(ys_[0], a)
                a = dve(lambda e: e.scalar_tensor_tensor(xt, ys_[1], wt2[:, t:t + 1], xt, ALU.mult, ALU.add), a, t_w2)
                yg.put(ys_[1], a)
                t_out[t] = a
            t_gyfree[0] = tg
            return t_out

        t_gxfree, t_gyfree = [None], [None]

        def mamba(t_in):
            bar = everyone()
            for ln in lines:
                ln.wait(bar)
            ra, fa = Area(RA, NRA), Area(FA, NFA - 3072)

            def wsplit(name, n, i):
                out = [ra.take(n) for _ in range(2)]
                tk = []
                for a in range(0, n, 1536):
                    b = min(n, a + 1536)
                    t = ch_w[i % 2](wst[i % 2][:, 0:b - a], d[name][:, a:b], bar, wst_free[i % 2])
                    tt = split(out[0][:, a:b], out[1][:, a:b], wst[i % 2][:, 0:b - a], t, on=dve)
                    wst_free[i % 2] = tt
                    tk += tt
                    i += 1
                return out, tk, i

            wst_free = [None, None]
            Wi, t_wi, i = wsplit("in", 2048, 0)
            Wx, t_wx, i = wsplit("xp", 768, i)
            Wd, t_wd, i = wsplit("dt", 512, i)
            Wp, t_wp, i = wsplit("outw", 1024, i)
            XC2 = [W1Q[:, :, :].rearrange("p a b -> p (a b)").rearrange("p (m n) -> p m n", m=4),
                   W2Q[:, :, :].rearrange("p a b -> p (a b)").rearrange("p (m n) -> p m n", m=4)]
            DT = [ra.take(CH) for _ in range(2)]
            BCt = ra.take(CH)
            tmps = Slots([fa.take(D) for _ in range(2)])
            st_ = fa.take(40)
            st64 = fa.take(128)
            xr = fa.take(4 * 516).rearrange("p (m n) -> p m n", m=4)
            xc = fa.take(4 * CH).rearrange("p (m n) -> p m n", m=4)
            sz = fa.take(4 * CH).rearrange("p (m n) -> p m n", m=4)
            dl = fa.take(4 * CH).rearrange("p (m n) -> p m n", m=4)
            uu = fa.take(4 * CH).rearrange("p (m n) -> p m n", m=4)
            w6 = [FA[:, NFA - 3072 + CH * i:NFA - 3072 + CH * i + CH] for i in range(6)]
            bs = Slots([fa.take(CH) for _ in range(2)])
            sh = Slots([fa.take(CH) for _ in range(4)])
            sbb = Slots(w6[0:3])
            shc = Slots(w6[3:6])
            for s_ in (sbb, shc):
                s_.free = [(i, wst_free) for i, _ in s_.free]
            state, An = st64[:, 0:64], st64[:, 64:128]
            t_an = act(lambda e: e.activation(An, cst("Alog"), ACT.Exp), t_c)
            t_an = dve(lambda e: e.tensor_scalar(An, An, -1.0, None, ALU.mult), t_an)
            t_z = dve(lambda e: e.memset(xr[:, :, 0:3], 0.0))
            t_st = dve(lambda e: e.memset(state, 0.0))
            t_out = [None] * NT
            t_xc2 = t_dt = t_bc = t_y = t_xr = None
            for ch in range(NCH):
                t_xn, _ = norm(ch, tmps, st_, t_in, None)
                if ch:
                    t_z = dve(lambda e: e.tensor_copy(xr[:, :, 0:3], xr[:, :, 512:515]), t_xr)
                t_xr, t_xc, t_sz = [], [], []
                W3 = [w.rearrange("p (k n) -> p k n", k=2) for w in Wi]
                for m in range(8):
                    bk, fr = banks.get()
                    g = group(bk, [q for k in range(2) for q in three([w[:, k, m * P:m * P + P] for w in W3], xn(k, ch))],
                              t_xn, t_wi, *fr)
                    if m < 4:
                        a = act(lambda e: e.activation(xr[:, m, 3:515], bk, ACT.Copy), g, t_z)
                        banks.put(bk, a)
                        cw = cst("cw")
                        v = xc[:, m, :]
                        a = dve(lambda e: e.tensor_scalar(v, xr[:, m, 0:512], cw[:, 4 * m:4 * m + 1], None, ALU.mult), a, t_z, t_y)
                        for w in range(1, 4):
                            a = dve(lambda e: e.scalar_tensor_tensor(v, xr[:, m, w:w + 512], cw[:, 4 * m + w:4 * m + w + 1],
                                                                     v, ALU.mult, ALU.add), a)
                        t_xr.append(a)
                        a = act(lambda e: e.activation(v, v, ACT.Silu), a)
                        tt = split(XC2[0][:, m, :], XC2[1][:, m, :], v, a, t_xc2, on=dve)
                        t_xc.append([a] + tt)
                    else:
                        a = act(lambda e: e.activation(sz[:, m - 4, :], bk, ACT.Silu), g, t_y)
                        banks.put(bk, a)
                        t_sz.append(a)
                X3 = [w.rearrange("p (k n) -> p k n", k=4) for w in Wx]
                bd, fd = banks.get()
                bb, fb = banks.get()
                g1 = group(bd, [q for k in range(4) for q in three([w[:, k, 0:P] for w in X3], [x[:, k, :] for x in XC2])],
                           t_xc, t_wx, *fd)
                g2 = group(bb[0:64, :], [q for k in range(4) for q in three([w[:, k, P:P + 64] for w in X3], [x[:, k, :] for x in XC2])],
                           *fb)
                t_xc2 = g2
                t_dd = split(DT[0], DT[1], bd, g1, t_dt)
                banks.put(bd, *t_dd)
                a = act(lambda e: e.activation(BCt[0:64, :], bb[0:64, :], ACT.Copy), g2, t_bc)
                t_bb = dve(lambda e: e.tensor_tensor(BCt[32:64, :], bb[32:64, :], BCt[32:64, :].bitcast(F), ALU.subtract), a)
                banks.put(bb, t_bb)
                D3 = [w.rearrange("p (m n) -> p m n", m=4) for w in Wd]
                dd = []
                for m in range(4):
                    bk, fr = banks.get()
                    g = group(bk, three([w[:, m, :] for w in D3], DT), t_dd, t_wd, *fr)
                    b = cst("dtb")[:, m:m + 1]
                    v = dl[:, m, :]
                    u = uu[:, m, :]
                    a = act(lambda e: e.activation(v, bk, ACT.Abs, bias=b), g, t_y)
                    r = act(lambda e: e.activation(u, bk, ACT.Relu, bias=b), g, t_y)
                    banks.put(bk, a, r)
                    dd.append((v, u, a, r))
                t_dt = g
                ee = [act(lambda e, v=v: e.activation(v, v, ACT.Exp, scale=-1.0), a) for v, u, a, r in dd]
                ll = [act(lambda e, v=v: e.activation(v, v, ACT.Ln, bias=1.0), x) for (v, u, a, r), x in zip(dd, ee)]
                t_dl, t_u = [], []
                for m in range(4):
                    v, u, _, r = dd[m]
                    a = dve(lambda e: e.tensor_tensor(v, v, u, ALU.add), ll[m], r)
                    t_dl.append(a)
                    t_u.append(dve(lambda e: e.tensor_tensor(u, v, xc[:, m, :], ALU.mult), a, t_xc[m]))
                ys = [banks.get() for _ in range(4)]
                ab = Slots([banks.get() for _ in range(2)])
                cb, cfree = banks.get()
                bb, bfree = banks.get()
                gy = [None] * 4
                live = {}
                pend = []

                def spread_b(n):
                    return mm(bb, HOT[0:64, n:n + 1].broadcast_to([64, P]), BCt[0:64, :], True, True, t_bb, t_hot,
                              *live.get("b", bfree), inc=True)

                def store_b(g):
                    s_, f_ = bs.get()
                    t = act(lambda e: e.activation(s_, bb, ACT.Copy), g, *f_)
                    live["b"] = [t]
                    return s_, t

                def bring_c(n):
                    return mm(cb, HOT[0:64, 16 + n:17 + n].broadcast_to([64, P]), BCt[0:64, :], True, True,
                              *live.get("c", cfree), inc=True)

                def close():
                    n, m, h_, t3, gC = pend.pop(0)
                    c_, fc_ = shc.get()
                    t4 = dve(lambda e: e.tensor_tensor(c_, h_, cb, ALU.mult), t3, gC(), *fc_)
                    sh.put(h_, t4, live.get("s"))
                    live["c"] = [t4]
                    if m == 3 and n + 1 < DN:
                        tc[n + 1] = bring_c(n + 1)
                    yb, fy = ys[m]
                    gy[m] = mm(yb, ident, c_, n == 0, n == DN - 1, t4, *(fy if n == 0 else ()), inc=True)
                    shc.put(c_, gy[m])

                nb = store_b(spread_b(0))
                tc = {0: bring_c(0)}
                for n in range(DN):
                    Bs, t_B = nb
                    for m in range(4):
                        if m == 0 and n + 1 < DN:
                            gb = spread_b(n + 1)
                        k = 16 * m + n
                        (a_, _), fa_ = ab.get()
                        fa_ = fa_ or _
                        t1 = act(lambda e: e.activation(a_, dl[:, m, :], ACT.Exp, scale=An[:, k:k + 1]), t_dl[m], t_an, *fa_)
                        b_, fb_ = sbb.get()
                        t2 = pool(lambda e: e.tensor_tensor(b_, uu[:, m, :], Bs, ALU.mult), t_u[m], t_B, *fb_)
                        h_, fh_ = sh.get()
                        init = state[:, k:k + 1] if ch else 0.0
                        t3 = dve(lambda e: e.tensor_tensor_scan(h_, a_, b_, init, ALU.mult, ALU.add), t1, t2, t_st, *fh_)
                        ab.put((a_, _), t3)
                        sbb.put(b_, t3)
                        if len(pend) == 2:
                            close()
                        if m == 2 and n + 1 < DN:
                            nb = store_b(gb)
                        if ch + 1 < NCH:
                            live["s"] = dve(lambda e: e.tensor_copy(state[:, k:k + 1], h_[:, CH - 1:CH]), t3)
                        pend.append((n, m, h_, t3, lambda n=n: tc[n]))
                    bs.put(Bs, t2)
                while pend:
                    close()
                t_bc = pe.last
                t_st = live.get("s")
                for x in ((cb, live["c"]), (bb, live["b"])):
                    banks.put(x[0], *x[1])
                for (a_, _), f in ab.free:
                    banks.put(a_, *f)
                t_y, t_ys = [], []
                for m in range(4):
                    yb, _ = ys[m]
                    u = uu[:, m, :]
                    a = dve(lambda e: e.scalar_tensor_tensor(u, xc[:, m, :], cst("Dp")[:, m:m + 1], yb, ALU.mult, ALU.add), gy[m])
                    banks.put(yb, a)
                    a = dve(lambda e: e.tensor_tensor(u, u, sz[:, m, :], ALU.mult), a, t_sz[m])
                    tt = split(XC2[0][:, m, :], XC2[1][:, m, :], u, a, t_xc2, on=dve)
                    t_ys.append(tt)
                    t_y += [a] + tt
                P3 = [w.rearrange("p (k n) -> p k n", k=4) for w in Wp]
                for i in range(TC):
                    bk, fr = banks.get()
                    g = group(bk[:, 0:D], [q for k in range(4) for q in three([x[:, k, i * P:i * P + P] for x in XC2],
                                                                              [w[:, k, :] for w in P3])], t_ys, t_wp, *fr)
                    xt = X[:, ch * TC + i, :]
                    a = dve(lambda e: e.tensor_tensor(xt, bk[:, 0:D], xt, ALU.add), g)
                    banks.put(bk, a)
                    t_out[ch * TC + i] = a
                t_xc2 = g
                t_y.append(g)
            return t_out

        class Pairs:

            def get(self):
                if not self.own:
                    raise AssertionError
                return self.own.pop(0)

            def put(self, bk, *tokens):
                self.own.append((bk, list(tokens)))

        banks2 = Pairs()

        def lend():
            frs = {}
            got = [banks.get() for _ in range(8)]
            for b, f in got:
                frs[b.offset] = (b, f)
            order = sorted(frs)
            lst = [frs[o] for o in order]
            banks2.own = [(PS[:, 2 * i:2 * i + 2, :], lst[2 * i][1] + lst[2 * i + 1][1]) for i in range(3)]
            for b, f in lst[6:]:
                banks.put(b, *f)

        def unlend():
            for bk, f in banks2.own:
                banks.put(bk[:, 0, :], *f)
                banks.put(bk[:, 1, :], *f)
            banks2.own = []

        zt = FA[:, 14000:14000 + D]
        t_zero = pool(lambda e: e.memset(zt, 0.0))
        t_gx = Chan("s_gz")(GX.rearrange("(b p) d -> p b d", p=P), zt.unsqueeze(1).broadcast_to([P, NB, D]), t_zero, t_w2q)
        t = ffn0(t_x)
        for ln in lines:
            ln.wait(t_gx)
        lend()
        t = attention(t)
        unlend()
        early.close()
        NRA, NFA = 10240, 17088
        WE = sb("WE", [P, NE * 768], F)
        RA = sb("RB", [P, NRA], R)
        FA = sb("FB", [P, NFA], F)
        wst = stage_of()
        t_we = [Chan(f"s_we{i}")(WE[:, i * 3072:i * 3072 + 3072], d["wr"][:, i * 3072:i * 3072 + 3072], everyone())
                for i in range(4)]
        t = ffn0(t)
        t = experts(t)
        t = mamba(t)
        t = experts(t)
        co = Chan("s_out")
        for h in range(4):
            t_o = co(d["out"][:, 2 * h:2 * h + 2, :], X[:, 2 * h:2 * h + 2, :], t[2 * h], t[2 * h + 1])
        sp.wait(t_o)


def layout(i):
    f = np.float32
    x = np.asarray(i["L0_attn_x"])[0]

    def kt(w, k):
        return np.ascontiguousarray(w.reshape(k, P, -1).transpose(1, 0, 2))

    perm = np.array([h * 16 + c for h in range(NH) for c in list(range(0, 16, 2)) + list(range(1, 16, 2))])
    g = {n: np.asarray(i[n]) for n in i}
    wqkv = np.concatenate([g["L0_attn_Wq"][perm].T, g["L0_attn_Wk"][perm].T, g["L0_attn_Wv"].T], axis=1)
    bqkv = np.concatenate([g["L0_attn_bq"][perm], g["L0_attn_bk"][perm], g["L0_attn_bv"]])
    half = 8
    inv = (f(1.0) / np.power(f(10000.0), np.arange(half, dtype=f) / f(half))).astype(f)
    ang = (np.arange(S, dtype=f)[:, None] * inv[None, :]).astype(f)
    cos, sin = np.cos(ang).astype(f), np.sin(ang).astype(f)
    CC = np.concatenate([cos, cos], axis=1).reshape(NT, P, 16).transpose(1, 0, 2).reshape(P, NT * 16)
    SS = np.concatenate([-sin, sin], axis=1).reshape(NT, P, 16).transpose(1, 0, 2).reshape(P, NT * 16)
    hot = np.zeros((P, 32), f)
    for n in range(32):
        hot[n, n] = 1
        hot[32 + n, n] = 1

    def rows(v):
        return np.broadcast_to(np.asarray(v)[None, :], (P, len(v)))

    def cols(v, k):
        return np.asarray(v).reshape(k, P, -1).transpose(1, 0, 2).reshape(P, -1)

    a = np.arange(P)
    neg = f(-1e30)
    mS = np.where(a[None, :] > a[:, None], neg, f(0))
    mT = np.where(a[:, None] > a[None, :], neg, f(0))

    parts = {
        "ident": np.eye(P, dtype=f), "CC": CC, "SS": SS, "iota": rows(np.arange(32, dtype=f)),
        "b2": rows(g["L0_ffn_b2"]), "bqkv": rows(bqkv), "bo": rows(g["L0_attn_bo"]),
        "b1": cols(g["L0_ffn_b1"], 8), "cw": cols(g["L1_attn_conv1d_weight"], 4),
        "dtb": cols(g["L1_attn_dt_proj_bias"], 4), "Alog": cols(g["L1_attn_A_log"], 4),
        "Dp": cols(g["L1_attn_D"], 4), "gb": rows(g["L1_ffn_gate_bias"]), "hot": hot,
    }
    cst = np.concatenate([parts[n] for n in CONST], axis=1)
    xpw = g["L1_attn_x_proj_weight"].T
    xp = np.concatenate([xpw[:, 0:P], xpw[:, P:], xpw[:, P:]], axis=1)
    wgs, wus, wds = g["L1_ffn_wg_s"], g["L1_ffn_wu_s"], g["L1_ffn_wd_s"]
    we = []
    for s in range(2):
        we.append((wgs[:, s * P:s * P + P], wus[:, s * P:s * P + P], wds[s * P:s * P + P]))
    for e in range(NE):
        we.append((g["L1_ffn_wg"][e], g["L1_ffn_wu"][e], g["L1_ffn_wd"][e]))
    we = np.stack([np.concatenate([a_[0:P], b_[0:P], a_[P:], b_[P:], c_], axis=1) for a_, b_, c_ in we])
    return {
        "x": np.ascontiguousarray(x.reshape(NT, P, D).transpose(1, 0, 2)),
        "cst": np.ascontiguousarray(cst.astype(f)),
        "b16": np.concatenate([np.eye(P, dtype=f), mS, mT, np.triu(np.ones((P, P), f), 1), np.ones((P, P), f)], axis=1).astype(f),
        "w1": kt(g["L0_ffn_w1"].T, 2).reshape(P, 2048), "w2": kt(g["L0_ffn_w2"].T, 8).reshape(P, 2048),
        "qkv": kt(wqkv, 2).reshape(P, 1536), "o": kt(g["L0_attn_Wo"].T, 2).reshape(P, 512),
        "in": kt(g["L1_attn_in_proj_weight"].T, 2).reshape(P, 2048), "xp": kt(xp, 4).reshape(P, 768),
        "dt": np.ascontiguousarray(g["L1_attn_dt_proj_weight"].T), "outw": kt(g["L1_attn_out_proj_weight"].T, 4).reshape(P, 1024),
        "cen": kt(g["L1_ffn_centroids"].T, 2).reshape(P, 32), "we": np.ascontiguousarray(we[0:2]), "wr": np.ascontiguousarray(we[2:].transpose(1, 0, 2).reshape(P, NE * 768)),
    }


def kernel(**inputs):
    import concourse.bacc as bacc
    from concourse.bass_utils import run_bass_kernel_spmd as run

    arrays = {f"in_{k}": v for k, v in layout(inputs).items()}
    nc = bacc.Bacc("TRN2", target_bir_lowering=False, num_devices=1)
    d = {}
    for k, v in arrays.items():
        d[k[3:]] = nc.dram_tensor(k, v.shape, mybir.dt.from_np(v.dtype), kind="ExternalInput").ap()
    d["out"] = nc.dram_tensor("out", (P, NT, D), F, kind="ExternalOutput").ap()
    build(nc, d)
    r = run(nc, [arrays], core_ids=[0])
    o = r.results[0]["out"]
    return np.ascontiguousarray(o.transpose(1, 0, 2)).reshape(1, S, D)
```

```python
from contextlib import ExitStack

import numpy as np
import concourse.bass as bass
from concourse import mybir

F = mybir.dt.float32
R = mybir.dt.float32r
BF = mybir.dt.bfloat16
U32 = mybir.dt.uint32
ALU = mybir.AluOpType
ACT = mybir.ActivationFunctionType
AX = mybir.AxisListType.X

P = 128
S = 1024
D = 256
NT = S // P
CH = 512
NCH = S // CH
TC = CH // P
FF = 1024
NH = 16
DI = 512
DN = 16
NE = 16
EPS = 1e-5
NB = (2 * S + NE * (P - 1)) // P
WB = 4

CONST = {}
_at = 0
for _name, _n in (("ident", 128), ("CC", 128), ("SS", 128), ("iota", 32), ("b2", 256), ("bqkv", 768), ("bo", 256),
                  ("b1", 8), ("cw", 16), ("dtb", 4), ("Alog", 64), ("Dp", 4), ("gb", 16), ("hot", 32)):
    CONST[_name] = (_at, _n)
    _at += _n
NCONST = _at


class Line:

    def __init__(self, engine, sem):
        self.e, self.sem, self.n, self.waited = engine, sem, 0, {}

    def wait(self, *tokens):
        for t in tokens:
            if t is None:
                continue
            if isinstance(t, list):
                self.wait(*t)
                continue
            key, sem, v = t
            if self.waited.get(key, 0) < v:
                self.waited[key] = v
                self.e.wait_ge(sem, v)

    def __call__(self, fn, *tokens, inc=True):
        self.wait(*tokens)
        if not inc:
            fn(self.e)
            return None
        self.n += 1
        fn(self.e).then_inc(self.sem, 1)
        return (self.sem.name, self.sem, self.n)

    @property
    def last(self):
        return (self.sem.name, self.sem, self.n) if self.n else None


class Slots:

    def __init__(self, items):
        self.free = [(i, []) for i in items]

    def get(self):
        return self.free.pop(0)

    def put(self, item, *tokens):
        self.free.append((item, list(tokens)))


class Area:

    def __init__(self, t, n):
        self.t, self.n, self.at = t, n, 0

    def take(self, n):
        a = self.at
        self.at += n
        assert self.at <= self.n, (self.at, self.n)
        return self.t[:, a:a + n]


def build(nc, d):
    ctx = ExitStack()
    with ctx:
        def sb(name, shape, dt):
            return ctx.enter_context(nc.sbuf_tensor(name, shape, dt))

        nsem = [0]

        def sem(name):
            nsem[0] += 1
            return ctx.enter_context(nc.semaphore(name))

        PS = ctx.enter_context(nc.psum_tensor("PS", [P, 8, 512], F))
        X = sb("X", [P, NT, D], F)
        C = sb("C", [P, NCONST], F)
        BC16 = sb("BC16", [P, 3 * P], BF)
        W1Q = sb("W1Q", [P, 2, FF], R)
        W2Q = sb("W2Q", [P, 8, D], R)
        XN = sb("XN", [P, 2, 2, NCH, CH], R)
        HOT = sb("HOT", [P, 32], R)
        TRI = sb("TRI", [P, 2 * P], BF)
        SM = sb("SM", [P, 320], F)
        early = ExitStack()
        NRA, NFA = 22528, 17792
        RA = early.enter_context(nc.sbuf_tensor("RA", [P, NRA], R))
        FA = early.enter_context(nc.sbuf_tensor("FA", [P, NFA], F))
        GX = nc.dram_tensor("GX", [NB * P, D], F, kind="Internal").ap()
        GY = nc.dram_tensor("GY", [NB * P, D], F, kind="Internal").ap()

        pe = Line(nc.tensor, sem("s_pe"))
        act = Line(nc.scalar, sem("s_act"))
        dve = Line(nc.vector, sem("s_dve"))
        pool = Line(nc.gpsimd, sem("s_pool"))
        sp = Line(nc.sync, sem("s_sp"))
        lines = (pe, act, dve, pool)

        def cst(name):
            a, n = CONST[name]
            return C[:, a:a + n]

        ident = cst("ident")
        identb, maskS, maskT = (BC16[:, i * P:(i + 1) * P] for i in range(3))

        class Chan:

            def __init__(self, name):
                self.sem, self.n = sem(name), 0

            def __call__(self, out, in_, *tokens):
                sp.wait(*tokens)
                self.n += 16
                nc.sync.dma_start(out, in_).then_inc(self.sem, 16)
                return (self.sem.name, self.sem, self.n)

        def everyone():
            return [x.last for x in lines]

        banks = Slots([PS[:, i, :] for i in range(8)])

        def mm(out, lhsT, rhs, start, stop, *tokens, inc=False, skip=False):
            return pe(lambda e: e.matmul(out, lhsT, rhs, start=start, stop=stop, skip_group_check=skip),
                      *tokens, inc=inc)

        def group(out, pairs, *tokens, start=True, stop=True, skip=False):
            t = None
            for i, (a, b) in enumerate(pairs):
                t = mm(out, a, b, start and i == 0, stop and i == len(pairs) - 1,
                       *(tokens if i == 0 else ()), inc=i == len(pairs) - 1, skip=skip)
            return t

        def three(a, b):
            return [(a[0], b[0]), (a[1], b[0]), (a[0], b[1])]

        def tr(out, in_, *tokens, inc=True):
            return pe(lambda e: e.matmul(out, in_, ident, start=True, stop=True, is_transpose=True),
                      *tokens, inc=inc)

        def split(hi, lo, src, *tokens, on=None):
            on = on or act
            if on is act:
                t1 = act(lambda e: e.activation(hi, src, ACT.Copy), *tokens)
            else:
                t1 = on(lambda e: e.tensor_copy(hi, src), *tokens)
            t2 = dve(lambda e: e.tensor_tensor(lo, src, hi.bitcast(F), ALU.subtract), t1, *tokens)
            return [t1, t2]

        t_x = [None] * NT

        def load_x(h):
            t = Chan(f"s_x{h}")(X[:, h * 4:h * 4 + 4, :], d["x"][:, h * 4:h * 4 + 4, :])
            t_x[4 * h:4 * h + 4] = [t] * 4

        b16 = FA[:, NFA - 640:NFA]
        t_w = [Chan("s_w1")(FA[:, 0:2048], d["w1"])]
        load_x(0)
        t_c = Chan("s_c")(C[:, :], d["cst"])
        t_w.append(Chan("s_w2")(FA[:, 4096:6144], d["w2"]))
        load_x(1)
        t_b16 = Chan("s_b16")(b16, d["b16"])

        def quantize():
            for i, Q in enumerate((W1Q, W2Q)):
                w, tmp = FA[:, 4096 * i:4096 * i + 2048], FA[:, 4096 * i + 2048:4096 * i + 4096]
                Qf = Q[:, :, :].rearrange("p a b -> p (a b)")
                s = SM[:, i * 4:i * 4 + 4]
                t = act(lambda e: e.activation(tmp, w, ACT.Abs, accum_out=s[:, 0:1]), t_w[i])
                bk, fr = banks.get()
                t = mm(bk[:, 0:1], ones1, s[:, 0:1], True, True, t, t_ones, *fr, inc=True)
                t = dve(lambda e: e.tensor_scalar(s[:, 1:2], bk[:, 0:1], 1.0 / (FF * D), 0.7, ALU.mult, ALU.mult), t)
                banks.put(bk, t)
                t = dve(lambda e: e.tensor_scalar(s[:, 2:3], s[:, 1:2], -1.0, None, ALU.mult), t)
                t = dve(lambda e: e.tensor_scalar(tmp, w, s[:, 2:3], None, ALU.is_le), t)
                t = dve(lambda e: e.scalar_tensor_tensor(Qf, w, s[:, 1:2], tmp, ALU.is_ge, ALU.subtract), t)
                yield t

        ones1 = FA[:, 8192:8320]
        t_ones = pool(lambda e: e.memset(ones1, 1.0))
        b2h = SM[:, 8:8 + 256]
        quantized = quantize()
        t_w1q = next(quantized)
        t_b2h = pool(lambda e: e.tensor_scalar(b2h, cst("b2"), 0.5, None, ALU.mult), t_c)
        eps = SM[:, 300:304]
        mhalf = SM[:, 304:308]
        t_eps = pool(lambda e: e.memset(mhalf, -0.5))

        class Norm:

            def __init__(self, ch, tmps, st, t_in, t_xnfree=None):
                self.ch, self.tmps, self.st, self.t_in, self.t_xnfree = ch, tmps, st, t_in, t_xnfree
                self.pair = self.single = False
                self.gen = self.steps()
                self.done = False

            def step(self):
                if not self.done:
                    self.done = next(self.gen, self) is self

            def finish(self, pair=False):
                self.pair = pair
                while not self.done:
                    self.step()
                return self.xn, self.n

            def steps(self):
                ch, tmps, st, t_in = self.ch, self.tmps, self.st, self.t_in
                tk = []
                for i in range(TC):
                    t = ch * TC + i
                    a = dve(lambda e: e.bn_stats(st[:, i * 6:i * 6 + 6], X[:, t, :]), t_in[t])
                    tk.append(dve(lambda e: e.bn_aggr(st[:, 24 + 2 * i:26 + 2 * i], st[:, i * 6:i * 6 + 6]), a))
                    if i % 2:
                        yield
                mv = st[:, 24:32].rearrange("p (t c) -> p t c", c=2)
                rs = st[:, 32:36]
                a = pool(lambda e: e.tensor_scalar(rs, mv[:, :, 1], EPS, None, ALU.add), tk)
                a = pool(lambda e: e.tensor_tensor(rs, rs, mhalf, ALU.pow), a, t_eps)
                yield
                got = []
                for i in range(TC):
                    t = ch * TC + i
                    tmp, fr = tmps.get()
                    n = dve(lambda e: e.tensor_scalar(tmp, X[:, t, :], st[:, 24 + 2 * i:25 + 2 * i], rs[:, i:i + 1],
                                                      ALU.subtract, ALU.mult), a, *fr)
                    got.append((tmp, n))
                    if i == 1:
                        yield
                self.n = n
                yield
                if self.single:
                    yield
                    self.xn = []
                    for k in range(2):
                        bk, fr = banks.get()
                        for i, (tmp, n) in enumerate(got):
                            p = tr(bk[:, i * P:i * P + P], tmp[:, k * P:k * P + P], n, t_c, *fr, inc=i == TC - 1)
                        yield
                        tt = split(XN[:, 0, k, ch, :], XN[:, 1, k, ch, :], bk, p, self.t_xnfree)
                        banks.put(bk, *tt)
                        self.xn += tt
                        yield
                    return
                if self.pair:
                    bp, f0 = banks2.get()
                    b0, b1, f1 = bp[:, 0, :], bp[:, 1, :], []
                else:
                    b0, f0 = banks.get()
                    b1, f1 = banks.get()
                for i, (tmp, n) in enumerate(got):
                    tr(b0[:, i * P:i * P + P], tmp[:, 0:P], n, t_c, *f0, inc=False)
                    p = tr(b1[:, i * P:i * P + P], tmp[:, P:2 * P], *f1)
                    tmps.put(tmp, p)
                yield
                self.xn = []
                for k, b in ((0, b0), (1, b1)):
                    tt = split(XN[:, 0, k, ch, :], XN[:, 1, k, ch, :], b, p, self.t_xnfree)
                    if not self.pair:
                        banks.put(b, *tt)
                    self.xn += tt
                    if k == 0:
                        yield
                if self.pair:
                    banks2.put(bp, *self.xn)

        def xn(k, ch, a=0, b=CH):
            return (XN[:, 0, k, ch, a:b], XN[:, 1, k, ch, a:b])

        first = Area(FA[:, 8320:], 2200)
        first_tmps = Slots([first.take(D) for _ in range(TC)])
        norms0 = [Norm(ch, first_tmps, first.take(40), t_x) for ch in range(NCH)]
        norms0[0].finish()
        t_w2q = next(quantized)
        t_hot = dve(lambda e: e.tensor_copy(HOT[:, :], cst("hot")), t_c)
        t_tri = dve(lambda e: e.tensor_copy(TRI[:, :], b16[:, 384:640]), t_b16)
        t_c16 = dve(lambda e: e.tensor_copy(BC16[:, :], b16[:, 0:384]), t_b16)

        def ffn0(norms, meanwhile, ahead, at):
            ra, fa = Area(RA[:, NRA - 8192:], 8192), Area(FA[:, at:], NFA - at)
            H = [ra.take(8 * CH).rearrange("p (f n) -> p f n", f=8) for _ in range(2)]
            t_hfree = [None] * 8
            hs = Slots([fa.take(CH) for _ in range(4)])
            tmps = Slots([fa.take(D) for _ in range(4)])
            sts = [fa.take(40) for _ in range(2 * NCH)]
            t_out = [None] * NT
            nexts = []
            for ch in range(NCH):
                t_xn, t_n = norms[ch].finish()
                Hh, Hl = H
                xa = X[:, ch * TC:ch * TC + TC, :]
                t_b = pool(lambda e: e.tensor_tensor(xa, xa, b2h.unsqueeze(1).broadcast_to([P, TC, D]), ALU.add),
                           t_n, t_b2h)
                accs = [banks.get() for _ in range(TC)]
                t_h = []

                def down(f):
                    for i in range(TC):
                        acc, fr = accs[i]
                        t = group(acc[:, 0:D], [(Hh[:, f, i * P:i * P + P], W2Q[:, f, :]),
                                                (Hl[:, f, i * P:i * P + P], W2Q[:, f, :])],
                                  t_h[f], t_w2q, *(fr if f == 0 else ()), start=f == 0, stop=f == 7)
                        if f == 7:
                            accs[i] = (acc, t)
                    t_hfree[f] = t

                for f in range(8):
                    bk, fr = banks.get()
                    ps = [(W1Q[:, k, f * P:f * P + P], x) for k in range(2) for x in xn(k, ch)]
                    t = group(bk, ps, t_xn, t_w1q, *fr)
                    h, fh = hs.get()
                    b1 = cst("b1")[:, f:f + 1]
                    t = act(lambda e: e.activation(h, bk, ACT.Gelu, bias=b1), t, *fh)
                    banks.put(bk, t)
                    tt = split(Hh[:, f, :], Hl[:, f, :], h, t, t_hfree[f], on=dve)
                    hs.put(h, *tt)
                    t_h.append(tt)
                    (norms[1] if ch == 0 else nexts[0]).step()
                    if ch and meanwhile:
                        next(meanwhile, None)
                    if f > 1:
                        down(f - 2)
                down(6)
                down(7)
                for i in range(TC):
                    acc, t = accs[i]
                    xt = X[:, ch * TC + i, :]
                    t = dve(lambda e: e.scalar_tensor_tensor(xt, acc[:, 0:D], 0.5, xt, ALU.mult, ALU.add), t, t_b)
                    banks.put(acc, t)
                    t_out[ch * TC + i] = t
                nexts.append(Norm(ch, ahead[ch] if ahead else tmps, sts[2 + ch], t_out, pe.last))
            for _ in meanwhile or ():
                pass
            return nexts

        def chain(*gens):
            for g_ in gens:
                yield from g_

        def weave(*gens):
            live_ = [[g_, n_, 0.0] for g_, n_ in gens]
            while live_:
                for x in list(live_):
                    x[2] += x[1]
                    while x[2] >= 1:
                        x[2] -= 1
                        if next(x[0], live_) is live_:
                            live_.remove(x)
                            break

        def stage_of():
            return [FA[:, NFA - 3072:NFA - 1536], FA[:, NFA - 1536:NFA]]

        wst = stage_of()
        ch_w = [Chan("s_wst0"), Chan("s_wst1")]

        Wq = [RA[:, i * 1536:i * 1536 + 1536].rearrange("p (k n) -> p k n", k=2) for i in range(2)]
        Wo = [RA[:, 3072 + i * 512:3584 + i * 512].rearrange("p (k n) -> p k n", k=2) for i in range(2)]
        QT = RA[:, 4096:8192].rearrange("p (j n) -> p j n", j=8)
        V = FA[:, 0:4096].rearrange("p (t n) -> p t n", t=8)
        t_att = {}

        def attention_weights():
            t = ch_w[0](wst[0], d["qkv"], t_tri, t_c16)
            u = ch_w[1](wst[1][:, 0:512], d["o"], t_tri, t_c16)
            yield
            t_att["q"] = split(Wq[0].rearrange("p k n -> p (k n)"), Wq[1].rearrange("p k n -> p (k n)"), wst[0], t, on=dve)
            yield
            t_att["zq"] = pool(lambda e: e.memset(QT.bitcast(F), 0.0))
            vv = V.rearrange("p t (h c) -> p (t h) c", c=32)
            t_att["v"] = [pool(lambda e: e.memset(vv[:, :, 16:17], 1.0), t_w1q, t_w2q),
                          pool(lambda e: e.memset(vv[:, :, 17:32], 0.0), t_w1q, t_w2q)]
            t_att["o"] = split(Wo[0].rearrange("p k n -> p (k n)"), Wo[1].rearrange("p k n -> p (k n)"), wst[1][:, 0:512], u, on=dve)

        def attention(norms):
            bar = everyone()
            for ln in lines:
                ln.wait(bar)
            ra, fa = Area(RA[:, 4096:], NRA - 4096), Area(FA, NFA - 3072)
            ra.take(8 * CH)
            KT = ra.take(8 * S).rearrange("p (j n) -> p j n", j=8)
            Qall = ra.take(TC * 1024)
            kk = ra.take(2048)
            Ks = Slots([kk[:, 0:1024], kk[:, 1024:2048]])
            fa.take(8 * 512)
            PT = Slots([fa.take(CH) for _ in range(16)])
            LAG = 2
            sets = Slots([])
            set0 = (fa.take(512), fa.take(512), fa.take(512))
            raw = fa.take(512)
            sts_ = [fa.take(40) for _ in range(NCH)]
            rc = fa.take(16)
            M = fa.take(16)
            Mn = fa.take(16)
            att = wst[0][:, 0:1024].rearrange("p (t n) -> p t n", t=TC)
            w1_ = wst[1]
            set1 = (w1_[:, 0:512], w1_[:, 512:1024], w1_[:, 1024:1536])
            t_wq, t_wo = t_att["q"], t_att["o"]
            t_wst = [t_wq[1], t_wo[1]]
            sets.free = [(set0, []), (set1, list(t_wst))]
            t_attfree = list(t_wst)
            pads = []
            Qv = Qall.bitcast(F).rearrange("p (t h c) -> p (t h) c", t=TC, c=64)
            pads.append(pool(lambda e: e.memset(Qv[:, :, 32:48], 0.0)))
            kv = kk.bitcast(F).rearrange("p (t h c) -> p (t h) c", t=2, c=64)
            pads.append(pool(lambda e: e.memset(kv[:, :, 32:34], -1.0)))
            pads.append(pool(lambda e: e.memset(kv[:, :, 34:48], 0.0)))
            zq = t_att["zq"]
            pads += t_att["v"]
            t_out = [None] * NT
            Q4 = Qall.rearrange("p (t h c) -> p t h c", t=TC, c=64)
            shared = {"fin": [], "raw": None, "kt": [], "qfree": None, "att": t_attfree, "qt": [zq, zq]}

            def keys(t, i, ks, tg):
                bk, fr = banks2.get()
                for jj in range(8):
                    p = tr(bk[:, jj // 4, (jj % 4) * P:(jj % 4) * P + P], ks[:, jj * P:jj * P + P].bitcast(F),
                           tg, *fr, inc=jj == 7)
                Ks.put(ks, p)
                dst = KT[:, :, t * P:t * P + P]
                src = bk.rearrange("p b (j n) -> p (b j) n", n=P)
                if i % 2:
                    tk = act(lambda e: e.activation(dst, src, ACT.Copy), p)
                else:
                    tk = dve(lambda e: e.tensor_copy(dst, src), p)
                banks2.put(bk, tk)
                shared["kt"].append(tk)

            def project(ch):
                if ch:
                    qkv0, f0_ = sets.get()
                    tmps = Slots([])
                    tmps.free = [(qkv0[b_][:, c_:c_ + 256], list(f0_)) for b_ in (1, 2) for c_ in (0, 256)]
                    norms[1].tmps = tmps
                    norms[1].st = sts_[1]
                t_xn, t_n = norms[ch].finish(pair=True)
                if ch:
                    sets.put(qkv0, *[f for _, f in tmps.free])
                xa = X[:, ch * TC:ch * TC + TC, :]
                bo = cst("bo").unsqueeze(1).broadcast_to([P, TC, D])
                t_b = pool(lambda e: e.tensor_tensor(xa, xa, bo, ALU.add), t_n, t_c)
                if ch:
                    z_ = pool(lambda e: e.memset(Qv[:, :, 32:34], 0.0), shared["qfree"])
                else:
                    z_ = pads
                t_q, late = [], []
                yield
                for i in range(TC):
                    t = ch * TC + i
                    A = [xn(k, ch, i * P, i * P + P) for k in range(2)]
                    bk, fr = banks2.get()
                    m0 = group(bk[:, 0, :], [p for k in range(2) for p in three(A[k], [w[:, k, 0:512] for w in Wq])],
                               t_xn, t_wq, *fr)
                    m1 = group(bk[:, 1, 0:256], [p for k in range(2) for p in three(A[k], [w[:, k, 512:768] for w in Wq])])
                    yield
                    st, fs = sets.get()
                    qk, t1b, t2b = st
                    bq = cst("bqkv")[:, 0:512]
                    bv = cst("bqkv")[:, 512:768].rearrange("p (h c) -> p h c", c=16)
                    r1 = dve(lambda e: e.tensor_tensor(qk, bk[:, 0, :], bq, ALU.add), m0, *fs)
                    vt = V[:, t, :].rearrange("p (h c) -> p h c", c=32)[:, :, 0:16]
                    r2 = dve(lambda e: e.tensor_tensor(vt, bk[:, 1, 0:256].rearrange("p (h c) -> p h c", c=16), bv, ALU.add),
                             m1, pads)
                    banks2.put(bk, r1, r2)
                    cs = cst("CC")[:, t * 16:t * 16 + 16].unsqueeze(1).broadcast_to([P, 32, 16])
                    q3 = qk.rearrange("p (h c) -> p h c", c=16)
                    o3 = t1b.rearrange("p (h c) -> p h c", c=16)
                    w3 = t2b.rearrange("p (h c) -> p h c", c=16)
                    se = cst("SS")[:, t * 16:t * 16 + 8].unsqueeze(1).broadcast_to([P, 32, 8])
                    so = cst("SS")[:, t * 16 + 8:t * 16 + 16].unsqueeze(1).broadcast_to([P, 32, 8])
                    a = pool(lambda e: e.tensor_tensor(o3, q3, cs, ALU.mult), r1, *fs)
                    b = dve(lambda e: e.tensor_tensor(w3[:, :, 0:8], q3[:, :, 8:16], se, ALU.mult), r1)
                    c = dve(lambda e: e.tensor_tensor(w3[:, :, 8:16], q3[:, :, 0:8], so, ALU.mult))
                    yield
                    r = dve(lambda e: e.tensor_tensor(qk, t1b, t2b, ALU.add), a, b, c)
                    rq = qk[:, 0:256].rearrange("p (h c) -> p h c", c=16)
                    rk = qk[:, 256:512].rearrange("p (h c) -> p h c", c=16)
                    Q3 = Q4[:, i, :, :]
                    ks, fk = Ks.get()
                    K3 = ks.rearrange("p (h c) -> p h c", c=64)
                    g1 = act(lambda e: e.activation(K3[:, :, 0:16], rk, ACT.Copy), r, pads, *fk)
                    e1 = act(lambda e: e.activation(Q3[:, :, 0:16], rq, ACT.Copy), z_, shared["qfree"])
                    g2 = act(lambda e: e.activation(K3[:, :, 16:32], rk, ACT.Copy))
                    e2 = act(lambda e: e.activation(Q3[:, :, 48:64], rq, ACT.Copy))
                    g3 = dve(lambda e: e.tensor_tensor(K3[:, :, 48:64], rk, K3[:, :, 0:16].bitcast(F), ALU.subtract), g1)
                    e3 = dve(lambda e: e.tensor_tensor(Q3[:, :, 16:32], rq, Q3[:, :, 0:16].bitcast(F), ALU.subtract), e1)
                    sets.put(st, e3, e2, g3, g2)
                    t_q.append([e1, e2, e3])
                    yield
                    late.append((t, i, ks, [g1, g2, g3]))
                    if i:
                        keys(*late.pop(0))
                        yield
                keys(*late.pop(0))
                shared["q", ch] = [t_q, z_]
                shared["b", ch] = t_b

            def turn(ch, g, toks, free):
                bk, fr = banks2.get()
                for b in range(2):
                    j = 2 * g + b
                    for i in range(TC):
                        p = tr(bk[:, b, i * P:i * P + P], Qall[:, i * 1024 + j * P:i * 1024 + j * P + P].bitcast(F),
                               toks, *fr, inc=b == 1 and i == TC - 1)
                q4 = QT[:, 4 * (g % 2):4 * (g % 2) + 4, :].rearrange("p (h b) n -> p h b n", b=2)
                tk = [dve(lambda e: e.tensor_copy(q4[0:64, :, 0, :], bk[0:64]), p, free),
                      act(lambda e: e.activation(q4[64:128, :, 1, :], bk[64:128], ACT.Copy), p, free)]
                banks2.put(bk, *tk)
                return tk, p

            def maxima(ch, g):
                tq, _ = turn(ch, g, shared["q", ch], shared["qt"][g % 2])
                for _ in range(2):
                    yield
                M3 = M.rearrange("p (t h) -> p t h", t=TC)
                N3 = Mn.rearrange("p (t h) -> p t h", t=TC)
                kt_ = list(shared["kt"])
                t_m = shared.get("m")
                rs_ = []
                if ch == 0:
                    rs_.append(dve(lambda e: e.memset(N3[:, 0, :], -3.4e38), t_m))

                def score(out, i, hh, c0, c1, start, stop, *toks, inc=False):
                    return mm(out, QT[:, 4 * (g % 2) + hh, i * P:i * P + P], KT[:, 2 * g + hh // 2, c0:c1], start, stop,
                              *toks, inc=inc)

                for i in range(TC):
                    w = (ch * TC + i) * P
                    if i % 2 == 0:
                        bk, fr = banks2.get()
                        for u in range(2):
                            m = mm(bk[:, u, :], identb, maskS.unsqueeze(1).broadcast_to([P, 4, P]), True, False, t_c16, tq, kt_, *fr)
                            for s_ in range(4):
                                d0 = w + s_ // 2 * P
                                m = score(bk[:, u, s_ * P:s_ * P + P], i + s_ // 2, 2 * (s_ % 2) + u, d0, d0 + P, False, s_ == 3,
                                          inc=s_ == 3)
                        bv_ = bk.rearrange("p b (s n) -> p b s n", n=P)
                        mo_ = M[:, i * 4:i * 4 + 8].rearrange("p (s b) -> p b s", b=2)
                        r = dve(lambda e: e.reduce_max(mo_, bv_, AX), m, t_m)
                        banks2.put(bk, r)
                        rs_.append(r)
                        yield
                    if not w:
                        continue
                    hpb = 2 if w <= 256 else 1
                    per = 2 * hpb if w <= 512 else 1
                    for h0 in range(0, 4, per):
                        bk, fr = banks2.get()
                        if per == 1:
                            flat = bk.rearrange("p b n -> p (b n)")
                            score(flat[:, 0:512], i, h0, 0, 512, True, True, tq, kt_, *fr)
                            m = score(flat[:, 512:w], i, h0, 512, w, True, True, inc=True)
                            r = dve(lambda e: e.reduce_max(N3[:, i, h0:h0 + 1], flat[:, 0:w], AX), m, t_m)
                        else:
                            for u in range(per):
                                m = score(bk[:, u % 2, (u // 2) * w:(u // 2) * w + w], i, h0 + u, 0, w, True, True, tq, kt_,
                                          *fr, inc=u == per - 1)
                            src = bk[:, :, 0:hpb * w].rearrange("p b (h n) -> p b h n", h=hpb)
                            dst = N3[:, i, h0:h0 + per].rearrange("p (h b) -> p b h", b=2)
                            r = dve(lambda e: e.reduce_max(dst, src, AX), m, t_m)
                        banks2.put(bk, r)
                        rs_.append(r)
                        yield
                r = dve(lambda e: e.tensor_tensor(M, M, Mn, ALU.max), rs_)
                a = dve(lambda e: e.tensor_copy(Q4[:, :, 4 * g:4 * g + 4, 32], M3), r)
                b = dve(lambda e: e.tensor_tensor(Q4[:, :, 4 * g:4 * g + 4, 33], M3, Q4[:, :, 4 * g:4 * g + 4, 32].bitcast(F),
                                                  ALU.subtract), a)
                shared["m"] = b
                for _ in range(2):
                    yield
                shared["q2", g], shared["qfree"] = turn(ch, g, [a, b], m)

            def heads(ch, g):
                nk = ch * TC + TC
                pend = []
                acc = None
                tq2 = shared["q2", g]

                def pv(kt, slots):
                    c0 = max(0, (kt - ch * TC) * P)
                    for hh in range(4):
                        pt, te = slots[hh]
                        t = mm(acc[0][32 * hh:32 * hh + 32, c0:CH], V[:, kt, (4 * g + hh) * 32:(4 * g + hh) * 32 + 32],
                               pt[:, c0:CH], kt == 0, kt == nk - 1, te, *acc[1], inc=hh == 3)
                    for pt, te in slots:
                        PT.put(pt, t)
                    return t

                for kt in range(nk + LAG):
                    if kt < nk:
                        slots = []
                        c0 = max(0, (kt - ch * TC) * P)
                        for hh in range(4):
                            bk, fr = banksT.get()
                            pt, fp = PT.get()
                            t = mm(bk[:, c0:CH], KT[:, 2 * g + hh // 2, kt * P:kt * P + P], QT[:, 4 * (g % 2) + hh, c0:CH],
                                   True, True, tq2, *fr, inc=True)
                            te = act(lambda e: e.activation(pt[:, c0:], bk[:, c0:], ACT.Exp, scale=0.25), t, *fp)
                            banksT.put(bk, te)
                            if kt >= ch * TC:
                                dd = pt[:, c0:c0 + P]
                                te = pool(lambda e: e.affine_select(out=dd, in_=dd, compare_op=ALU.is_ge, fill=0.0, base=0,
                                                                    pattern=[[1, P]], channel_multiplier=-1), te)
                            slots.append((pt, te))
                            yield
                        pend.append((kt, slots))
                    if kt >= LAG:
                        if kt == LAG:
                            acc = banks.get()
                        t = pv(*pend.pop(0))
                        yield
                        if kt == LAG and shared["fin"]:
                            finish(*shared["fin"].pop(0))
                shared["qt"][g % 2] = t
                t = dve(lambda e: e.tensor_copy(raw, acc[0]), t, shared["raw"])
                banks.put(acc[0], t)
                shared["fin"].append((g, t))
                yield

            def finish(g, t):
                bk, fr = banksT.get()
                for i in range(TC):
                    p = tr(bk[:, i * P:i * P + P], raw[:, i * P:i * P + P], t, *fr, inc=i == TC - 1)
                shared["raw"] = p
                b4 = bk.rearrange("p (t h c) -> p t h c", h=4, c=32)
                r3 = rc.rearrange("p (t h) -> p t h", h=4)
                a = dve(lambda e: e.reciprocal(r3, b4[:, :, :, 16]), p, shared.get("rc"))
                o4 = att[:, :, g * 64:g * 64 + 64].rearrange("p t (h c) -> p t h c", c=16)
                a = dve(lambda e: e.tensor_tensor(o4, b4[:, :, :, 0:16], r3.unsqueeze(3).broadcast_to([P, TC, 4, 16]),
                                                  ALU.mult), a, shared["att"])
                shared["rc"] = a
                banksT.put(bk, a)

            def output(ch):
                while shared["fin"]:
                    finish(*shared["fin"].pop(0))
                yield
                bk, fr = banks2.get()
                for i in range(TC):
                    for k in range(2):
                        p = tr(bk[:, k, i * P:i * P + P], att[:, i, k * P:k * P + P], shared["rc"], *fr,
                               inc=i == TC - 1 and k == 1)
                shared["att"] = p
                AT = [XN[:, s_, :, ch, :] for s_ in range(2)]
                tt = split(AT[0], AT[1], bk, p)
                banks2.put(bk, *tt)
                yield
                for i in range(TC):
                    bk, fr = banksT.get()
                    A = [[a[:, k, i * P:i * P + P] for a in AT] for k in range(2)]
                    m = group(bk[:, 0:D], [q for k in range(2) for q in three(A[k], [w[:, k, :] for w in Wo])],
                              tt, t_wo, *fr)
                    xt = X[:, ch * TC + i, :]
                    t = dve(lambda e: e.tensor_tensor(xt, bk[:, 0:D], xt, ALU.add), m, shared["b", ch])
                    banksT.put(bk, t)
                    t_out[ch * TC + i] = t
                    yield

            weave((project(0), 1))
            weave((maxima(0, 0), 1))
            for g in range(3):
                weave((maxima(0, g + 1), 0.6), (heads(0, g), 1))
            weave((chain(heads(0, 3), output(0)), 1), (chain(project(1), maxima(1, 0)), 0.8))
            for g in range(3):
                weave((maxima(1, g + 1), 0.65), (heads(1, g), 1))
            weave((heads(1, 3), 1))
            weave((output(1), 1))
            nn_ = [PT.get() for _ in range(8)]
            out_ = []
            for ch in range(NCH):
                tm = Slots([])
                tm.free = [(b_[:, 0:D], f_) for b_, f_ in nn_[4 * ch:4 * ch + 4]]
                out_.append(Norm(ch, tm, sts_[ch], t_out, pe.last))
            return out_

        nmoe = [0]
        ch_g = [Chan(f"s_g{i}") for i in range(2)]
        ch_y = [Chan(f"s_y{i}") for i in range(2)]
        ch_s = [Chan(f"s_s{i}") for i in range(2)]
        s_scat = sem("s_scat")
        s_gath = [sem(f"s_gath{i}") for i in range(NT)]

        def experts(norms, t_in, meanwhile, last):
            u_ = nmoe[0]
            nmoe[0] += 1
            bar = everyone()
            for ln in lines:
                ln.wait(bar)
            ra, fa = Area(RA, NRA), Area(FA, NFA)
            Cn = [ra.take(32).rearrange("p (k n) -> p k n", k=2) for _ in range(2)]
            WS = [[ra.take(768) for _ in range(2)] for _ in range(2)]
            H = Slots([[ra.take(CH) for _ in range(2)] for _ in range(3)])
            XT = fa.take(NT * D).rearrange("p (t n) -> p t n", t=NT)
            st_, cen = [fa.take(40) for _ in range(NCH)], fa.take(32)
            tmps = Slots([XT[:, i, :] for i in range(NT)])
            bufs = Slots([fa.take(CH) for _ in range(4)])
            small = Area(fa.take(1100), 1100)
            xin = Slots([fa.take(WB * D) for _ in range(2)])
            yout = Slots([fa.take(WB * D) for _ in range(2)])
            xts = Slots([fa.take(2 * D) for _ in range(2)])
            hb = Slots([fa.take(2 * P) for _ in range(2)])
            sg = Slots([fa.take(2 * P) for _ in range(2)])
            hts = Slots([fa.take(2 * P) for _ in range(2)])
            yg = Slots([fa.take(D) for _ in range(6)])
            sts = [fa.take(768) for _ in range(2)]
            t = ch_w[0](cen, d["cen"], bar)
            t_cn = split(Cn[0].rearrange("p k n -> p (k n)"), Cn[1].rearrange("p k n -> p (k n)"), cen, t, on=dve)
            t_ld = [ch_s[n](sts[n], d["we"][n], bar) for n in range(2)]
            t_xns, t_n = [], []
            if norms is None:
                norms = [Norm(ch, tmps, st_[ch], t_in) for ch in range(NCH)]

            def t8(n):
                return small.take(NT * n).rearrange("p (t e) -> p t e", t=NT)

            aff, bi, o1, o2, top, ix = t8(16), t8(16), t8(16), t8(16), t8(8), t8(8).bitcast(U32)
            mb = t8(8).bitcast(BF)
            wt1, wt2, sm, s1, s2 = (small.take(NT) for _ in range(5))
            i1, i2 = small.take(NT).bitcast(U32), small.take(NT).bitcast(U32)
            nblk, endb, base, one16 = (small.take(16) for _ in range(4))
            eid = small.take(32).bitcast(U32)
            es = small.take(32)
            z = dve(lambda e: e.memset(one16, 1.0))
            ixs = []
            for ch in range(NCH):
                t_xn, tn = norms[ch].finish()
                t_xns.append(t_xn)
                t_n.append(tn)
                bk, fr = banks.get()
                for i in range(TC):
                    A = [xn(k, ch, i * P, i * P + P) for k in range(2)]
                    m = group(bk[:, i * 16:i * 16 + 16], [q for k in range(2) for q in three(A[k], [w[:, k, :] for w in Cn])],
                              t_xn, t_cn, *fr)
                ts = slice(ch * TC, ch * TC + TC)
                for _ in range(8):
                    norms[1].step()
                a = act(lambda e: e.activation(aff[:, ts, :], bk[:, 0:16 * TC].rearrange("p (t e) -> p t e", e=16), ACT.Sigmoid), m)
                banks.put(bk, a)
                gb = cst("gb").unsqueeze(1).broadcast_to([P, TC, 16])
                b = dve(lambda e: e.tensor_tensor(bi[:, ts, :], aff[:, ts, :], gb, ALU.add), a)
                tops = [dve(lambda e: e.max(top[:, i, :], bi[:, i, :]), b) for i in range(ch * TC, ch * TC + TC)]
                ixs += [dve(lambda e: e.max_index(ix[:, i, :], top[:, i, :], bi[:, i, :]), tops[i % TC])
                        for i in range(ch * TC, ch * TC + TC)]
            io = cst("iota")[:, 0:16].unsqueeze(1).broadcast_to([P, NT, 16])
            c1 = dve(lambda e: e.tensor_tensor(o1, io, ix[:, :, 0:1].broadcast_to([P, NT, 16]), ALU.is_equal), ixs)
            c2 = dve(lambda e: e.tensor_tensor(o2, io, ix[:, :, 1:2].broadcast_to([P, NT, 16]), ALU.is_equal), ixs)
            c = dve(lambda e: e.tensor_tensor(mb, o1, o2, ALU.add), c1, c2)
            bk, fr = banks.get()
            for t in range(NT):
                ps = [(TRI[:, P:2 * P], mb[:, u, :]) for u in range(t)] + [(TRI[:, 0:P], mb[:, t, :])]
                group(bk[:, t * 16:t * 16 + 16], ps, c, t_tri, *fr)
            m = group(bk[:, 128:144], [(TRI[:, P:2 * P], mb[:, u, :]) for u in range(NT)])

            t_ws = [split(WS[n][0], WS[n][1], sts[n], t_ld[n]) for n in range(2)]

            accs = [banks.get() for _ in range(4)]
            fin = [None] * NT

            def down(n, ch, hh, tt):
                for i in range(TC):
                    t = ch * TC + i
                    acc, f_ = accs[t // 2]
                    o = acc[:, (t % 2) * D:(t % 2) * D + D]
                    fin[t] = group(o, three([x[:, i * P:i * P + P] for x in hh], [x[:, 512:768] for x in WS[n]]), tt,
                                   *(f_ if n == 0 else ()), start=n == 0 and t % 2 == 0, stop=n == 1, skip=True)
                H.put(hh, fin[t])

            def gateup(n, ch):
                bg, fg = banks.get()
                bu, fu = banks.get()
                X2 = [xn(k, ch) for k in range(2)]
                w = WS[n]
                mg = group(bg, [q for k in range(2) for q in three([x[:, k * 256:k * 256 + P] for x in w], X2[k])],
                           t_ws[n], t_xns[ch], *fg)
                mu = group(bu, [q for k in range(2) for q in three([x[:, k * 256 + P:k * 256 + 2 * P] for x in w], X2[k])], *fu)
                s_, fs = bufs.get()
                t = act(lambda e: e.activation(s_, bg, ACT.Silu), mg, *fs)
                banks.put(bg, t)
                return n, ch, bu, mu, s_, t

            def middle(n, ch, bu, mu, s_, t):
                h, fh = bufs.get()
                t = dve(lambda e: e.scalar_tensor_tensor(h, s_, 0.1, bu, ALU.mult, ALU.mult), t, mu, *fh)
                banks.put(bu, t)
                bufs.put(s_, t)
                hh, fhh = H.get()
                tt = split(hh[0], hh[1], h, t, *fhh, on=dve)
                bufs.put(h, *tt)
                return n, ch, hh, tt

            cb, cf = bufs.get()
            g0 = gateup(0, 0)
            r = bk[:, 0:128].rearrange("p (t e) -> p t e", e=16)
            ui = i1.bitcast(U32)
            nu = nblk.bitcast(U32)
            c = dve(lambda e: e.tensor_scalar(nu, bk[:, 128:144], float(P - 1), None, ALU.add), m)
            c = dve(lambda e: e.tensor_scalar(nu, nu, 7, None, ALU.logical_shift_right), c)
            c = dve(lambda e: e.tensor_copy(base, nu), c)
            c = dve(lambda e: e.tensor_tensor_scan(endb, one16, base, 0.0, ALU.mult, ALU.add), c, z)
            ce = c
            c = dve(lambda e: e.tensor_tensor(base, endb, base, ALU.subtract), c)
            c = dve(lambda e: e.tensor_scalar(base, base, float(P), None, ALU.mult), c)
            c = dve(lambda e: e.tensor_tensor(bi, r, base.unsqueeze(1).broadcast_to([P, NT, 16]), ALU.add), c)
            banks.put(bk, c)
            t_i = []
            for o, s_, ii in ((o1, s1, i1), (o2, s2, i2)):
                a = dve(lambda e: e.tensor_tensor(cb[:, 0:128].rearrange("p (t e) -> p t e", e=16), bi, o, ALU.mult), c, *cf, *t_i[-1:])
                a = dve(lambda e: e.reduce_sum(s_, cb[:, 0:128].rearrange("p (t e) -> p t e", e=16), AX), a)
                t_i.append(dve(lambda e: e.tensor_copy(ii, s_), a))
            pool.wait(t_i, t_n, t_gx if u_ == 0 else None, t_gxfree[0])
            for t in range(NT):
                for ii in (i1, i2):
                    nc.gpsimd.indirect_dma_start(GX, bass.IndirectOffsetOnAxis(ap=ii[:, t:t + 1], axis=0), XT[:, t, :],
                                                 None).then_inc(s_scat, 16)
            t_sc = (s_scat.name, s_scat, 16 * 2 * NT * (u_ + 1))
            cmp0 = cb[0:1, 0:NB * 16].rearrange("p (b e) -> p b e", e=16)
            a = dve(lambda e: e.tensor_tensor(cmp0, cst("iota")[0:1, 0:NB].unsqueeze(2).broadcast_to([1, NB, 16]),
                                              endb[0:1, :].unsqueeze(1).broadcast_to([1, NB, 16]), ALU.is_ge), ce, t_i)
            a = dve(lambda e: e.reduce_sum(es[0:1, 0:NB], cmp0, AX), a)
            bufs.put(cb, a)
            t_e = dve(lambda e: e.tensor_scalar(eid[0:1, 0:NB], es[0:1, 0:NB], float(NE - 1), 768.0, ALU.min, ALU.mult), a)
            a1 = dve(lambda e: e.tensor_tensor(o1, o1, aff, ALU.mult), t_i)
            a2 = dve(lambda e: e.tensor_tensor(o2, o2, aff, ALU.mult), t_i)
            a1 = dve(lambda e: e.reduce_sum(wt1, o1, AX), a1)
            a2 = dve(lambda e: e.reduce_sum(wt2, o2, AX), a2)
            a = dve(lambda e: e.tensor_tensor(sm, wt1, wt2, ALU.add), a1, a2)
            a = dve(lambda e: e.tensor_scalar(sm, sm, 1e-9, 2.0, ALU.add, ALU.mult), a)
            a = dve(lambda e: e.reciprocal(sm, sm), a)
            t_w1 = dve(lambda e: e.tensor_tensor(wt1, wt1, sm, ALU.mult), a)
            t_w2 = dve(lambda e: e.tensor_tensor(wt2, wt2, sm, ALU.mult), a)
            g1 = gateup(0, 1)
            m0 = middle(*g0)
            g2 = gateup(1, 0)
            m1 = middle(*g1)
            down(*m0)
            g3 = gateup(1, 1)
            m2 = middle(*g2)
            down(*m1)
            m3 = middle(*g3)
            down(*m2)
            down(*m3)
            t_x1 = [None] * NT
            for t in range(NT):
                acc, _ = accs[t // 2]
                o = acc[:, (t % 2) * D:(t % 2) * D + D]
                xt = X[:, t, :]
                t_x1[t] = dve(lambda e: e.scalar_tensor_tensor(xt, o, 0.5, xt, ALU.mult, ALU.add), fin[t | 1], t_n)
            for a in range(4):
                banks.put(accs[a][0], t_x1[2 * a], t_x1[2 * a + 1])

            t_ld, t_st = {}, []
            gx3 = GX.rearrange("(b p) d -> p b d", p=P)
            gy3 = GY.rearrange("(b p) d -> p b d", p=P)
            groups = [(a, min(NB, a + WB)) for a in range(0, NB, WB)]

            def fetch(gi):
                a, b = groups[gi]
                x_, f_ = xin.get()
                t = ch_g[gi % 2](x_.rearrange("p (b n) -> p b n", n=D)[:, 0:b - a, :], gx3[:, a:b, :], t_sc, *f_)
                return x_, t

            gs = [fetch(0), fetch(1)]
            pairs = [(b, min(NB, b + 2)) for b in range(0, NB, 2)]
            outs = {}

            def stage1(pi):
                a, b = pairs[pi]
                x_, tl = gs[a // WB]
                bk, fr = banks.get()
                for u in range(a, b):
                    for k in range(2):
                        p = tr(bk[:, (u - a) * D + k * P:(u - a) * D + k * P + P],
                               x_[:, (u % WB) * D + k * P:(u % WB) * D + k * P + P], tl, *fr, inc=u == b - 1 and k == 1)
                if b % WB == 0 or b == NB:
                    xin.put(x_, p)
                    if len(gs) < len(groups):
                        gs.append(fetch(len(gs)))
                xt, fx = xts.get()
                w = (b - a) * D
                t = act(lambda e: e.activation(xt[:, 0:w], bk[:, 0:w], ACT.Copy), p, *fx)
                banks.put(bk, t)
                return xt, t

            def stage2(pi, xt, t):
                a, b = pairs[pi]
                bk, fr = banks.get()
                regs = []
                for u in range(a, b):
                    pe.wait(t_e)
                    v = nc.tensor.value_load(eid[0:1, u:u + 1], min_val=0, max_val=768 * (NE - 1))
                    regs.append(v)
                    for k in range(2):
                        m = mm(bk[:, (u - a) * D:(u - a) * D + D], xt[:, (u - a) * D + k * P:(u - a) * D + k * P + P],
                               WE[:, bass.ds(v + k * 256, 256)], k == 0, k == 1, t, t_we, *fr, inc=u == b - 1 and k == 1)
                xts.put(xt, m)
                s_, fs = sg.get()
                h_, fh = hb.get()
                nn = b - a
                b3 = bk.rearrange("p (u g n) -> p u g n", u=2, g=2)
                s3 = s_.rearrange("p (u n) -> p u n", u=2)
                h3 = h_.rearrange("p (u n) -> p u n", u=2)
                q = act(lambda e: e.activation(s3[:, 0:nn, :], b3[:, 0:nn, 0, :], ACT.Silu), m, *fs)
                q = dve(lambda e: e.tensor_tensor(h3[:, 0:nn, :], s3[:, 0:nn, :], b3[:, 0:nn, 1, :], ALU.mult), q, *fh)
                banks.put(bk, q)
                sg.put(s_, q)
                return regs, h_, q

            def stage3(pi, regs, h_, q):
                a, b = pairs[pi]
                bk, fr = banks.get()
                for u in range(b - a):
                    p = tr(bk[:, u * P:u * P + P], h_[:, u * P:u * P + P], q, *fr, inc=u == b - a - 1)
                hb.put(h_, p)
                ht, fh = hts.get()
                w = (b - a) * P
                t = dve(lambda e: e.tensor_copy(ht[:, 0:w], bk[:, 0:w]), p, *fh)
                banks.put(bk, t)
                return regs, ht, t

            def stage4(pi, regs, ht, t):
                a, b = pairs[pi]
                bk, fr = banks.get()
                for u in range(a, b):
                    v = regs[u - a]
                    m = mm(bk[:, (u - a) * D:(u - a) * D + D], ht[:, (u - a) * P:(u - a) * P + P],
                           WE[:, bass.ds(v + 512, 256)], True, True, t, *fr, inc=u == b - 1)
                hts.put(ht, m)
                gi = a // WB
                if gi not in outs:
                    outs[gi] = yout.get()
                y_, fy = outs[gi]
                o = (a % WB) * D
                w = (b - a) * D
                if pi % 2:
                    t = act(lambda e: e.activation(y_[:, o:o + w], bk[:, 0:w], ACT.Copy), m, *fy)
                else:
                    t = dve(lambda e: e.tensor_copy(y_[:, o:o + w], bk[:, 0:w]), m, *fy)
                banks.put(bk, t)
                outs.setdefault(("t", gi), []).append(t)
                if b % WB == 0 or b == NB:
                    ga, gb_ = groups[gi]
                    t = ch_y[gi % 2](gy3[:, ga:gb_, :], y_.rearrange("p (b n) -> p b n", n=D)[:, 0:gb_ - ga, :],
                                     outs[("t", gi)], t_gyfree[0])
                    yout.put(y_, t)
                    t_st.append(t)

            q1, q2, q3 = {}, {}, {}
            for i in range(len(pairs) + 3):
                if i < len(pairs):
                    q1[i] = stage1(i)
                if 0 <= i - 1 < len(pairs):
                    q2[i - 1] = stage2(i - 1, *q1.pop(i - 1))
                if 0 <= i - 2 < len(pairs):
                    q3[i - 2] = stage3(i - 2, *q2.pop(i - 2))
                if 0 <= i - 3 < len(pairs):
                    stage4(i - 3, *q3.pop(i - 3))
                next(meanwhile, None)
            t_gxfree[0] = [gs[-1][1], gs[-2][1]]
            pool.wait(t_st)
            t_out = [None] * NT
            nexts = [Norm(ch, Slots([b_[:, 0:D] for b_, _ in bufs.free]), st_[ch], t_out) for ch in range(NCH)]
            for n_ in nexts:
                for i, (_, f_) in enumerate(bufs.free):
                    n_.tmps.free[i] = (n_.tmps.free[i][0], f_)
            for t in range(NT):
                ys_ = []
                for ii in (i1, i2):
                    y_, f_ = yg.get()
                    pool.wait(*f_)
                    nc.gpsimd.indirect_dma_start(y_, None, GY, bass.IndirectOffsetOnAxis(ap=ii[:, t:t + 1], axis=0))\
                        .then_inc(s_gath[t], 16)
                    ys_.append(y_)
                tg = (s_gath[t].name, s_gath[t], 32 * (u_ + 1))
                xt = X[:, t, :]
                a = dve(lambda e: e.scalar_tensor_tensor(xt, ys_[0], wt1[:, t:t + 1], xt, ALU.mult, ALU.add), tg, t_x1[t], t_w1)
                yg.put(ys_[0], a)
                a = dve(lambda e: e.scalar_tensor_tensor(xt, ys_[1], wt2[:, t:t + 1], xt, ALU.mult, ALU.add), a, t_w2)
                yg.put(ys_[1], a)
                t_out[t] = a
                if not last and t >= TC:
                    nexts[0].step()
            t_gyfree[0] = tg
            return t_out, nexts

        t_gxfree, t_gyfree = [None], [None]

        t_mam, wst_free = {}, [None, None]

        def mamba_weights():
            ra, bar, i = Area(RA, 8704), everyone(), 0
            for name, n in (("in", 2048), ("xp", 768), ("dt", 512), ("outw", 1024)):
                out = [ra.take(n) for _ in range(2)]
                tk = []
                for a in range(0, n, 1536):
                    b = min(n, a + 1536)
                    w = wst[i % 2][:, 0:b - a]
                    t = ch_w[i % 2](w, d[name][:, a:b], bar, wst_free[i % 2])
                    yield
                    tt = split(out[0][:, a:b], out[1][:, a:b], w, t, bar, on=dve)
                    wst_free[i % 2] = tt
                    tk += tt
                    i += 1
                    yield
                t_mam[name] = out, tk

        def mamba(norms):
            bar = everyone()
            for ln in lines:
                ln.wait(bar)
            ra, fa = Area(RA[:, 8704:], NRA - 8704), Area(FA, NFA - 3072)
            (Wi, t_wi), (Wx, t_wx), (Wd, t_wd), (Wp, t_wp) = (t_mam[n] for n in ("in", "xp", "dt", "outw"))
            XC2 = [W1Q[:, :, :].rearrange("p a b -> p (a b)").rearrange("p (m n) -> p m n", m=4),
                   W2Q[:, :, :].rearrange("p a b -> p (a b)").rearrange("p (m n) -> p m n", m=4)]
            DT = [ra.take(CH) for _ in range(2)]
            BCt = ra.take(CH)
            sts = [b2h[:, 40 * c_:40 * c_ + 40] for c_ in range(2)]
            st64 = b2h[:, 80:208]
            wa = Area(WE, NE * 768)
            xrs = [a_.take(4 * 516).rearrange("p (m n) -> p m n", m=4) for a_ in (wa, fa)]
            xc, sz, dl, uu = zip(*[[a_.take(4 * CH).rearrange("p (m n) -> p m n", m=4) for _ in range(4)] for a_ in (wa, fa)])
            BCs = [BCt, XN[:, 0, 0, 1, :]]
            w6 = [FA[:, NFA - 3072 + CH * i:NFA - 3072 + CH * i + CH] for i in range(6)]
            bs = Slots([fa.take(CH) for _ in range(3)])
            sh = Slots([fa.take(CH) for _ in range(4)])
            tmps = Slots([x[:, 0:D] for x, _ in sh.free])
            sbb = Slots(w6[0:3])
            shc = Slots(w6[3:6])
            for s_ in (sbb, shc):
                s_.free = [(i, wst_free) for i, _ in s_.free]
            state, An = st64[:, 0:64], st64[:, 64:128]
            t_an = act(lambda e: e.activation(An, cst("Alog"), ACT.Exp), t_c)
            t_an = dve(lambda e: e.tensor_scalar(An, An, -1.0, None, ALU.mult), t_an)
            t_st = dve(lambda e: e.memset(state, 0.0))
            t_out = [None] * NT
            W3 = [w.rearrange("p (k n) -> p k n", k=2) for w in Wi]
            X3 = [w.rearrange("p (k n) -> p k n", k=4) for w in Wx]
            D3 = [w.rearrange("p (m n) -> p m n", m=4) for w in Wd]
            P3 = [w.rearrange("p (k n) -> p k n", k=4) for w in Wp]
            cw = cst("cw")
            norms[1].tmps, norms[1].st = tmps, sts[1]
            xns = [norms[ch].finish()[0] for ch in range(NCH)]
            got, free = {}, {"xr": None, "xc2": None, "dt": None}

            def enter(ch):
                xr = xrs[ch]
                if ch:
                    t_z = dve(lambda e: e.tensor_copy(xr[:, :, 0:3], xrs[0][:, :, 512:515]), free["xr"])
                else:
                    t_z = dve(lambda e: e.memset(xr[:, :, 0:3], 0.0))
                tr_, tc_, tz_, tx_ = [], [], [], []
                for m in range(8):
                    bk, fr = banks.get()
                    g = group(bk, [q for k in range(2) for q in three([w[:, k, m * P:m * P + P] for w in W3], xn(k, ch))],
                              xns[ch], t_wi, *fr)
                    if m < 4:
                        a = act(lambda e: e.activation(xr[:, m, 3:515], bk, ACT.Copy), g, t_z)
                        tx_.append(a)
                        free["xr"] = list(tx_)
                    else:
                        a = act(lambda e: e.activation(sz[ch][:, m - 4, :], bk, ACT.Silu), g)
                        tz_.append(a)
                    banks.put(bk, a)
                    yield
                for w in range(4):
                    for m in range(4):
                        v = xc[ch][:, m, :]
                        c_ = cw[:, 4 * m + w:4 * m + w + 1]
                        if w == 0:
                            tc_.append(dve(lambda e: e.tensor_scalar(v, xr[:, m, 0:512], c_, None, ALU.mult), tx_[m], t_z))
                        else:
                            tc_[m] = dve(lambda e: e.scalar_tensor_tensor(v, xr[:, m, w:w + 512], c_, v, ALU.mult, ALU.add), tc_[m])
                    yield
                got["x", ch] = [act(lambda e, v=xc[ch][:, m, :]: e.activation(v, v, ACT.Silu), tc_[m]) for m in range(4)]
                got["z", ch] = tz_
                yield

            def steps_of(ch, ring):
                t_xc = []
                for m in range(4):
                    v = xc[ch][:, m, :]
                    t_xc.append(split(XC2[0][:, m, :], XC2[1][:, m, :], v, got["x", ch][m], free["xc2"], on=dve))
                    yield
                bd, fd = ring.get()
                g1 = group(bd, [q for k in range(4) for q in three([w[:, k, 0:P] for w in X3], [x[:, k, :] for x in XC2])],
                           t_xc, t_wx, *fd)
                yield
                t_dd = split(DT[0], DT[1], bd, g1, free["dt"])
                ring.put(bd, *t_dd)
                yield
                bb, fb = ring.get()
                g2 = group(bb[0:64, :], [q for k in range(4) for q in three([w[:, k, P:P + 64] for w in X3],
                                                                            [x[:, k, :] for x in XC2])], *fb)
                free["xc2"] = g2
                yield
                bc = BCs[ch]
                z = dve(lambda e: e.memset(bc[64:128, :].bitcast(F), 0.0), g2)
                a = act(lambda e: e.activation(bc[0:64, :], bb[0:64, :], ACT.Copy), g2)
                t_bb = dve(lambda e: e.tensor_tensor(bc[32:64, :], bb[32:64, :], bc[32:64, :].bitcast(F), ALU.subtract), a)
                ring.put(bb, t_bb)
                got["b", ch] = [t_bb, z]
                yield
                dd = []
                for m in range(4):
                    bk, fr = ring.get()
                    g = group(bk, three([w[:, m, :] for w in D3], DT), t_dd, t_wd, *fr)
                    b = cst("dtb")[:, m:m + 1]
                    v, u = dl[ch][:, m, :], uu[ch][:, m, :]
                    yield
                    a = act(lambda e: e.activation(v, bk, ACT.Abs, bias=b), g)
                    if ch:
                        r = act(lambda e: e.activation(u, bk, ACT.Relu, bias=b), g)
                    else:
                        r = dve(lambda e: e.tensor_scalar(u, bk, b, 0.0, ALU.add, ALU.max), a)
                    ring.put(bk, a, r)
                    dd.append((v, u, a, r))
                    yield
                free["dt"] = g
                ee = [act(lambda e, v=v: e.activation(v, v, ACT.Exp, scale=-1.0), a) for v, u, a, r in dd]
                yield
                ll = [act(lambda e, v=v: e.activation(v, v, ACT.Ln, bias=1.0), x) for (v, u, a, r), x in zip(dd, ee)]
                yield
                t_dl, t_u = [], []
                for m in range(4):
                    v, u, _, r = dd[m]
                    a = dve(lambda e: e.tensor_tensor(v, v, u, ALU.add), ll[m], r)
                    t_dl.append(a)
                    t_u.append(dve(lambda e: e.tensor_tensor(u, v, xc[ch][:, m, :], ALU.mult), a, got["x", ch][m]))
                    yield
                got["dl", ch], got["u", ch] = t_dl, t_u

            def states(ch, ys, ab, cb, ring):
                t_bb, t_dl, t_u = got["b", ch], got["dl", ch], got["u", ch]
                bc = BCs[ch]
                cb, cfree = cb
                live = {}
                pend = []
                gy = got["y", ch] = [None] * 4

                def spread_b(n):
                    bb, f_ = ring.get()
                    return bb, mm(bb, HOT[:, n:n + 1].broadcast_to([P, P]), bc, True, True, t_bb, t_hot,
                                  *f_, inc=True)

                def store_b(bb, g):
                    s_, f_ = bs.get()
                    t = act(lambda e: e.activation(s_, bb, ACT.Copy), g, *f_)
                    ring.put(bb, t)
                    return s_, t

                def bring_c(n):
                    return mm(cb, HOT[:, 16 + n:17 + n].broadcast_to([P, P]), bc, True, True,
                              *live.get("c", cfree), inc=True)

                def close():
                    n, m, h_, t3 = pend.pop(0)
                    c_, fc_ = shc.get()
                    t4 = dve(lambda e: e.tensor_tensor(c_, h_, cb, ALU.mult), t3, tc[n], *fc_)
                    sh.put(h_, t4, live.get("s"))
                    live["c"] = [t4]
                    if m == 3 and n + 1 < DN:
                        tc[n + 1] = bring_c(n + 1)
                    yb, fy = ys[m]
                    gy[m] = mm(yb, ident, c_, n == 0, n == DN - 1, t4, *(fy if n == 0 else ()), inc=True)
                    shc.put(c_, gy[m])

                nb = [store_b(*spread_b(0)), store_b(*spread_b(1))]
                tc = {0: bring_c(0)}
                for n in range(DN):
                    Bs, t_B = nb.pop(0)
                    for m in range(4):
                        if m == 0 and n + 2 < DN:
                            gb = spread_b(n + 2)
                        k = 16 * m + n
                        a_, fa_ = ab.get()
                        t1 = act(lambda e: e.activation(a_, dl[ch][:, m, :], ACT.Exp, scale=An[:, k:k + 1]), t_dl[m], t_an, *fa_)
                        b_, fb_ = sbb.get()
                        t2 = pool(lambda e: e.tensor_tensor(b_, uu[ch][:, m, :], Bs, ALU.mult), t_u[m], t_B, *fb_)
                        h_, fh_ = sh.get()
                        init = state[:, k:k + 1] if ch else 0.0
                        t3 = dve(lambda e: e.tensor_tensor_scan(h_, a_, b_, init, ALU.mult, ALU.add), t1, t2, t_st, *fh_)
                        ab.put(a_, t3)
                        sbb.put(b_, t3)
                        if len(pend) == 2:
                            close()
                        if m == 1 and n + 2 < DN:
                            nb.append(store_b(*gb))
                        if ch + 1 < NCH:
                            live["s"] = dve(lambda e: e.tensor_copy(state[:, k:k + 1], h_[:, CH - 1:CH]), t3)
                        pend.append((n, m, h_, t3))
                        if m % 2:
                            yield
                    bs.put(Bs, t2)
                while pend:
                    close()
                got["s", ch] = live.get("s")
                got["c"] = live["c"]

            def gate(ch, ys):
                got["ys", ch], out = [], []
                for m in range(4):
                    yb, _ = ys[m]
                    u = uu[ch][:, m, :]
                    a = dve(lambda e: e.scalar_tensor_tensor(u, xc[ch][:, m, :], cst("Dp")[:, m:m + 1], yb, ALU.mult, ALU.add),
                            got["y", ch][m])
                    out.append((yb, [a]))
                    a = dve(lambda e: e.tensor_tensor(u, u, sz[ch][:, m, :], ALU.mult), a, got["z", ch][m])
                    got["ys", ch].append(split(XC2[0][:, m, :], XC2[1][:, m, :], u, a, free["xc2"]))
                return out

            def leave(ch, ring):
                for i in range(TC):
                    bk, fr = ring.get()
                    g = group(bk[:, 0:D], [q for k in range(4) for q in three([x[:, k, i * P:i * P + P] for x in XC2],
                                                                              [w[:, k, :] for w in P3])], got["ys", ch], t_wp, *fr)
                    yield
                    xt = X[:, ch * TC + i, :]
                    a = dve(lambda e: e.tensor_tensor(xt, bk[:, 0:D], xt, ALU.add), g)
                    ring.put(bk, a)
                    t_out[ch * TC + i] = a
                    yield
                free["xc2"] = g
                if ch == 0:
                    nx = Norm(0, Slots([XTs[:, i, :] for i in range(TC)]), sts[0], t_out, pe.last)
                    nx.single = True
                    got["nx"] = nx
                    while not nx.done:
                        nx.step()
                        yield

            weave((chain(enter(0), steps_of(0, banks)), 1), (chain(range(8), enter(1)), 1))
            ys = [banks.get() for _ in range(4)]
            ab = Slots([])
            ab.free = [banks.get() for _ in range(2)]
            cb = banks.get()
            weave((states(0, ys, ab, cb, banks), 1), (steps_of(1, banks), 1))
            t_st = got["s", 0]
            ys = gate(0, ys)
            weave((states(1, ys, ab, (cb[0], got["c"]), banks), 1), (leave(0, banks), 1))
            got["we"] = [Chan(f"s_wf{i}")(WE[:, i * 4096:i * 4096 + 4096], d["wr"][:, i * 4096:i * 4096 + 4096], got["ys", 0])
                         for i in range(3)]
            banks.put(cb[0], *got["c"])
            for b_, f_ in ab.free:
                banks.put(b_, *f_)
            for b_, f_ in gate(1, ys):
                banks.put(b_, *f_)
            accs = [banks.get() for _ in range(TC)]
            for k in range(4):
                for i in range(TC):
                    g = group(accs[i][0][:, 0:D], three([x[:, k, i * P:i * P + P] for x in XC2], [w[:, k, :] for w in P3]),
                              got["ys", 1][k], t_wp, *accs[i][1], start=k == 0, stop=k == 3)
                    if k == 3:
                        t = TC + i
                        a = dve(lambda e: e.tensor_tensor(X[:, t, :], accs[i][0][:, 0:D], X[:, t, :], ALU.add), g)
                        banks.put(accs[i][0], a)
                        t_out[t] = a
            t_we.extend(got["we"])
            return [got["nx"], Norm(1, Slots([XTs[:, TC + i, :] for i in range(TC)]), sts[1], t_out, pe.last)]

        class Pairs:

            def get(self):
                if not self.own:
                    raise AssertionError
                return self.own.pop(0)

            def put(self, bk, *tokens):
                self.own.append((bk, list(tokens)))

        banks2 = Pairs()
        banksT = Slots([])

        def lend():
            frs = {}
            got = [banks.get() for _ in range(8)]
            for b, f in got:
                frs[b.offset] = (b, f)
            order = sorted(frs)
            lst = [frs[o] for o in order]
            banks2.own = [(PS[:, 2 * i:2 * i + 2, :], lst[2 * i][1] + lst[2 * i + 1][1]) for i in range(2)]
            banksT.free = lst[4:7]
            banks.put(lst[7][0], *lst[7][1])

        def unlend():
            for bk, f in banks2.own:
                banks.put(bk[:, 0, :], *f)
                banks.put(bk[:, 1, :], *f)
            banks2.own = []
            for b, f in banksT.free:
                banks.put(b, *f)

        zt = FA[:, 14000:14000 + D]
        t_zero = pool(lambda e: e.memset(zt, 0.0))
        t_gx = Chan("s_gz")(GX.rearrange("(b p) d -> p b d", p=P), zt.unsqueeze(1).broadcast_to([P, NB, D]), t_zero, t_w2q)
        t = ffn0(norms0, attention_weights(), None, 10600)
        for ln in lines:
            ln.wait(t_gx)
        lend()
        t = attention(t)
        unlend()
        early.close()
        NRA, NFA = 10240, 17088
        WE = sb("WE", [P, NE * 768], F)
        RA = sb("RB", [P, NRA], R)
        FA = sb("FB", [P, NFA], F)
        wst = stage_of()
        XTs = FA[:, 0:NT * D].rearrange("p (t n) -> p t n", t=NT)
        t_we = [Chan(f"s_we{i}")(WE[:, i * 3072:i * 3072 + 3072], d["wr"][:, i * 3072:i * 3072 + 3072], everyone())
                for i in range(4)]
        bar = everyone()
        for ln in lines:
            ln.wait(bar)
        t = ffn0(t, None, [Slots([XTs[:, c_ * TC + i, :] for i in range(TC)]) for c_ in range(NCH)], 2304)
        _, t = experts(t, None, mamba_weights(), False)
        t = mamba(t)
        t, _ = experts(t, None, iter(()), True)
        co = Chan("s_out")
        for h in range(4):
            t_o = co(d["out"][:, 2 * h:2 * h + 2, :], X[:, 2 * h:2 * h + 2, :], t[2 * h], t[2 * h + 1])
        sp.wait(t_o)


def layout(i):
    f = np.float32
    x = np.asarray(i["L0_attn_x"])[0]

    def kt(w, k):
        return np.ascontiguousarray(w.reshape(k, P, -1).transpose(1, 0, 2))

    perm = np.array([h * 16 + c for h in range(NH) for c in list(range(0, 16, 2)) + list(range(1, 16, 2))])
    g = {n: np.asarray(i[n]) for n in i}
    wqkv = np.concatenate([g["L0_attn_Wq"][perm].T, g["L0_attn_Wk"][perm].T, g["L0_attn_Wv"].T], axis=1)
    bqkv = np.concatenate([g["L0_attn_bq"][perm], g["L0_attn_bk"][perm], g["L0_attn_bv"]])
    half = 8
    inv = (f(1.0) / np.power(f(10000.0), np.arange(half, dtype=f) / f(half))).astype(f)
    ang = (np.arange(S, dtype=f)[:, None] * inv[None, :]).astype(f)
    cos, sin = np.cos(ang).astype(f), np.sin(ang).astype(f)
    CC = np.concatenate([cos, cos], axis=1).reshape(NT, P, 16).transpose(1, 0, 2).reshape(P, NT * 16)
    SS = np.concatenate([-sin, sin], axis=1).reshape(NT, P, 16).transpose(1, 0, 2).reshape(P, NT * 16)
    hot = np.zeros((P, 32), f)
    for n in range(32):
        hot[n, n] = 1
        hot[32 + n, n] = 1

    def rows(v):
        return np.broadcast_to(np.asarray(v)[None, :], (P, len(v)))

    def cols(v, k):
        return np.asarray(v).reshape(k, P, -1).transpose(1, 0, 2).reshape(P, -1)

    a = np.arange(P)
    neg = f(-1e30)
    mS = np.where(a[None, :] > a[:, None], neg, f(0))
    mT = np.where(a[:, None] > a[None, :], neg, f(0))

    parts = {
        "ident": np.eye(P, dtype=f), "CC": CC, "SS": SS, "iota": rows(np.arange(32, dtype=f)),
        "b2": rows(g["L0_ffn_b2"]), "bqkv": rows(bqkv), "bo": rows(g["L0_attn_bo"]),
        "b1": cols(g["L0_ffn_b1"], 8), "cw": cols(g["L1_attn_conv1d_weight"], 4),
        "dtb": cols(g["L1_attn_dt_proj_bias"], 4), "Alog": cols(g["L1_attn_A_log"], 4),
        "Dp": cols(g["L1_attn_D"], 4), "gb": rows(g["L1_ffn_gate_bias"]), "hot": hot,
    }
    cst = np.concatenate([parts[n] for n in CONST], axis=1)
    xpw = g["L1_attn_x_proj_weight"].T
    xp = np.concatenate([xpw[:, 0:P], xpw[:, P:], xpw[:, P:]], axis=1)
    wgs, wus, wds = g["L1_ffn_wg_s"], g["L1_ffn_wu_s"], g["L1_ffn_wd_s"]
    we = []
    for s in range(2):
        we.append((wgs[:, s * P:s * P + P], wus[:, s * P:s * P + P], wds[s * P:s * P + P]))
    for e in range(NE):
        we.append((g["L1_ffn_wg"][e], g["L1_ffn_wu"][e], g["L1_ffn_wd"][e]))
    we = np.stack([np.concatenate([a_[0:P], b_[0:P], a_[P:], b_[P:], c_], axis=1) for a_, b_, c_ in we])
    return {
        "x": np.ascontiguousarray(x.reshape(NT, P, D).transpose(1, 0, 2)),
        "cst": np.ascontiguousarray(cst.astype(f)),
        "b16": np.concatenate([np.eye(P, dtype=f), mS, mT, np.triu(np.ones((P, P), f), 1), np.ones((P, P), f)], axis=1).astype(f),
        "w1": kt(g["L0_ffn_w1"].T, 2).reshape(P, 2048), "w2": kt(g["L0_ffn_w2"].T, 8).reshape(P, 2048),
        "qkv": kt(wqkv, 2).reshape(P, 1536), "o": kt(g["L0_attn_Wo"].T, 2).reshape(P, 512),
        "in": kt(g["L1_attn_in_proj_weight"].T, 2).reshape(P, 2048), "xp": kt(xp, 4).reshape(P, 768),
        "dt": np.ascontiguousarray(g["L1_attn_dt_proj_weight"].T), "outw": kt(g["L1_attn_out_proj_weight"].T, 4).reshape(P, 1024),
        "cen": kt(g["L1_ffn_centroids"].T, 2).reshape(P, 32), "we": np.ascontiguousarray(we[0:2]), "wr": np.ascontiguousarray(we[2:].transpose(1, 0, 2).reshape(P, NE * 768)),
    }


def kernel(**inputs):
    import concourse.bacc as bacc
    from concourse.bass_utils import run_bass_kernel_spmd as run

    arrays = {f"in_{k}": v for k, v in layout(inputs).items()}
    nc = bacc.Bacc("TRN2", target_bir_lowering=False, num_devices=1)
    d = {}
    for k, v in arrays.items():
        d[k[3:]] = nc.dram_tensor(k, v.shape, mybir.dt.from_np(v.dtype), kind="ExternalInput").ap()
    d["out"] = nc.dram_tensor("out", (P, NT, D), F, kind="ExternalOutput").ap()
    build(nc, d)
    r = run(nc, [arrays], core_ids=[0])
    o = r.results[0]["out"]
    return np.ascontiguousarray(o.transpose(1, 0, 2)).reshape(1, S, D)
```
